# Optimizing a Trainium2 kernel written in Bass

```python
import numpy as np
import jax
import jax.numpy as jnp

def _softmax(x, axis=-1):
    return jax.nn.softmax(x, axis=axis)

def _gelu(x):
    return jax.nn.gelu(x, approximate=True)

def _silu(x):
    return jax.nn.silu(x)

def _sigmoid(x):
    return jax.nn.sigmoid(x)

def _layernorm(x, axis=-1, eps=1e-05):
    m = jnp.mean(x, axis=axis, keepdims=True)
    v = jnp.var(x, axis=axis, keepdims=True)
    return (x - m) / jnp.sqrt(v + eps)

def _scatter_add(tgt, idx, src, axis=0):
    return tgt.at[idx].add(src)

def _segment_sum(src, seg, n):
    return jax.ops.segment_sum(src, seg, n)
kernel_name = 'mk_flamingo_gated_d1_seqx_r8_3ce19a'

def setup_inputs(seed: int=0):
    np.random.seed(seed)
    _w = jnp.asarray

    def _rec_inputs():
        import jax
        import jax.numpy as jnp
        _rk = jax.random.key(seed)
        x = -0.0002928 + 1 * jax.random.normal(jax.random.fold_in(_rk, 1), (64, 64, 128), jnp.float32)
        _lenS = 64 - jax.random.randint(jax.random.fold_in(_rk, 7), (64,), 0, max(1, 64 // 4) + 1, jnp.int32)
        _lenS2 = 64 - jax.random.randint(jax.random.fold_in(_rk, 8), (64,), 0, max(1, 64 // 4) + 1, jnp.int32)
        _ctx_1024P = jax.random.normal(jax.random.fold_in(_rk, 11), (64, 16, 128), jnp.float32)
        _ctx_1024c = jax.random.dirichlet(jax.random.fold_in(_rk, 511), 0.3 * jnp.ones((16,), jnp.float32), (64, 64))
        _ctx_1024t = jnp.einsum('bsk,bkd->bsd', _ctx_1024c, _ctx_1024P)
        _ctx_1024t = _ctx_1024t * jax.lax.rsqrt(jnp.mean(jnp.square(_ctx_1024t)) + 1e-12) * 0.953939
        ctx_1024 = -1.39393e-06 + 0.999914 * (_ctx_1024t + 0.3 * jax.random.normal(jax.random.fold_in(_rk, 611), (64, 64, 128), jnp.float32))
        _validS = jnp.arange(64)[None, :] < _lenS[:, None]
        _validS2 = jnp.arange(64)[None, :] < _lenS2[:, None]
        _causal = jnp.tril(jnp.ones((64, 64), dtype=bool))
        mask_Bx1xS2_if1 = jnp.where(jnp.ones((64, 1, 64), dtype=bool), 1, 0).astype(jnp.int32)
        _g = jax.random.normal(jax.random.fold_in(_rk, 9001), (2, 1), jnp.float32)
        _g = jnp.sign(_g) * jnp.maximum(jnp.abs(_g), 1.0) + (_g == 0) * 1.0
        g_xattn = _g[0]
        g_ffn = _g[1]
        return (x, ctx_1024, mask_Bx1xS2_if1, g_xattn, g_ffn)
    x, ctx_1024, mask_Bx1xS2_if1, g_xattn, g_ffn = _rec_inputs()

    def _L0_xattn_setup():
        import math
        import jax, jax.numpy as jnp
        import numpy as np
        N_HEADS = 16
        NEG_INF = -1000000000.0

        def _rope(x):
            hd = x.shape[-1]
            S = x.shape[-2]
            half = hd // 2
            div_term = jnp.exp(jnp.arange(half, dtype=jnp.float32) * -(math.log(10000.0) / half))
            ang = jnp.arange(S, dtype=jnp.float32)[:, None] * div_term[None, :]
            cos, sin = (jnp.cos(ang), jnp.sin(ang))
            xr = x.reshape(x.shape[:-1] + (half, 2))
            xe, xo = (xr[..., 0], xr[..., 1])
            re = xe * cos - xo * sin
            im = xe * sin + xo * cos
            return jnp.stack([re, im], axis=-1).reshape(x.shape)
        key = jax.random.key(seed)
        ks = jax.random.split(key, 12)
        B, S, D = (2, 256, 128)
        std = 1.0 / math.sqrt(D)
        inp = {'query': jax.random.normal(ks[0], (B, S, D), jnp.float32), 'key': jax.random.normal(ks[1], (B, S, D), jnp.float32), 'value': jax.random.normal(ks[2], (B, S, D), jnp.float32), 'mask': jnp.ones((B, 1, S), jnp.int32), 'Wq': jax.random.normal(ks[3], (D, D), jnp.float32) * std, 'bq': jax.random.normal(ks[4], (D,), jnp.float32) * std, 'Wk': jax.random.normal(ks[5], (D, D), jnp.float32) * std, 'bk': jax.random.normal(ks[6], (D,), jnp.float32) * std, 'Wv': jax.random.normal(ks[7], (D, D), jnp.float32) * std, 'bv': jax.random.normal(ks[8], (D,), jnp.float32) * std, 'Wo': jax.random.normal(ks[9], (D, D), jnp.float32) * std, 'bo': jax.random.normal(ks[10], (D,), jnp.float32) * std}
        return inp
    _L0_xattn_all = _L0_xattn_setup()
    _L0_xattn_in = {k: v for k, v in _L0_xattn_all.items() if k in ('Wq', 'bq', 'Wk', 'bk', 'Wv', 'bv', 'Wo', 'bo')}
    del _L0_xattn_all

    def _L0_ffn_setup():
        import jax, jax.numpy as jnp
        import numpy as np
        B, S, D, F, E = (4, 256, 128, 512, 8)
        key = jax.random.key(seed)
        ks = jax.random.split(key, 7)
        s1 = 1.0 / np.sqrt(D)
        s2 = 1.0 / np.sqrt(F)
        x = jax.random.normal(ks[0], (B, S, D), dtype=jnp.float32)
        W1 = jax.random.uniform(ks[1], (E, D, F), jnp.float32, -s1, s1)
        b1 = jax.random.uniform(ks[2], (E, F), jnp.float32, -s1, s1)
        W2 = jax.random.uniform(ks[3], (E, F, D), jnp.float32, -s2, s2)
        b2 = jax.random.uniform(ks[4], (E, D), jnp.float32, -s2, s2)
        Wr = jax.random.uniform(ks[5], (D, E), jnp.float32, -s1, s1)
        br = jax.random.uniform(ks[6], (E,), jnp.float32, -s1, s1)
        return {'x': x, 'W1': W1, 'b1': b1, 'W2': W2, 'b2': b2, 'Wr': Wr, 'br': br}
    _L0_ffn_all = _L0_ffn_setup()
    _L0_ffn_in = {k: v for k, v in _L0_ffn_all.items() if k in ('W1', 'b1', 'W2', 'b2', 'Wr', 'br')}
    del _L0_ffn_all
    return {'x': x, 'ctx_1024': ctx_1024, 'mask_Bx1xS2_if1': mask_Bx1xS2_if1, 'g_xattn': g_xattn, 'g_ffn': g_ffn, 'L0_xattn_Wq': _L0_xattn_in['Wq'], 'L0_xattn_bq': _L0_xattn_in['bq'], 'L0_xattn_Wk': _L0_xattn_in['Wk'], 'L0_xattn_bk': _L0_xattn_in['bk'], 'L0_xattn_Wv': _L0_xattn_in['Wv'], 'L0_xattn_bv': _L0_xattn_in['bv'], 'L0_xattn_Wo': _L0_xattn_in['Wo'], 'L0_xattn_bo': _L0_xattn_in['bo'], 'L0_ffn_W1': _L0_ffn_in['W1'], 'L0_ffn_b1': _L0_ffn_in['b1'], 'L0_ffn_W2': _L0_ffn_in['W2'], 'L0_ffn_b2': _L0_ffn_in['b2'], 'L0_ffn_Wr': _L0_ffn_in['Wr'], 'L0_ffn_br': _L0_ffn_in['br']}

def reference(x, ctx_1024, mask_Bx1xS2_if1, g_xattn, g_ffn, L0_xattn_Wq, L0_xattn_bq, L0_xattn_Wk, L0_xattn_bk, L0_xattn_Wv, L0_xattn_bv, L0_xattn_Wo, L0_xattn_bo, L0_ffn_W1, L0_ffn_b1, L0_ffn_W2, L0_ffn_b2, L0_ffn_Wr, L0_ffn_br):
    import jax
    import jax.numpy as jnp

    def _L0_xattn_ref(query, key, value, mask, Wq, bq, Wk, bk, Wv, bv, Wo, bo):
        import math
        import jax, jax.numpy as jnp
        import numpy as np
        N_HEADS = 16
        NEG_INF = -1000000000.0

        def _rope(x):
            hd = x.shape[-1]
            S = x.shape[-2]
            half = hd // 2
            div_term = jnp.exp(jnp.arange(half, dtype=jnp.float32) * -(math.log(10000.0) / half))
            ang = jnp.arange(S, dtype=jnp.float32)[:, None] * div_term[None, :]
            cos, sin = (jnp.cos(ang), jnp.sin(ang))
            xr = x.reshape(x.shape[:-1] + (half, 2))
            xe, xo = (xr[..., 0], xr[..., 1])
            re = xe * cos - xo * sin
            im = xe * sin + xo * cos
            return jnp.stack([re, im], axis=-1).reshape(x.shape)
        B, S, D = query.shape
        H = N_HEADS
        hd = D // H

        def proj(x, W, b):
            return (x @ W.T + b).reshape(B, S, H, hd).transpose(0, 2, 1, 3)
        q = proj(query, Wq, bq)
        k = proj(key, Wk, bk)
        v = proj(value, Wv, bv)
        q = _rope(q)
        k = _rope(k)
        scores = jnp.einsum('bhqd,bhkd->bhqk', q, k) / math.sqrt(hd)
        m = mask[:, :, None, :]
        scores = jnp.where(m == 0, NEG_INF, scores)
        p_attn = jax.nn.softmax(scores, axis=-1)
        x = jnp.einsum('bhqk,bhkd->bhqd', p_attn, v)
        x = x.transpose(0, 2, 1, 3).reshape(B, S, D)
        return x @ Wo.T + bo

    def _L0_ffn_ref(x, W1, b1, W2, b2, Wr, br):
        import jax, jax.numpy as jnp
        import numpy as np
        B, S, D, F, E = (4, 256, 128, 512, 8)
        b, s, d = x.shape
        e = Wr.shape[1]
        logits = x @ Wr + br
        idx = jnp.argmax(logits, axis=-1)
        probs = jax.nn.softmax(logits, axis=-1)
        gates = jnp.take_along_axis(probs, idx[..., None], axis=-1)[..., 0]
        xf = x.reshape(-1, d)
        idxf = idx.reshape(-1)
        gf = gates.reshape(-1)
        out = jnp.zeros_like(xf)
        for ei in range(e):
            h = jax.nn.gelu(xf @ W1[ei] + b1[ei], approximate=False)
            y = h @ W2[ei] + b2[ei]
            mask = (idxf == ei).astype(xf.dtype)
            out = out + y * (gf * mask)[:, None]
        return out.reshape(b, s, d)
    x = x + jnp.tanh(g_xattn[0]) * _L0_xattn_ref(_layernorm(x, axis=-1), ctx_1024, ctx_1024, mask_Bx1xS2_if1, L0_xattn_Wq, L0_xattn_bq, L0_xattn_Wk, L0_xattn_bk, L0_xattn_Wv, L0_xattn_bv, L0_xattn_Wo, L0_xattn_bo)
    x = x + jnp.tanh(g_ffn[0]) * _L0_ffn_ref(_layernorm(x, axis=-1), L0_ffn_W1, L0_ffn_b1, L0_ffn_W2, L0_ffn_b2, L0_ffn_Wr, L0_ffn_br)
    return x

_drawn_inputs = setup_inputs


def setup_inputs(seed=0):
    import zlib

    import numpy as np

    out = dict(_drawn_inputs(seed))
    spreads = {}
    factors = {'L0_xattn_bq': 3.559,
     'L0_xattn_bk': 6.037,
     'L0_ffn_b1': 8.0,
     'L0_ffn_b2': 8.0,
     'L0_ffn_br': 4.38}
    for name, (base, spread) in spreads.items():
        noise = np.random.default_rng([zlib.crc32(name.encode()), seed]).standard_normal(out[name].shape)
        drawn = base * np.exp(spread * noise) if base else spread * noise
        out[name] = jnp.asarray(drawn.astype(out[name].dtype))
    for name, factor in factors.items():
        out[name] = (out[name] * factor).astype(out[name].dtype)
    return out
```

```python
import math
from contextlib import ExitStack

import numpy as np

import concourse.bass as bass
from concourse import mybir

F32 = mybir.dt.float32
F16 = mybir.dt.float16
I32 = mybir.dt.int32
ALU = mybir.AluOpType
ACT = mybir.ActivationFunctionType
AX = mybir.AxisListType

P = 128
B, S, D = 64, 64, 128
H, HD = 16, 8
T = B * S // P
NE, FF = 8, 512
FC = FF // P
NS = T + NE - 1
NA = 4
STK = 32
ROW_MAX, ROW_MASK = 24, 25
MASKED = -60000.0
SCALE = 1.0 / math.sqrt(HD)
EPS = 1e-5
W1_SCALE = 64.0
OUT_OF_RANGE = 8192.0
ROW = 2 * D
RING = 4

C_ID, C_SEL, C_COS, C_SIN = 0, 128, 256, 512
C_IOTA, C_REV, C_TILE, C_PART, C_ONE, C_POW, C_EPS, NCF = 768, 896, 904, 936, 937, 953, 954, 955
K_ID, K_TRI, K_ONE, K_EXP, NCH = 0, 128, 256, 384, 384 + NE * P


def constants():
    f = np.zeros((P, NCF), np.float32)
    h = np.zeros((P, NCH), np.float16)
    r = np.arange(P)
    f[:, C_ID:C_ID + P] = np.eye(P)
    f[:, C_SEL:C_SEL + P] = (r[:, None] // 16 == r[None, :] // 16) & (r[:, None] % 16 == HD)
    half = HD // 2
    div = np.exp(np.arange(half, dtype=np.float32) * np.float32(-(math.log(10000.0) / half)))
    ang = (np.arange(S, dtype=np.float32)[:, None] * div[None, :]).astype(np.float32)
    cos, sin = np.cos(ang.astype(np.float64)), np.sin(ang.astype(np.float64))
    c = np.repeat(cos, 2, axis=1)
    s = np.stack([-sin, sin], axis=-1).reshape(S, HD)
    f[:, C_COS:C_COS + 2 * D] = np.tile(c, (P // S, 2 * H))
    f[:, C_SIN:C_SIN + 2 * D] = np.tile(s, (P // S, 2 * H))
    f[:, C_IOTA:C_IOTA + P] = r[None, :]
    f[:, C_REV:C_REV + NE] = NE - np.arange(NE)[None, :]
    f[:, C_TILE:C_TILE + T] = np.arange(T)[None, :]
    f[:, C_PART] = r + 1
    f[:, C_ONE:C_ONE + H] = 1
    f[:, C_POW] = -0.5
    f[:, C_EPS] = EPS
    h[:, K_ID:K_ID + P] = np.eye(P)
    h[:, K_TRI:K_TRI + P] = r[:, None] < r[None, :]
    h[:, K_ONE:K_ONE + P] = 1
    e = h[:, K_EXP:].reshape(P, NE, P)
    for i in range(NE):
        e[i, i, :] = 1
        e[32 + i, i, :] = 1
    return f, h


def wait(eng, sem, n):
    if isinstance(n, int) and n <= 0:
        return
    eng.wait_ge(sem, n)


def alone(eng, passed):
    eng.sem_inc(passed, 1)


def build(nc, x, ctx_in, mask, g_x, g_f, Wq, bq, Wk, bk, Wv, bv, Wo, bo, W1, b1, W2, b2, Wr, br,
          const_f, const_h, rows, out):
    stack = ExitStack()
    with stack:
        def sb(name, shape, dt=F32):
            return stack.enter_context(nc.sbuf_tensor(name, shape, dt))

        def sem(name):
            return stack.enter_context(nc.semaphore(name))

        cf = sb("cf", [P, NCF])
        ch = sb("ch", [P, NCH], F16)
        ident = cf[:, C_ID:C_ID + P]
        sel = cf[:, C_SEL:C_SEL + P]
        cos_t = cf[:, C_COS:C_COS + 2 * D]
        sin_t = cf[:, C_SIN:C_SIN + 2 * D]
        iota = cf[:, C_IOTA:C_IOTA + P]
        power = cf[:, C_POW:C_POW + 1]
        eps = cf[:, C_EPS:C_EPS + 1]
        ident_h = ch[:, K_ID:K_ID + P]
        tri_h = ch[:, K_TRI:K_TRI + P]
        ones_h = ch[:, K_ONE:K_ONE + P]
        exp_h = ch[:, K_EXP:].rearrange("p (e n) -> p e n", e=NE)
        w_nat = sb("w_nat", [P, 4, D])
        wT = sb("wT", [P, 4, D])
        bias_qk = sb("bias_qk", [P, 2 * D])
        bias_rot = sb("bias_rot", [P, 2 * D])
        bias_tmp = sb("bias_tmp", [P, 2 * D])
        bv_bc = sb("bv_bc", [P, D])
        bo_col = sb("bo_col", [P, 1])
        c_tmp = sb("c_tmp", [P, D])
        c_col = sb("c_col", [P, 4])
        c_bc = sb("c_bc", [P, D])
        attn_c = sb("attn_c", [P, D])
        gates = sb("gates", [P, 2])
        tg = sb("tg", [P, 2])
        mask_i = sb("mask_i", [T, P], I32)
        mask_n = sb("mask_n", [T, P])
        mask_f = sb("mask_f", [P, T])
        mask_b = sb("mask_b", [P, T])
        wr_f = sb("wr_f", [P, NE])
        wr_h = sb("wr_h", [P, 2, NE], F16)
        br_bc = sb("br_bc", [P, NE])
        w1_f = sb("w1_f", [P, 2, FF])
        w1_h = sb("w1_h", [P, NE, FF], F16)
        w1_l = sb("w1_l", [P, NE, FF], F16)
        w2_f = sb("w2_f", [P, NE, FC, D])
        b1_f = sb("b1_f", [P, FF])
        b1_h = sb("b1_h", [P, FF], F16)
        b2_f = sb("b2_f", [P, D])
        b2_h = sb("b2_h", [P, D], F16)

        x_all = sb("x_all", [P, T, D])
        ctx_sb = sb("ctx_sb", [P, RING, D])
        st6 = sb("st6", [P, 2, 6])
        mv = sb("mv", [P, 2, 2])
        rstd = sb("rstd", [P, 2, 1])
        rvar = sb("rvar", [P, 2, 2])
        z = sb("z", [P, 2, D])
        zcT = sb("zcT", [P, 2, 2, D])
        qk = sb("qk", [P, 2, 2 * D])
        rot = sb("rot", [P, 2, 2 * D])
        rot_s = sb("rot_s", [P, 2, 2 * D])
        stq = sb("stq", [P, RING, H, STK], F16)
        stk = sb("stk", [P, 2, H, STK], F16)
        kT = sb("kT", [P, 2, NA, P], F16)
        qT = sb("qT", [P, RING, NA, P], F16)
        q2T = sb("q2T", [P, 2, NA, P], F16)
        kbd = sb("kbd", [P, RING, 2, 2 * NA, 2, S], F16)
        vx = sb("vx", [P, RING, 2, 8, 32])
        mx = sb("mx", [P, 2, H])
        pr = sb("pr", [P, 2, 2, 8, S])
        oT = sb("oT", [P, 2, 2, P])
        rden = sb("rden", [P, 2, H])
        on = sb("on", [P, 2, D])
        onT = sb("onT", [P, 2, P])
        xg = sb("xg", [P, 2, D])
        row = sb("row", [P, RING, ROW])
        row_h = row[:, :, :].bitcast(F16)
        st6b = sb("st6b", [P, 2, 6])
        mvb = sb("mvb", [P, 2, 2])
        rstdb = sb("rstdb", [P, 2, 1])
        z2 = sb("z2", [P, 2, D])
        z2T = sb("z2T", [P, 2, 2, P], F16)
        logit = sb("logit", [P, T, NE])

        lmax = sb("lmax", [P, T])
        ldif = sb("ldif", [P, T, NE])
        lexp = sb("lexp", [P, T, NE])
        lsum = sb("lsum", [P, T])
        gate = sb("gate", [P, T])
        gate_h = sb("gate_h", [P, 2, T], F16)
        eq = sb("eq", [P, T, NE])
        cand = sb("cand", [P, T, NE])
        cmax = sb("cmax", [P, T])
        oh_f = sb("oh_f", [P, T, NE])
        oh = sb("oh", [P, T, NE], F16)
        cum = sb("cum", [P, 2, 16 + T, NE])
        n_f = sb("n_f", [P, NE])
        n_i = sb("n_i", [P, 2, NE], I32)
        base = sb("base", [P, 2, 4 + NE])
        rank = sb("rank", [P, 3, T, NE])
        dest = sb("dest", [P, T])
        dest_i = sb("dest_i", [P, 3, T], I32)
        dest_f = sb("dest_f", [P, 2, T])
        place = sb("place", [P, T, P], F16)
        pay = sb("pay", [P, T, 4, NS], F16)
        tile_h = sb("tile_h", [P, T], F16)
        idx = sb("idx", [P, 4, NS])
        slot_gate = sb("slot_gate", [P, 2, NS])
        te_c = sb("te_c", [1, NS, NE - 1])
        te_f = sb("te_f", [1, NS])
        te_i = sb("te_i", [1, NS], I32)

        idx_s = sb("idx_s", [P, RING], I32)
        idx_o = sb("idx_o", [P, RING], I32)
        got = sb("got", [P, RING, ROW])
        got_h = got[:, :, :].bitcast(F16)
        gT = sb("gT", [P, 2, 2, P], F16)
        hT = sb("hT", [P, 2, FC, P])
        fin = sb("fin", [P, RING, D])

        ps = [stack.enter_context(nc.psum_tensor(f"ps{i}", [P, 1024], F32)) for i in range(4)]
        bank = [ps[i // 2][:, 512 * (i % 2):512 * (i % 2) + 512] for i in range(8)]

        def f_ps_T(par):
            return bank[par][:, 0:P].bitcast(F16)

        ps_st = ps[0]
        ps_s = ps[1]
        ps_zc = bank[4][:, 0:2 * D]
        ps_z2 = bank[4][:, 256:384].bitcast(F16)
        ps_stk = bank[5].bitcast(F16)
        ps_oT = bank[5][:, 0:2 * P]
        ps_onT = bank[5][:, 256:256 + P]
        ps_proj = bank[6][:, 0:3 * D]
        ps_lg = bank[6][:, 384:384 + NE]
        ps_q2 = bank[7][:, 0:2 * P].bitcast(F16)
        ps_o = bank[7][:, 256:256 + 2 * P]
        ps_op = bank[7][:, 0:D]

        s_const, s_wts, s_x0, s_x1, s_w1hi, s_w1lo, s_w2ld, s_bld = (sem(n) for n in (
            "const_loaded", "weights_loaded", "x_first_loaded", "x_loaded", "w1_hi_made", "w1_lo_made", "w2_loaded",
            "expert_biases_loaded"))
        s_w1ld = [sem(f"w1_loaded{i}") for i in range(2)]
        s_z0, s_wrs, s_bh, s_mb = sem("zeroed"), sem("router_split"), sem("expert_biases_split"), sem("mask_bias_made")
        s_init, s_mn, s_prep, s_setT, s_setE, s_tg = (sem(n) for n in (
            "buffers_zeroed", "mask_ready", "setup_steps", "setup_transposed", "setup_copied", "gates_ready"))
        ctx_ld = [sem(f"ctx_loaded{i}") for i in range(RING)]
        kbd_ld = [sem(f"kbd_loaded{i}") for i in range(RING)]
        row_st = [sem(f"row_stored{i}") for i in range(RING)]
        (bn_s, bn_a, rs1, z_rdy, zcT_done, zcT_ev, proj_done, qk_ev, v_ev, rope1, rope2, rope3, rope_done,
         hi_done, lo_done, stk_done, k_ev, q_ev, s_done, mx_done, nm_done, q2_done, q2_ev, st_done, p_rdy,
         pv_done, o_ev, oT_done, rden_done, on_done, onT_done, onT_ev, op_done, xg_done, x2_done, bn2_s, bn2_a, rs2, z2_done,
         zh_done, zl_done, z2T_done, z2T_ev, lg_done, lg_ev) = (sem(n) for n in (
             "stats", "mean_var", "rstd_made", "z_made", "zc_transposed", "zc_copied", "projected", "qk_copied",
             "v_copied", "rope_cos", "rope_sin", "rope_sum", "rope_made", "hi_made", "lo_made",
             "stacks_transposed", "k_copied", "q_copied", "scores_made", "max_made", "negmax_made",
             "q2_transposed", "q2_copied", "scoresT_made", "probs_made", "pv_made", "o_copied",
             "o_transposed", "rden_made", "o_normalised", "on_transposed", "on_copied", "attn_projected", "xg_made", "x2_made", "stats2",
             "mean_var2", "rstd2_made", "z2_made", "z2_hi_made", "z2_lo_made", "z2_transposed", "z2_copied",
             "logits_made", "logits_copied"))
        sp_passed, pool_passed, dve_passed = sem("sp_passed"), sem("pool_passed"), sem("dve_passed")
        rv1, rv2, mrow = sem("var_eps"), sem("var_eps2"), sem("max_row_cleared")
        km_done, kb_done, f_io = sem("keys_masked"), sem("mask_rows_made"), sem("ffn_index_out")
        r_dif, r_oh, r_pay = sem("route_differences"), sem("route_onehot"), sem("route_payload")
        r_step, r_exp, r_pe, r_tiles = (sem(n) for n in ("route_step", "route_exp", "route_products", "route_tiles"))
        (f_idx, f_T, f_Tev, f_h, f_gelu, f_y, f_x2, f_fin, f_zero) = (sem(n) for n in (
            "ffn_index", "ffn_transposed", "ffn_copied", "ffn_hidden", "ffn_gelu", "ffn_y", "ffn_x2", "ffn_final",
            "ffn_zeroed"))
        f_got = [sem(f"ffn_gathered{i}") for i in range(RING)]
        f_st = [sem(f"ffn_scattered{i}") for i in range(RING)]

        ctx_d = ctx_in.rearrange("b s d -> (b s) d").rearrange("(t p) d -> t p d", p=P)
        x_d = x.rearrange("b s d -> (b s) d").rearrange("(t p) d -> p t d", p=P)
        rows_d = rows.rearrange("(t p) n -> t p n", p=P)
        out_d = out.rearrange("b s d -> (b s) d")
        vec = lambda a: a.rearrange("(o n) -> o n", o=1)

        def swapped(a):
            return a.rearrange("p (c two) -> p c two", two=2)[:, :, ::-1]

        def paired(a):
            return a.rearrange("p (c two) -> p c two", two=2)

        def tile_of(a, t):
            return a[:, bass.ds(t, 1), :].rearrange("p o n -> p (o n)")

        LAST_LAG = 7
        PRO = 8

        def pipeline(eng, step):
            for i in range(PRO):
                step(i, i, 0)
            with eng.Fori(0, (T - PRO) // RING) as u:
                for k in range(RING):
                    step(PRO + k, u * RING + (PRO + k), u)
            for i in range(T, T + LAST_LAG):
                step(i, i, 0)

        def stage(i, it, lag, u):
            looped = not isinstance(it, int)
            t0 = i - lag
            on_ = looped or 0 <= t0 < T
            rnd = u + t0 // RING if looped else t0 // RING
            return on_, it - lag, t0 % RING, t0 % 2, rnd

        F_PRO, F_LAST = 7, 5

        def ffn_pipeline(eng, step):
            for i in range(F_PRO):
                step(i, i, 0)
            with eng.Fori(0, (NS - F_PRO) // RING) as u:
                for k in range(RING):
                    step(F_PRO + k, u * RING + (F_PRO + k), u)
            for i in range(NS, NS + F_LAST):
                step(i, i, 0)

        def fstage(i, it, lag, u):
            looped = not isinstance(it, int)
            t0 = i - lag
            on_ = looped or 0 <= t0 < NS
            rnd = u + t0 // RING if looped else t0 // RING
            return on_, it - lag, t0 % RING, t0 % 2, rnd

        N_WTS = 16 * 15
        block = stack.enter_context(nc.Block())

        @block.sync
        def _(sp):
            sp.dma_start(cf[:, :], const_f).then_inc(s_const, 16)
            sp.dma_start(x_all[:, 0:4, :], x_d[:, 0:4, :]).then_inc(s_x0, 16)
            sp.dma_start(ch[:, :], const_h).then_inc(s_const, 16)
            for n, w in enumerate((Wq, Wk, Wv, Wo)):
                sp.dma_start(w_nat[:, n, :], w).then_inc(s_wts, 16)
            sp.dma_start(mask_i[:, :], mask.rearrange("(t b) o s -> t (b o s)", b=2)).then_inc(s_wts, 16)
            sp.dma_start(bias_qk[:, 0:D], vec(bq).partition_broadcast(P)).then_inc(s_wts, 16)
            sp.dma_start(bias_qk[:, D:2 * D], vec(bk).partition_broadcast(P)).then_inc(s_wts, 16)
            sp.dma_start(bv_bc[:, :], vec(bv).partition_broadcast(P)).then_inc(s_wts, 16)
            sp.dma_start(bo_col[:, :], bo.rearrange("(p o) -> p o", o=1)).then_inc(s_wts, 16)
            sp.dma_start(gates[:, 0:1], vec(g_x).partition_broadcast(P)).then_inc(s_wts, 16)
            sp.dma_start(gates[:, 1:2], vec(g_f).partition_broadcast(P)).then_inc(s_wts, 16)
            sp.dma_start(wr_f[:, :], Wr).then_inc(s_wts, 16)
            sp.dma_start(br_bc[:, :], vec(br).partition_broadcast(P)).then_inc(s_wts, 16)
            sp.wait_ge(s_z0, 2)
            for r in (0, 32):
                sp.dma_start(b1_f[r:r + NE, :], b1).then_inc(s_bld, 16)
                sp.dma_start(b2_f[r:r + NE, :], b2).then_inc(s_bld, 16)
            sp.dma_start(x_all[:, 4:T, :], x_d[:, 4:T, :]).then_inc(s_x1, 16)

            for s in range(RING):
                sp.sem_inc(row_st[s], 16)

            def step(i, it, u):
                on_, t, s, par, rnd = stage(i, it, 0, u)
                if on_:
                    wait(sp, zcT_done, t - RING + 1)
                    alone(sp, sp_passed)
                    sp.dma_start(ctx_sb[:, s, :], ctx_d[bass.ds(t, 1), :, :].rearrange("o p d -> (o p) d")
                                 ).then_inc(ctx_ld[s], 16)
                if isinstance(it, int) and it < NE:
                    wait(sp, s_w1lo, it - 1)
                    sp.dma_start(w1_f[:, it % 2, :], W1[it]).then_inc(s_w1ld[it % 2], 16)
                    sp.dma_start(w2_f[:, it, :, :], W2[it].rearrange("(c p) d -> p c d", p=P)).then_inc(s_w2ld, 16)
                on_, t, s, par, rnd = stage(i, it, 2, u)
                if on_:
                    sp.wait_ge(k_ev, t + 1)
                    alone(sp, sp_passed)
                    wait(sp, st_done, t - RING + 1)
                    alone(sp, sp_passed)
                    for g in range(4):
                        r = slice(STK * g, STK * g + STK)
                        sp.dma_start(kbd[r, s, g // 2, :, g % 2, :],
                                     kT[r, par, :, :].rearrange("p a (b k) -> p (a b) k", b=2)).then_inc(kbd_ld[s], 16)
                on_, t, s, par, rnd = stage(i, it, 6, u)
                if on_:
                    sp.wait_ge(zl_done, t + 1)
                    alone(sp, sp_passed)
                    sp.dma_start(rows_d[bass.ds(t, 1), :, :].rearrange("o p n -> (o p) n"), row[:, s, :]
                                 ).then_inc(row_st[s], 16)

            pipeline(sp, step)
            for s in range(RING):
                sp.wait_ge(row_st[s], 16 + 16 * T // RING)

        @block.gpsimd
        def _(pool):
            pool.memset(kbd[:, :, :, :, :, :], 0.0).then_inc(s_init, 1)
            pool.wait_ge(s_const, 32)
            pool.wait_ge(s_wts, 16 * 13)
            pool.tensor_tensor(bias_rot[:, :], bias_qk[:, :], cos_t, ALU.mult).then_inc(rope1, 1)
            pool.tensor_tensor(paired(bias_tmp[:, :]), swapped(bias_qk[:, :]), paired(sin_t), ALU.mult).then_inc(rope2, 1)
            pool.wait_ge(rope1, 1)
            pool.wait_ge(rope2, 1)
            pool.tensor_tensor(bias_rot[:, :], bias_rot[:, :], bias_tmp[:, :], ALU.add).then_inc(rope3, 1)
            pool.wait_ge(rope3, 1)
            pool.wait_ge(s_setE, 6)
            pool.wait_ge(s_x0, 16)
            pool.wait_ge(s_x1, 16)

            def step(i, it, u):
                on_, t, s, par, rnd = stage(i, it, 0, u)
                if on_:
                    pool.wait_ge(bn_a, t + 1)
                    pool.tensor_tensor(rvar[:, par, 0:1], mv[:, par, 1:2], eps, ALU.add).then_inc(rv1, 1)
                    pool.wait_ge(rv1, t + 1)
                    pool.tensor_tensor(rstd[:, par, :], rvar[:, par, 0:1], power, ALU.pow).then_inc(rs1, 1)
                on_, t, s, par, rnd = stage(i, it, 5, u)
                if on_:
                    wait(pool, x2_done, t - 1)
                    pool.tensor_tensor(xg[:, par, :], tile_of(x_all, t), attn_c[:, :], ALU.add).then_inc(xg_done, 1)
                on_, t, s, par, rnd = stage(i, it, 1, u)
                if on_:
                    wait(pool, q2_done, t - RING + 1)
                    alone(pool, pool_passed)
                    pool.memset(stq[:, s, :, ROW_MAX:ROW_MAX + 1], 0.0).then_inc(mrow, 1)
                if on_:
                    pool.wait_ge(qk_ev, t + 1)
                    pool.wait_ge(rope1, t + 1)
                    wait(pool, hi_done, 2 * t - 2)
                    wait(pool, lo_done, 2 * t - 2)
                    pool.tensor_tensor(rot[:, par, :], qk[:, par, :], cos_t, ALU.mult).then_inc(rope1, 1)
                    pool.tensor_tensor(paired(rot_s[:, par, :]), swapped(qk[:, par, :]), paired(sin_t),
                                       ALU.mult).then_inc(rope2, 1)
                    pool.wait_ge(rope2, t + 2)
                    pool.tensor_tensor(rot[:, par, :], rot[:, par, :], rot_s[:, par, :], ALU.add).then_inc(rope3, 1)
                    pool.wait_ge(rope3, t + 2)
                    pool.tensor_tensor(rot[:, par, :], rot[:, par, :], bias_rot[:, :], ALU.add).then_inc(rope_done, 1)
                on_, t, s, par, rnd = stage(i, it, 5, u)
                if on_:
                    pool.wait_ge(bn2_a, t + 1)
                    pool.tensor_tensor(rvar[:, par, 1:2], mvb[:, par, 1:2], eps, ALU.add).then_inc(rv2, 1)
                    pool.wait_ge(rv2, t + 1)
                    pool.tensor_tensor(rstdb[:, par, :], rvar[:, par, 1:2], power, ALU.pow).then_inc(rs2, 1)
                on_, t, s, par, rnd = stage(i, it, 1, u)
                if on_:
                    pool.wait_ge(hi_done, 2 * t + 2)
                    q_f = rot[:, par, 0:D].rearrange("p (h d) -> p h d", d=HD)
                    k_f = rot[:, par, D:2 * D].rearrange("p (h d) -> p h d", d=HD)
                    pool.tensor_tensor(stq[:, s, :, 16:24], q_f, stq[:, s, :, 0:8], ALU.subtract
                                       ).then_inc(lo_done, 1)
                    pool.tensor_tensor(stk[:, par, :, 8:16], k_f, stk[:, par, :, 0:8], ALU.subtract
                                       ).then_inc(lo_done, 1)

            pipeline(pool, step)

            pool.wait_ge(f_zero, 1)
            for s in range(RING):
                pool.wait_ge(row_st[s], 16 + 16 * T // RING)

            def ffn(i, it, u):
                on_, t, s, par, rnd = fstage(i, it, 0, u)
                if on_:
                    pool.wait_ge(f_idx, t + 1)
                    wait(pool, f_x2, t - RING + 1)
                    wait(pool, f_T, t - RING + 1)
                    alone(pool, pool_passed)
                    pool.indirect_dma_start(
                        out=got[:, s, :], out_offset=None, in_=rows,
                        in_offset=bass.IndirectOffsetOnAxis(ap=idx_s[:, s:s + 1], axis=0),
                        bounds_check=B * S - 1, oob_is_err=False).then_inc(f_got[s], 16)
                on_, t, s, par, rnd = fstage(i, it, 4, u)
                if on_:
                    pool.wait_ge(f_fin, t + 1)
                    alone(pool, pool_passed)
                    pool.indirect_dma_start(
                        out=out_d, out_offset=bass.IndirectOffsetOnAxis(ap=idx_o[:, s:s + 1], axis=0),
                        in_=fin[:, s, :], in_offset=None,
                        bounds_check=B * S - 1, oob_is_err=False).then_inc(f_st[s], 16)

            ffn_pipeline(pool, ffn)
            for s in range(RING):
                pool.wait_ge(f_st[s], 16 * len(range(s, NS, RING)))

        @block.scalar
        def _(act):
            act.wait_ge(s_wts, 16 * 13)
            act.activation(tg[:, :], gates[:, :], ACT.Tanh).then_inc(s_tg, 1)
            for n in range(4):
                act.wait_ge(s_setT, n + 1)
                act.activation(wT[:, n, :], bank[n][:, 0:D], ACT.Copy).then_inc(s_setE, 1)
            act.wait_ge(s_setT, 5)
            act.activation(mask_f[:, :], bank[5][:, 0:T], ACT.Copy).then_inc(s_setE, 1)
            act.wait_ge(s_setT, 6)
            act.activation(attn_c[:, :], bank[6][:, 0:D], ACT.Copy).then_inc(s_setE, 1)

            def step(i, it, u):
                on_, t, s, par, rnd = stage(i, it, 1, u)
                if on_:
                    act.wait_ge(zcT_done, t + 1)
                    wait(act, proj_done, t - 1)
                    act.activation(zcT[:, par, :, :].rearrange("p a n -> p (a n)"), ps_zc, ACT.Copy).then_inc(zcT_ev, 1)
                on_, t, s, par, rnd = stage(i, it, 4, u)
                if on_:
                    act.wait_ge(q2_done, t + 1)
                    wait(act, st_done, t - 1)
                    act.activation(q2T[:, par, :, :].rearrange("p a n -> p (a n)"), ps_q2, ACT.Copy).then_inc(q2_ev, 1)
                on_, t, s, par, rnd = stage(i, it, 2, u)
                if on_:
                    act.wait_ge(k_ev, t + 1)
                    wait(act, s_done, t - RING + 1)
                    act.activation(qT[:, s, :, :].rearrange("p a n -> p (a n)"), ps_stk[:, 0:NA * P], ACT.Copy
                                   ).then_inc(q_ev, 1)
                if isinstance(it, int) and it < NE:
                    act.wait_ge(s_w1ld[it % 2], 16 * (it // 2 + 1))
                    act.activation(w1_h[:, it, :], w1_f[:, it % 2, :], ACT.Copy, scale=W1_SCALE).then_inc(s_w1hi, 1)
                on_, t, s, par, rnd = stage(i, it, 1, u)
                if on_:
                    act.wait_ge(proj_done, t + 1)
                    wait(act, rope_done, t - 1)
                    act.activation(qk[:, par, :], ps_proj[:, 0:2 * D], ACT.Copy).then_inc(qk_ev, 1)
                on_, t, s, par, rnd = stage(i, it, 5, u)
                if on_:
                    act.wait_ge(pv_done, t + 1)
                    wait(act, oT_done, t - 1)
                    act.activation(oT[:, par, :, :].rearrange("p a n -> p (a n)"), ps_o, ACT.Copy).then_inc(o_ev, 1)
                on_, t, s, par, rnd = stage(i, it, 1, u)
                if on_:
                    wait(act, pv_done, t - RING + 1)
                    v_ps = ps_proj[:, 2 * D:3 * D].rearrange("p (j hh d) -> p j hh d", hh=2, d=HD)
                    for b in range(2):
                        for hh in range(2):
                            act.activation(vx[64 * hh:64 * hh + 64, s, b, :, 16 * hh:16 * hh + HD],
                                           v_ps[64 * b:64 * b + 64, :, hh, :], ACT.Copy).then_inc(v_ev, 1)
                on_, t, s, par, rnd = stage(i, it, 4, u)
                if on_:
                    act.wait_ge(st_done, t + 1)
                    wait(act, pv_done, t - 1)
                    act.activation(pr[:, par, :, :, :].rearrange("p b j q -> p (b j q)"), ps_st[:, :], ACT.Exp,
                                   scale=SCALE).then_inc(p_rdy, 1)
                on_, t, s, par, rnd = stage(i, it, 5, u)
                if on_:
                    act.wait_ge(onT_done, t + 1)
                    wait(act, op_done, t - 1)
                    act.activation(onT[:, par, :], ps_onT, ACT.Copy).then_inc(onT_ev, 1)
                on_, t, s, par, rnd = stage(i, it, 6, u)
                if on_:
                    act.wait_ge(z2T_done, t + 1)
                    wait(act, lg_done, t - 1)
                    act.activation(z2T[:, par, :, :].rearrange("p a n -> p (a n)"), ps_z2, ACT.Copy).then_inc(z2T_ev, 1)

            pipeline(act, step)

            act.wait_ge(r_dif, 1)
            act.activation(lexp[:, :, :], ldif[:, :, :], ACT.Exp).then_inc(r_exp, 1)

            def ffn(i, it, u):
                on_, t, s, par, rnd = fstage(i, it, 2, u)
                if on_:
                    act.wait_ge(f_T, t + 1)
                    wait(act, f_h, t - 1)
                    act.activation(gT[:, par, :, :].rearrange("p a n -> p (a n)"), f_ps_T(par), ACT.Copy).then_inc(f_Tev, 1)
                on_, t, s, par, rnd = fstage(i, it, 3, u)
                if on_:
                    act.wait_ge(f_h, t + 1)
                    wait(act, f_y, t - 1)
                    act.activation(hT[:, par, :, :].rearrange("p c n -> p (c n)"), bank[2 + par], ACT.Gelu,
                                   scale=1.0 / W1_SCALE).then_inc(f_gelu, 1)

            ffn_pipeline(act, ffn)

        @block.tensor
        def _(pe):
            pe.wait_ge(s_const, 32)
            pe.wait_ge(s_wts, 16 * 13)
            for n in range(4):
                pe.transpose(bank[n][:, 0:D], w_nat[:, n, :], ident).then_inc(s_setT, 1)
            pe.wait_ge(s_mn, 2)
            pe.transpose(bank[5][:, 0:T], mask_n[:, :], cf[0:T, C_ID:C_ID + T]).then_inc(s_setT, 1)
            pe.wait_ge(s_prep, 4)
            pe.matmul(bank[6][:, 0:D], c_bc[:, :], ident, start=True, stop=True).then_inc(s_setT, 1)
            pe.wait_ge(s_setE, 6)

            def step(i, it, u):
                on_, t, s, par, rnd = stage(i, it, 1, u)
                if on_:
                    pe.wait_ge(z_rdy, t + 1)
                    pe.wait_ge(ctx_ld[s], rnd * 16 + 16)
                    wait(pe, zcT_ev, t)
                    wait(pe, z2T_ev, t - 5)
                    pe.transpose(ps_zc[:, 0:D], z[:, par, :], ident)
                    pe.transpose(ps_zc[:, D:2 * D], ctx_sb[:, s, :], ident).then_inc(zcT_done, 1)
                on_, t, s, par, rnd = stage(i, it, 4, u)
                if on_:
                    pe.wait_ge(nm_done, t + 1)
                    wait(pe, x2_done, t - 1)
                    for a in range(NA):
                        mm = pe.transpose(ps_q2[:, P * a:P * a + P],
                                          stq[:, s, 4 * a:4 * a + 4, :].rearrange("p h r -> p (h r)"), ident_h)
                    mm.then_inc(q2_done, 1)
                on_, t, s, par, rnd = stage(i, it, 2, u)
                if on_:
                    pe.wait_ge(lo_done, 2 * t + 2)
                    pe.wait_ge(hi_done, 2 * t + 2)
                    wait(pe, onT_ev, t - 3)
                    pe.wait_ge(mrow, t + 1)
                    wait(pe, q_ev, t)
                    for w in range(2):
                        for a in range(NA):
                            c = (w * NA + a) * P
                            src = stk[:, par, :, :] if w else stq[:, s, :, :]
                            mm = pe.transpose(ps_stk[:, c:c + P],
                                              src[:, 4 * a:4 * a + 4, :].rearrange("p h r -> p (h r)"), ident_h)
                    mm.then_inc(stk_done, 1)
                on_, t, s, par, rnd = stage(i, it, 1, u)
                if on_:
                    pe.wait_ge(zcT_ev, t + 1)
                    wait(pe, v_ev, t * 4)
                    wait(pe, lg_ev, t - 6)
                    pe.matmul(ps_proj[:, 0:D], zcT[:, par, 0, :], wT[:, 0, :], start=True, stop=True)
                    pe.matmul(ps_proj[:, D:3 * D], zcT[:, par, 1, :], wT[:, 1:3, :].rearrange("p a n -> p (a n)"),
                              start=True, stop=True).then_inc(proj_done, 1)
                on_, t, s, par, rnd = stage(i, it, 5, u)
                if on_:
                    pe.wait_ge(p_rdy, t + 1)
                    pe.wait_ge(v_ev, t * 4 + 4)
                    wait(pe, x2_done, t)
                    wait(pe, q2_ev, t + 2 if not isinstance(t, int) else min(t + 2, T))
                    for b in range(2):
                        for j in range(8):
                            r = 32 * (j % 4)
                            c = (j // 4) * P + b * S
                            mm = pe.matmul(ps_o[r:r + 32, c:c + S], vx[:, s, b, j, :], pr[:, par, b, j, :],
                                           start=True, stop=True)
                    mm.then_inc(pv_done, 1)
                on_, t, s, par, rnd = stage(i, it, 4, u)
                if on_:
                    pe.wait_ge(q2_ev, t + 1)
                    wait(pe, p_rdy, t)
                    for b in range(2):
                        for j in range(8):
                            mm = pe.matmul(ps_st[:, 512 * b + S * j:512 * b + S * j + S],
                                           kbd[:, s, j % 2, 2 * (j // 2) + b, :, :].rearrange("p h k -> p (h k)"),
                                           q2T[:, par, j // 2, S * b:S * b + S], start=True, stop=True)
                    mm.then_inc(st_done, 1)
                on_, t, s, par, rnd = stage(i, it, 5, u)
                if on_:
                    pe.wait_ge(o_ev, t + 1)
                    wait(pe, onT_ev, t)
                    wait(pe, q_ev, t + 4 if not isinstance(t, int) else min(t + 4, T))
                    for n in range(2):
                        mm = pe.transpose(ps_oT[:, P * n:P * n + P], oT[:, par, n, :], ident)
                    mm.then_inc(oT_done, 1)

                def scores(t, s, par, rnd, half):
                    if half == 0:
                        pe.wait_ge(kbd_ld[s], rnd * 64 + 64)
                        pe.wait_ge(q_ev, t + 1)
                        wait(pe, mx_done, t)
                    for j in range(4 * half, 4 * half + 4):
                        for b in range(2):
                            mm = pe.matmul(ps_s[S * b:S * b + S, P * j:P * j + P], qT[:, s, j // 2, S * b:S * b + S],
                                           kbd[:, s, j % 2, 2 * (j // 2) + b, :, :].rearrange("p h k -> p (h k)"),
                                           start=True, stop=True)
                    if half == 1:
                        mm.then_inc(s_done, 1)

                on_, t, s, par, rnd = stage(i, it, 3, u)
                if on_:
                    scores(t, s, par, rnd, 0)
                on_, t, s, par, rnd = stage(i, it, 5, u)
                if on_:
                    pe.wait_ge(on_done, t + 1)
                    pe.transpose(ps_onT, on[:, par, :], ident).then_inc(onT_done, 1)
                on_, t, s, par, rnd = stage(i, it, 3, u)
                if on_:
                    scores(t, s, par, rnd, 1)
                on_, t, s, par, rnd = stage(i, it, 5, u)
                if on_:
                    pe.wait_ge(onT_ev, t + 1)
                    pe.wait_ge(q2_ev, t + 2 if not isinstance(t, int) else min(t + 2, T))
                    pe.wait_ge(o_ev, t + 1)
                    pe.matmul(ps_op, onT[:, par, :], wT[:, 3, :], start=True, stop=True).then_inc(op_done, 1)
                on_, t, s, par, rnd = stage(i, it, 6, u)
                if on_:
                    pe.wait_ge(zl_done, t + 1)
                    wait(pe, z2T_ev, t)
                    pe.wait_ge(zcT_ev, t + 6 if not isinstance(t, int) else min(t + 6, T))
                    for n in range(2):
                        mm = pe.transpose(ps_z2[:, P * n:P * n + P], row_h[:, s, (2 + n) * D:(3 + n) * D], ident_h)
                    mm.then_inc(z2T_done, 1)
                on_, t, s, par, rnd = stage(i, it, 7, u)
                if on_:
                    pe.wait_ge(z2T_ev, t + 1)
                    pe.wait_ge(s_wrs, 2)
                    wait(pe, v_ev, t * 4 + 28 if not isinstance(t, int) else min(t * 4 + 28, 4 * T))
                    wait(pe, lg_ev, t)
                    pe.matmul(ps_lg, z2T[:, par, 0, :], wr_h[:, 0, :], start=True, stop=False)
                    pe.matmul(ps_lg, z2T[:, par, 1, :], wr_h[:, 0, :], start=False, stop=False)
                    pe.matmul(ps_lg, z2T[:, par, 0, :], wr_h[:, 1, :], start=False, stop=True).then_inc(lg_done, 1)

            pipeline(pe, step)

            pe.wait_ge(r_oh, 1)
            ohf = oh[:, :, :].rearrange("p t e -> p (t e)")
            pe.matmul(bank[0][:, 0:T * NE], tri_h, ohf, start=True, stop=True)
            pe.matmul(bank[1][:, 0:T * NE], ones_h, ohf, start=True, stop=True).then_inc(r_pe, 1)
            pe.wait_ge(r_pay, 6)
            for t in range(T):
                mm = pe.matmul(bank[2][:, 0:4 * NS], place[:, t, :], pay[:, t, :, :].rearrange("p c n -> p (c n)"),
                               start=(t == 0), stop=(t == T - 1))
            mm.then_inc(r_pe, 1)

            pe.wait_ge(r_tiles, 1)
            pe.wait_ge(s_w1lo, NE)
            pe.wait_ge(s_w2ld, 16 * NE)
            pe.wait_ge(s_bh, 4)

            def expert_of(t):
                return pe.value_load(te_i[0:1, bass.ds(t, 1)], min_val=0, max_val=NE - 1)

            def ffn(i, it, u):
                on_, t, s, par, rnd = fstage(i, it, 2, u)
                if on_:
                    pe.wait_ge(f_got[s], rnd * 16 + 16)
                    wait(pe, f_Tev, t - 1)
                    for n in range(2):
                        mm = pe.transpose(f_ps_T(par)[:, P * n:P * n + P], got_h[:, s, (2 + n) * D:(3 + n) * D], ident_h)
                    mm.then_inc(f_T, 1)
                on_, t, s, par, rnd = fstage(i, it, 3, u)
                if on_:
                    e = expert_of(t)
                    pe.wait_ge(f_Tev, t + 1)
                    wait(pe, f_gelu, t - 1)
                    for c in range(FC):
                        o = bank[2 + par][:, P * c:P * c + P]
                        w_h = w1_h[:, bass.ds(e, 1), P * c:P * c + P].rearrange("p o n -> p (o n)")
                        w_l = w1_l[:, bass.ds(e, 1), P * c:P * c + P].rearrange("p o n -> p (o n)")
                        one = exp_h[:, bass.ds(e, 1), :].rearrange("p o n -> p (o n)")
                        pe.matmul(o, b1_h[:, P * c:P * c + P], one, start=True, stop=False)
                        pe.matmul(o, w_h, gT[:, par, 0, :], start=False, stop=False)
                        pe.matmul(o, w_h, gT[:, par, 1, :], start=False, stop=False)
                        mm = pe.matmul(o, w_l, gT[:, par, 0, :], start=False, stop=True)
                    mm.then_inc(f_h, 1)
                on_, t, s, par, rnd = fstage(i, it, 4, u)
                if on_:
                    e = expert_of(t)
                    pe.wait_ge(f_gelu, t + 1)
                    wait(pe, f_fin, t - 1)
                    o = bank[4 + par][:, 0:D]
                    one = exp_h[:, bass.ds(e, 1), :].rearrange("p o n -> p (o n)")
                    pe.matmul(o, one, b2_h[:, :], start=True, stop=False)
                    for c in range(FC):
                        mm = pe.matmul(o, hT[:, par, c, :], w2_f[:, bass.ds(e, 1), c, :].rearrange("p o n -> p (o n)"),
                                       start=False, stop=(c == FC - 1))
                    mm.then_inc(f_y, 1)

            ffn_pipeline(pe, ffn)

        @block.vector
        def _(dve):
            dve.memset(b1_f[:, :], 0.0).then_inc(s_z0, 1)
            dve.memset(b2_f[:, :], 0.0).then_inc(s_z0, 1)
            dve.memset(stk[:, :, :, :], 0.0).then_inc(s_z0, 1)
            dve.memset(stq[:, :, :, :], 0.0).then_inc(s_z0, 1)
            dve.memset(vx[:, :, :, :, :], 0.0).then_inc(s_z0, 1)
            dve.wait_ge(s_z0, 5)
            dve.memset(stq[:, :, :, ROW_MASK:ROW_MASK + 1], 1.0).then_inc(s_z0, 1)
            dve.memset(stk[:, :, :, ROW_MAX:ROW_MAX + 1], 1.0).then_inc(s_z0, 1)
            for hh in range(2):
                dve.memset(vx[64 * hh:64 * hh + 64, :, :, :, 16 * hh + HD:16 * hh + HD + 1], 1.0).then_inc(s_z0, 1)
            dve.wait_ge(s_wts, 16 * 13)
            dve.wait_ge(s_const, 32)
            dve.tensor_copy(mask_n[:, :], mask_i[:, :]).then_inc(s_mn, 1)
            dve.wait_ge(s_mn, 1)
            dve.tensor_scalar(mask_n[:, :], mask_n[:, :], 0.0, None, ALU.not_equal).then_inc(s_mn, 1)
            dve.tensor_tensor(c_tmp[:, :], w_nat[:, 3, :], bv_bc[:, :], ALU.mult).then_inc(s_prep, 1)
            dve.wait_ge(s_prep, 1)
            dve.tensor_reduce(c_col[:, 0:1], c_tmp[:, :], AX.X, ALU.add).then_inc(s_prep, 1)
            dve.wait_ge(s_prep, 2)
            dve.wait_ge(s_tg, 1)
            dve.tensor_scalar(c_col[:, 1:2], c_col[:, 0:1], bo_col[:, :], tg[:, 0:1], ALU.add, ALU.mult).then_inc(s_prep, 1)
            dve.wait_ge(s_prep, 3)
            dve.tensor_scalar(c_bc[:, :], ones_h, c_col[:, 1:2], None, ALU.mult).then_inc(s_prep, 1)
            dve.tensor_copy(wr_h[:, 0, :], wr_f[:, :]).then_inc(s_wrs, 1)
            dve.wait_ge(s_wrs, 1)
            dve.tensor_tensor(wr_h[:, 1, :], wr_f[:, :], wr_h[:, 0, :], ALU.subtract).then_inc(s_wrs, 1)
            dve.wait_ge(s_bld, 64)
            dve.tensor_scalar(b1_h[:, :], b1_f[:, :], W1_SCALE, None, ALU.mult).then_inc(s_bh, 1)
            dve.tensor_copy(b2_h[:, :], b2_f[:, :]).then_inc(s_bh, 1)
            dve.wait_ge(s_bh, 2)
            lo = slice(32, 32 + NE)
            dve.scalar_tensor_tensor(out=b1_h[lo, :], in0=b1_f[lo, :], scalar=W1_SCALE, in1=b1_h[lo, :],
                                     op0=ALU.mult, op1=ALU.subtract).then_inc(s_bh, 1)
            dve.tensor_tensor(b2_h[lo, :], b2_f[lo, :], b2_h[lo, :], ALU.subtract).then_inc(s_bh, 1)
            dve.wait_ge(s_setE, 5)
            dve.tensor_scalar(mask_b[:, :], mask_f[:, :], 1.0, -MASKED, ALU.subtract, ALU.mult).then_inc(s_mb, 1)
            dve.wait_ge(s_mb, 1)
            dve.wait_ge(s_x0, 16)

            def ring_wait(sems, t, u, back, per):
                i_, it_ = t
                looped = not isinstance(it_, int)
                t0 = i_ - back
                if looped or t0 >= 0:
                    n = (u + t0 // RING if looped else t0 // RING) + 1
                    dve.wait_ge(sems[t0 % RING], n * per)

            def step(i, it, u):
                on_, t, s, par, rnd = stage(i, it, 0, u)
                if on_:
                    if isinstance(it, int) and it == 4:
                        dve.wait_ge(s_x1, 16)
                    dve.bn_stats(st6[:, par, :], tile_of(x_all, t)).then_inc(bn_s, 1)
                    dve.wait_ge(bn_s, t + 1)
                    alone(dve, dve_passed)
                    dve.bn_aggr(mv[:, par, :], st6[:, par, :]).then_inc(bn_a, 1)
                on_, t, s, par, rnd = stage(i, it, 6, u)
                if on_:
                    dve.wait_ge(rs2, t + 1)
                    wait(dve, zl_done, t - 1)
                    dve.tensor_scalar(z2[:, par, :], row[:, s, 0:D], mvb[:, par, 0:1], rstdb[:, par, :],
                                      ALU.subtract, ALU.mult).then_inc(z2_done, 1)
                    dve.wait_ge(z2_done, t + 1)
                    dve.tensor_copy(row_h[:, s, 2 * D:3 * D], z2[:, par, :]).then_inc(zh_done, 1)
                    dve.wait_ge(zh_done, t + 1)
                    dve.tensor_tensor(row_h[:, s, 3 * D:4 * D], z2[:, par, :], row_h[:, s, 2 * D:3 * D], ALU.subtract
                                      ).then_inc(zl_done, 1)
                on_, t, s, par, rnd = stage(i, it, 2, u)
                if on_:
                    dve.wait_ge(stk_done, t + 1)
                    ring_wait(kbd_ld, (i - 2, it), u, 2, 64)
                    dve.tensor_copy(kT[:, par, :, :].rearrange("p a n -> p (a n)"), ps_stk[:, NA * P:2 * NA * P]
                                    ).then_inc(k_ev, 1)
                on_, t, s, par, rnd = stage(i, it, 0, u)
                if on_:
                    dve.wait_ge(rs1, t + 1)
                    wait(dve, zcT_done, t - 1)
                    dve.tensor_scalar(z[:, par, :], tile_of(x_all, t), mv[:, par, 0:1], rstd[:, par, :],
                                      ALU.subtract, ALU.mult).then_inc(z_rdy, 1)
                if isinstance(it, int) and it < NE:
                    dve.wait_ge(s_w1hi, it + 1)
                    dve.scalar_tensor_tensor(out=w1_l[:, it, :], in0=w1_f[:, it % 2, :], scalar=W1_SCALE,
                                             in1=w1_h[:, it, :], op0=ALU.mult, op1=ALU.subtract).then_inc(s_w1lo, 1)
                on_, t, s, par, rnd = stage(i, it, 5, u)
                if on_:
                    dve.wait_ge(oT_done, t + 1)
                    wait(dve, on_done, t - 1)
                    o_ps = ps_oT.rearrange("p (h c) -> p h c", c=16)
                    dve.reciprocal(rden[:, par, :], o_ps[:, :, HD]).then_inc(rden_done, 1)
                    dve.wait_ge(rden_done, t + 1)
                    wait(dve, onT_done, t - 1)
                    dve.tensor_tensor(on[:, par, :].rearrange("p (h d) -> p h d", d=HD), o_ps[:, :, 0:HD],
                                      rden[:, par, :].rearrange("p (h o) -> p h o", o=1).broadcast_to([P, H, HD]),
                                      ALU.mult).then_inc(on_done, 1)
                on_, t, s, par, rnd = stage(i, it, 1, u)
                if on_:
                    dve.wait_ge(rope_done, t + 1)
                    wait(dve, stk_done, t - 1)
                    wait(dve, q2_done, t - RING + 1)
                    q_f = rot[:, par, 0:D].rearrange("p (h o d) -> p h o d", d=HD, o=1)
                    k_f = rot[:, par, D:2 * D]
                    dve.tensor_scalar(k_f, k_f, mask_f[:, bass.ds(t, 1)], None, ALU.mult).then_inc(km_done, 1)
                    dve.tensor_copy(stq[:, s, :, 0:16].rearrange("p h (c d) -> p h c d", c=2),
                                    q_f.broadcast_to([P, H, 2, HD])).then_inc(hi_done, 1)
                    dve.tensor_scalar(stk[:, par, :, ROW_MASK], cf[:, C_ONE:C_ONE + H], mask_b[:, bass.ds(t, 1)],
                                      None, ALU.mult).then_inc(kb_done, 1)
                    dve.wait_ge(km_done, t + 1)
                    k_hi = stk[:, par, :, 0:32].rearrange("p h (c d) -> p h c d", c=2)[:, :, :, 0:HD]
                    dve.tensor_copy(k_hi, k_f.rearrange("p (h o d) -> p h o d", d=HD, o=1).broadcast_to([P, H, 2, HD])
                                    ).then_inc(hi_done, 1)
                on_, t, s, par, rnd = stage(i, it, 3, u)
                if on_:
                    dve.wait_ge(s_done, t + 1)
                    dve.tensor_reduce(mx[:, par, :], ps_s[:, :].rearrange("p (h k) -> p h k", k=S), AX.X, ALU.max
                                      ).then_inc(mx_done, 1)
                    dve.wait_ge(mx_done, t + 1)
                    dve.wait_ge(stk_done, t + 1)
                    dve.tensor_scalar(stq[:, s, :, ROW_MAX], mx[:, par, :], -1.0, None, ALU.mult).then_inc(nm_done, 1)
                on_, t, s, par, rnd = stage(i, it, 5, u)
                if on_:
                    dve.wait_ge(op_done, t + 1)
                    dve.wait_ge(xg_done, t + 1)
                    dve.wait_ge(row_st[s], rnd * 16 + 16)
                    wait(dve, z2T_done, t - RING + 1)
                    dve.scalar_tensor_tensor(out=row[:, s, 0:D], in0=ps_op, scalar=tg[:, 0:1], in1=xg[:, par, :],
                                             op0=ALU.mult, op1=ALU.add).then_inc(x2_done, 1)
                    dve.wait_ge(x2_done, t + 1)
                    dve.bn_stats(st6b[:, par, :], row[:, s, 0:D]).then_inc(bn2_s, 1)
                    dve.wait_ge(bn2_s, t + 1)
                    alone(dve, dve_passed)
                    dve.bn_aggr(mvb[:, par, :], st6b[:, par, :]).then_inc(bn2_a, 1)
                on_, t, s, par, rnd = stage(i, it, 7, u)
                if on_:
                    dve.wait_ge(lg_done, t + 1)
                    dve.tensor_tensor(tile_of(logit, t), ps_lg, br_bc[:, :], ALU.add).then_inc(lg_ev, 1)

            pipeline(dve, step)

            steps = [0]

            def then(ins):
                steps[0] += 1
                ins.then_inc(r_step, 1)
                dve.wait_ge(r_step, steps[0])

            def bc(a, n):
                return a.rearrange("p (t o) -> p t o", o=1).broadcast_to([P, T, n])

            def over_t(a, n):
                return a.rearrange("p (o n) -> p o n", o=1).broadcast_to([P, T, n])

            dve.wait_ge(lg_ev, T)
            then(dve.memset(cum[:, :, :, :], 0.0))
            then(dve.memset(base[:, :, :], 0.0))
            then(dve.tensor_reduce(lmax[:, :], logit[:, :, :], AX.X, ALU.max))
            dve.tensor_tensor(ldif[:, :, :], logit[:, :, :], bc(lmax[:, :], NE), ALU.subtract).then_inc(r_dif, 1)
            then(dve.tensor_tensor(eq[:, :, :], logit[:, :, :], bc(lmax[:, :], NE), ALU.is_equal))
            then(dve.tensor_tensor(cand[:, :, :], eq[:, :, :], over_t(cf[:, C_REV:C_REV + NE], NE), ALU.mult))
            then(dve.tensor_reduce(cmax[:, :], cand[:, :, :], AX.X, ALU.max))
            dve.tensor_tensor(oh[:, :, :], cand[:, :, :], bc(cmax[:, :], NE), ALU.is_equal).then_inc(r_oh, 1)
            then(dve.tensor_tensor(oh_f[:, :, :], cand[:, :, :], bc(cmax[:, :], NE), ALU.is_equal))
            dve.wait_ge(r_exp, 1)
            then(dve.tensor_reduce(lsum[:, :], lexp[:, :, :], AX.X, ALU.add))
            then(dve.reciprocal(gate[:, :], lsum[:, :]))
            then(dve.tensor_copy(gate_h[:, 0, :], gate[:, :]))
            then(dve.tensor_tensor(gate_h[:, 1, :], gate[:, :], gate_h[:, 0, :], ALU.subtract))
            then(dve.tensor_copy(tile_h[:, :], cf[:, C_TILE:C_TILE + T]))
            dve.wait_ge(r_pe, 1)
            pre = bank[0][:, 0:T * NE].rearrange("p (t e) -> p t e", e=NE)
            tot = bank[1][:, 0:T * NE].rearrange("p (t e) -> p t e", e=NE)
            then(dve.tensor_copy(cum[:, 0, 16:16 + T, :], tot))
            for n in range(5):
                d = 1 << n
                a, b = cum[:, n % 2, :, :], cum[:, 1 - n % 2, :, :]
                then(dve.tensor_tensor(b[:, 16:16 + T, :], a[:, 16:16 + T, :], a[:, 16 - d:16 - d + T, :], ALU.add))
            run = cum[:, 1, 16:16 + T, :]
            then(dve.tensor_scalar(n_f[:, :], run[:, T - 1, :], float(P - 1), None, ALU.add))
            then(dve.tensor_copy(n_i[:, 0, :], n_f[:, :]))
            then(dve.tensor_scalar(n_i[:, 1, :], n_i[:, 0, :], 7, None, ALU.arith_shift_right))
            then(dve.tensor_copy(base[:, 0, 5:4 + NE], n_i[:, 1, 0:NE - 1]))
            for n in range(3):
                d = 1 << n
                a, b = base[:, n % 2, :], base[:, 1 - n % 2, :]
                then(dve.tensor_tensor(b[:, 4:4 + NE], a[:, 4:4 + NE], a[:, 4 - d:4 - d + NE], ALU.add))
            first = base[:, 1, 4:4 + NE]
            then(dve.tensor_tensor(rank[:, 0, :, :], run, tot, ALU.subtract))
            then(dve.tensor_tensor(rank[:, 1, :, :], rank[:, 0, :, :], pre, ALU.add))
            then(dve.scalar_tensor_tensor(out=rank[:, 0, :, :], in0=over_t(first, NE), scalar=float(P),
                                          in1=rank[:, 1, :, :], op0=ALU.mult, op1=ALU.add))
            then(dve.tensor_tensor(rank[:, 2, :, :], rank[:, 0, :, :], oh_f[:, :, :], ALU.mult))
            then(dve.tensor_reduce(dest[:, :], rank[:, 2, :, :], AX.X, ALU.add))
            then(dve.tensor_copy(dest_i[:, 0, :], dest[:, :]))
            then(dve.tensor_scalar(dest_i[:, 1, :], dest_i[:, 0, :], P - 1, None, ALU.bitwise_and))
            then(dve.tensor_scalar(dest_i[:, 2, :], dest_i[:, 0, :], 7, None, ALU.arith_shift_right))
            then(dve.tensor_copy(dest_f[:, 0, :], dest_i[:, 1, :]))
            then(dve.tensor_copy(dest_f[:, 1, :], dest_i[:, 2, :]))
            dve.tensor_tensor(place[:, :, :], over_t(iota, P), bc(dest_f[:, 0, :], P), ALU.is_equal).then_inc(r_pay, 1)
            dve.tensor_tensor(pay[:, :, 0, :], over_t(iota[:, 0:NS], NS), bc(dest_f[:, 1, :], NS), ALU.is_equal
                              ).then_inc(r_pay, 1)
            dve.wait_ge(r_pay, 2)
            for c, v in ((1, tile_h[:, :]), (2, gate_h[:, 0, :]), (3, gate_h[:, 1, :])):
                dve.tensor_tensor(pay[:, :, c, :], pay[:, :, 0, :], bc(v, NS), ALU.mult).then_inc(r_pay, 1)
            dve.wait_ge(r_pay, 5)
            dve.tensor_scalar(pay[:, :, 0, :], pay[:, :, 0, :], cf[:, C_PART:C_PART + 1], None, ALU.mult
                              ).then_inc(r_pay, 1)
            then(dve.tensor_tensor(te_c[:, :, :],
                                   cf[0:1, C_IOTA:C_IOTA + NS].rearrange("p (n o) -> p n o", o=1).broadcast_to([1, NS, NE - 1]),
                                   base[0:1, 1, 5:4 + NE].rearrange("p (o n) -> p o n", o=1).broadcast_to([1, NS, NE - 1]),
                                   ALU.is_ge))
            then(dve.tensor_reduce(te_f[:, :], te_c[:, :, :], AX.X, ALU.add))
            then(dve.tensor_copy(te_i[:, :], te_f[:, :]))
            dve.wait_ge(r_pe, 2)
            got_ps = bank[2][:, 0:4 * NS].rearrange("p (c n) -> p c n", c=4)
            then(dve.tensor_copy(idx[:, 0, :], got_ps[:, 0, :]))
            then(dve.tensor_scalar(idx[:, 1, :], idx[:, 0, :], 0.0, OUT_OF_RANGE, ALU.is_equal, ALU.mult))
            then(dve.scalar_tensor_tensor(out=idx[:, 2, :], in0=got_ps[:, 1, :], scalar=float(P), in1=idx[:, 1, :],
                                          op0=ALU.mult, op1=ALU.add))
            then(dve.scalar_tensor_tensor(out=idx[:, 3, :], in0=idx[:, 0, :], scalar=-1.0, in1=idx[:, 2, :],
                                          op0=ALU.add, op1=ALU.add))
            then(dve.tensor_copy(slot_gate[:, 0, :], got_ps[:, 2, :]))
            then(dve.tensor_tensor(slot_gate[:, 1, :], got_ps[:, 3, :], slot_gate[:, 0, :], ALU.add))
            then(dve.tensor_scalar(slot_gate[:, 0, :], slot_gate[:, 1, :], tg[:, 1:2], None, ALU.mult))
            dve.memset(got[:, :, :], 0.0).then_inc(f_zero, 1)
            dve.engine_nop().then_inc(r_tiles, 1)

            def ffn(i, it, u):
                on_, t, s, par, rnd = fstage(i, it, 0, u)
                if on_:
                    if s != s or not isinstance(it, int) or it >= RING:
                        dve.wait_ge(f_got[s], rnd * 16)
                    alone(dve, dve_passed)
                    dve.tensor_copy(idx_s[:, s:s + 1], idx[:, 3, bass.ds(t, 1)]).then_inc(f_idx, 1)
                on_, t, s, par, rnd = fstage(i, it, 2, u)
                if on_:
                    dve.wait_ge(f_got[s], rnd * 16 + 16)
                    wait(dve, f_st[s], rnd * 16)
                    alone(dve, dve_passed)
                    dve.tensor_copy(idx_o[:, s:s + 1], idx[:, 3, bass.ds(t, 1)]).then_inc(f_io, 1)
                    dve.tensor_copy(fin[:, s, :], got[:, s, 0:D]).then_inc(f_x2, 1)
                on_, t, s, par, rnd = fstage(i, it, 4, u)
                if on_:
                    dve.wait_ge(f_y, t + 1)
                    dve.wait_ge(f_x2, t + 1)
                    dve.scalar_tensor_tensor(out=fin[:, s, :], in0=bank[4 + par][:, 0:D],
                                             scalar=slot_gate[:, 0, bass.ds(t, 1)], in1=fin[:, s, :],
                                             op0=ALU.mult, op1=ALU.add).then_inc(f_fin, 1)

            ffn_pipeline(dve, ffn)


_INS = ['x', 'ctx_1024', 'mask_Bx1xS2_if1', 'g_xattn', 'g_ffn', 'L0_xattn_Wq', 'L0_xattn_bq', 'L0_xattn_Wk',
        'L0_xattn_bk', 'L0_xattn_Wv', 'L0_xattn_bv', 'L0_xattn_Wo', 'L0_xattn_bo', 'L0_ffn_W1', 'L0_ffn_b1',
        'L0_ffn_W2', 'L0_ffn_b2', 'L0_ffn_Wr', 'L0_ffn_br']


def kernel(**inputs):
    from concourse import bacc
    from concourse.bass_utils import run_bass_kernel_spmd

    nc = bacc.Bacc("TRN2", target_bir_lowering=False, num_devices=1)
    arrays, args = {}, []
    tables = dict(zip(("const_f", "const_h"), constants()))
    for name in _INS + list(tables):
        a = np.ascontiguousarray(tables[name] if name in tables else inputs[name])
        arrays[f"in_{name}"] = a
        args.append(nc.dram_tensor(f"in_{name}", a.shape, mybir.dt.from_np(a.dtype), kind="ExternalInput").ap())
    rows = nc.dram_tensor("rows", (B * S, ROW), F32, kind="Internal").ap()
    out = nc.dram_tensor("out_0", (B, S, D), F32, kind="ExternalOutput").ap()
    build(nc, *args, rows, out)
    r = run_bass_kernel_spmd(nc, [arrays], core_ids=[0])
    return r.results[0]["out_0"]
```

```python
import math
from contextlib import ExitStack

import numpy as np

import concourse.bass as bass
from concourse import mybir

F32 = mybir.dt.float32
F16 = mybir.dt.float16
I32 = mybir.dt.int32
ALU = mybir.AluOpType
ACT = mybir.ActivationFunctionType
AX = mybir.AxisListType

P = 128
B, S, D = 64, 64, 128
H, HD = 16, 8
T = B * S // P
NE, FF = 8, 512
FC = FF // P
NS = T + NE - 1
NA = 4
STK = 32
ROW_MAX, ROW_MASK = 24, 25
MASKED = -60000.0
SCALE = 1.0 / math.sqrt(HD)
EPS = 1e-5
OUT_OF_RANGE = 8192.0
ROW = 2 * D
RING = 4
UNROLL = 8
X_CH = 4
W_SCALE = 64.0

C_ID, C_SEL, C_COS, C_SIN = 0, 128, 256, 512
C_IOTA, C_REV, C_TILE, C_PART, C_ONE, C_POW, C_EPS, NCF = 768, 896, 904, 936, 937, 953, 954, 955
K_ID, K_TRI, K_ONE, K_EXP, NCH = 0, 128, 256, 384, 384 + NE * P


def constants():
    f = np.zeros((P, NCF), np.float32)
    h = np.zeros((P, NCH), np.float16)
    r = np.arange(P)
    f[:, C_ID:C_ID + P] = np.eye(P)
    f[:, C_SEL:C_SEL + P] = (r[:, None] // 16 == r[None, :] // 16) & (r[:, None] % 16 == HD)
    half = HD // 2
    div = np.exp(np.arange(half, dtype=np.float32) * np.float32(-(math.log(10000.0) / half)))
    ang = (np.arange(S, dtype=np.float32)[:, None] * div[None, :]).astype(np.float32)
    cos, sin = np.cos(ang.astype(np.float64)), np.sin(ang.astype(np.float64))
    c = np.repeat(cos, 2, axis=1)
    s = np.stack([-sin, sin], axis=-1).reshape(S, HD)
    f[:, C_COS:C_COS + 2 * D] = np.tile(c, (P // S, 2 * H))
    f[:, C_SIN:C_SIN + 2 * D] = np.tile(s, (P // S, 2 * H))
    f[:, C_IOTA:C_IOTA + P] = r[None, :]
    f[:, C_REV:C_REV + NE] = NE - np.arange(NE)[None, :]
    f[:, C_TILE:C_TILE + T] = np.arange(T)[None, :]
    f[:, C_PART] = r + 1
    f[:, C_ONE:C_ONE + H] = 1
    f[:, C_POW] = -0.5
    f[:, C_EPS] = EPS
    h[:, K_ID:K_ID + P] = np.eye(P)
    h[:, K_TRI:K_TRI + P] = r[:, None] < r[None, :]
    h[:, K_ONE:K_ONE + P] = 1
    e = h[:, K_EXP:].reshape(P, NE, P)
    for i in range(NE):
        e[i, i, :] = 1
        e[32 + i, i, :] = 1
    return f, h


def wait(eng, sem, n):
    if isinstance(n, int) and n <= 0:
        return
    eng.wait_ge(sem, n)


def alone(eng, passed):
    eng.sem_inc(passed, 1)


def build(nc, x, ctx_in, mask, g_x, g_f, Wq, bq, Wk, bk, Wv, bv, Wo, bo, W1, b1, W2, b2, Wr, br,
          const_f, const_h, rows, out):
    stack = ExitStack()
    with stack:
        def sb(name, shape, dt=F32):
            return stack.enter_context(nc.sbuf_tensor(name, shape, dt))

        def sem(name):
            return stack.enter_context(nc.semaphore(name))

        cf = sb("cf", [P, NCF])
        ch = sb("ch", [P, NCH], F16)
        ident = cf[:, C_ID:C_ID + P]
        cos_t = cf[:, C_COS:C_COS + 2 * D]
        sin_t = cf[:, C_SIN:C_SIN + 2 * D]
        iota = cf[:, C_IOTA:C_IOTA + P]
        power = cf[:, C_POW:C_POW + 1]
        eps = cf[:, C_EPS:C_EPS + 1]
        ident_h = ch[:, K_ID:K_ID + P]
        tri_h = ch[:, K_TRI:K_TRI + P]
        ones_h = ch[:, K_ONE:K_ONE + P]
        exp_h = ch[:, K_EXP:].rearrange("p (e n) -> p e n", e=NE)
        w_nat = sb("w_nat", [P, 4, D])
        w_h = sb("w_h", [P, 3, D], F16)
        w_l = sb("w_l", [P, 3, D], F16)
        woT = sb("woT", [P, D])
        bias_f = sb("bias_f", [P, 3 * D])
        bias_h = sb("bias_h", [P, 4 * D], F16)
        bv_bc = sb("bv_bc", [P, D])
        bo_col = sb("bo_col", [P, 1])
        c_tmp = sb("c_tmp", [P, D])
        c_col = sb("c_col", [P, 2])
        c_bc = sb("c_bc", [P, D])
        gates = sb("gates", [P, 2])
        tg = sb("tg", [P, 2])
        mask_i = sb("mask_i", [T, P], I32)
        mask_n = sb("mask_n", [T, P])
        mask_f = sb("mask_f", [P, T])
        mask_s = sb("mask_s", [P, T])
        mask_b = sb("mask_b", [P, T])
        wr_f = sb("wr_f", [P, NE])
        wr_h = sb("wr_h", [P, 2, NE], F16)
        br_bc = sb("br_bc", [P, NE])
        w1_f = sb("w1_f", [P, 2, FF])
        w1_h = sb("w1_h", [P, NE, FF], F16)
        w1_l = sb("w1_l", [P, NE, FF], F16)
        w2_f = sb("w2_f", [P, NE, FC, D])
        b1_f = sb("b1_f", [P, FF])
        b1_h = sb("b1_h", [P, FF], F16)
        b2_f = sb("b2_f", [P, D])
        b2_h = sb("b2_h", [P, D], F16)

        x_all = sb("x_all", [P, T, D])
        ctx_all = sb("ctx_all", [P, T, D])
        ctx_h = sb("ctx_h", [P, T, D], F16)
        ctx_l = sb("ctx_l", [P, T, D], F16)
        st6 = sb("st6", [P, T, 6])
        mv = sb("mv", [P, T, 2])
        rstd = sb("rstd", [P, T, 1])
        rvar = sb("rvar", [P, T, 1])
        z = sb("z", [P, 2, D])
        zT = sb("zT", [P, 2, 2, D], F16)
        cT = sb("cT", [P, 2, 2, D], F16)
        qk = sb("qk", [P, 2, 2 * D])
        rot = sb("rot", [P, 2, 2 * D])
        rot_s = sb("rot_s", [P, 2, 2 * D])
        stq = sb("stq", [P, RING, H, STK], F16)
        stk = sb("stk", [P, 2, H, STK], F16)
        kT = sb("kT", [P, 2, NA, P], F16)
        qT = sb("qT", [P, 2, NA, P], F16)
        q2T = sb("q2T", [P, 2, NA, P], F16)
        kbd = sb("kbd", [P, RING, 2, 2 * NA, 2, S], F16)
        vx = sb("vx", [P, UNROLL, 2, 8, 32])
        mx = sb("mx", [P, 2, H])
        pr = sb("pr", [P, 2, 2, 8, S])
        oT = sb("oT", [P, 2, 2, P])
        rden = sb("rden", [P, 2, H])
        on = sb("on", [P, 2, D])
        onT = sb("onT", [P, 2, P])
        row = sb("row", [P, RING, ROW])
        row_h = row[:, :, :].bitcast(F16)
        st6b = sb("st6b", [P, 2, 6])
        mvb = sb("mvb", [P, 2, 2])
        rstdb = sb("rstdb", [P, 2, 1])
        rvarb = sb("rvarb", [P, 2, 1])
        z2 = sb("z2", [P, 2, D])
        z2T = sb("z2T", [P, 2, 2, P], F16)
        logit = sb("logit", [P, T, NE])

        lmax = sb("lmax", [P, T])
        ldif = sb("ldif", [P, T, NE])
        lexp = sb("lexp", [P, T, NE])
        lsum = sb("lsum", [P, T])
        gate = sb("gate", [P, T])
        gate_h = sb("gate_h", [P, 2, T], F16)
        eq = sb("eq", [P, T, NE])
        cand = sb("cand", [P, T, NE])
        cmax = sb("cmax", [P, T])
        oh_f = sb("oh_f", [P, T, NE])
        oh = sb("oh", [P, T, NE], F16)
        cum = sb("cum", [P, 2, 16 + T, NE])
        n_f = sb("n_f", [P, NE])
        n_i = sb("n_i", [P, 2, NE], I32)
        base = sb("base", [P, 2, 4 + NE])
        rank = sb("rank", [P, 3, T, NE])
        dest = sb("dest", [P, T])
        dest_i = sb("dest_i", [P, 3, T], I32)
        dest_f = sb("dest_f", [P, 2, T])
        place = ctx_h
        pay = ctx_all[:, :, :].rearrange("p t d -> p (t d)")[:, 0:T * 2 * NS].bitcast(F16).rearrange(
            "p (t c n) -> p t c n", t=T, c=4)
        tile_h = sb("tile_h", [P, T], F16)
        idx = sb("idx", [P, 4, NS])
        slot_gate = sb("slot_gate", [P, 2, NS])
        te_c = sb("te_c", [1, NS, NE - 1])
        te_f = sb("te_f", [1, NS])
        te_i = sb("te_i", [1, NS], I32)

        idx_s = sb("idx_s", [P, RING], I32)
        idx_o = sb("idx_o", [P, RING], I32)
        got = sb("got", [P, RING, ROW])
        got_h = got[:, :, :].bitcast(F16)
        gT = sb("gT", [P, 2, 2, P], F16)
        hT = sb("hT", [P, 2, FC, P])
        fin = sb("fin", [P, RING, D])

        ps = [stack.enter_context(nc.psum_tensor(f"ps{i}", [P, 1024], F32)) for i in range(4)]
        bank = [ps[i // 2][:, 512 * (i % 2):512 * (i % 2) + 512] for i in range(8)]

        pick = exp_h[:, 0, :]

        def f_ps_T(par):
            return bank[par][:, 0:P].bitcast(F16)

        ps_st = ps[0]
        ps_s = ps[1]
        ps_z = bank[4][:, 0:D]
        ps_c = bank[4][:, D:2 * D].bitcast(F16)
        ps_q2 = bank[4][:, 0:2 * P].bitcast(F16)
        ps_lg = bank[4][:, 256:256 + NE]
        ps_stk = bank[5].bitcast(F16)
        ps_onT = bank[5][:, 0:P]
        ps_op = bank[5][:, 256:256 + D]
        ps_proj = bank[6][:, 0:3 * D]
        ps_z2 = bank[6][:, 384:384 + P].bitcast(F16)
        ps_o = bank[7][:, 0:2 * P]
        ps_oT = bank[7][:, 256:256 + 2 * P]

        s_const, s_wts, s_w1hi, s_w1lo, s_w2ld, s_bld, s_qkb = (sem(n) for n in (
            "const_loaded", "weights_loaded", "w1_hi_made", "w1_lo_made", "w2_loaded", "expert_biases_loaded",
            "biases_loaded"))
        s_x = [sem(f"x_loaded{c}") for c in range(X_CH)]
        s_c = [sem(f"context_loaded{c}") for c in range(X_CH)]
        s_ch, s_cl = sem("context_hi_made"), sem("context_lo_made")
        s_late = sem("late_weights_loaded")
        s_wh, s_wl, s_bq = sem("weights_hi_made"), sem("weights_lo_made"), sem("biases_split")
        s_w1ld = [sem(f"w1_loaded{i}") for i in range(2)]
        s_z0, s_wrs, s_bh, s_mb = sem("zeroed"), sem("router_split"), sem("expert_biases_split"), sem("mask_bias_made")
        s_init, s_mn, s_prep, s_setT, s_setE, s_tg = (sem(n) for n in (
            "buffers_zeroed", "mask_ready", "setup_steps", "setup_transposed", "setup_copied", "gates_ready"))
        kbd_ld = [sem(f"kbd_loaded{i}") for i in range(RING)]
        row_st = [sem(f"row_stored{i}") for i in range(RING)]
        (bn_s, bn_a, rs1, z_rdy, zcT_done, zch_ev, c_ev, zcl_ev, proj_done, qk_ev, v_ev, rope1, rope2, rope_done,
         hi_done, lo_done, stk_done, k_ev, q_ev, s_done, mx_done, nm_done, q2_done, q2_ev, st_done, p_rdy,
         pv_done, o_ev, oT_done, rden_done, on_done, onT_done, onT_ev, op_done, x2_done, bn2_s, bn2_a, rs2, z2_done,
         zh_done, zl_done, z2T_done, z2T_ev, lg_done, lg_ev) = (sem(n) for n in (
             "stats", "mean_var", "rstd_made", "z_made", "zc_transposed", "z_hi_made", "context_copied", "z_lo_made", "projected",
             "qk_copied", "v_copied", "rope_cos", "rope_sin", "rope_made", "hi_made", "lo_made",
             "stacks_transposed", "k_copied", "q_copied", "scores_made", "max_made", "negmax_made",
             "q2_transposed", "q2_copied", "scoresT_made", "probs_made", "pv_made", "o_copied",
             "o_transposed", "rden_made", "o_normalised", "on_transposed", "on_copied", "attn_projected", "x2_made",
             "stats2", "mean_var2", "rstd2_made", "z2_made", "z2_hi_made", "z2_lo_made", "z2_transposed", "z2_copied",
             "logits_made", "logits_copied"))
        sp_passed, pool_passed, dve_passed = sem("sp_passed"), sem("pool_passed"), sem("dve_passed")
        rv1, rv2, mrow = sem("var_eps"), sem("var_eps2"), sem("max_row_cleared")
        kb_done, f_io = sem("mask_rows_made"), sem("ffn_index_out")
        r_dif, r_oh, r_pay = sem("route_differences"), sem("route_onehot"), sem("route_payload")
        r_step, r_exp, r_pe, r_tiles = (sem(n) for n in ("route_step", "route_exp", "route_products", "route_tiles"))
        (f_idx, f_T, f_Tev, f_h, f_gelu, f_y, f_x2, f_fin, f_zero) = (sem(n) for n in (
            "ffn_index", "ffn_transposed", "ffn_copied", "ffn_hidden", "ffn_gelu", "ffn_y", "ffn_x2", "ffn_final",
            "ffn_zeroed"))
        f_got = [sem(f"ffn_gathered{i}") for i in range(RING)]
        f_st = [sem(f"ffn_scattered{i}") for i in range(RING)]

        c_d = ctx_in.rearrange("b s d -> (b s) d").rearrange("(t p) d -> p t d", p=P)
        x_d = x.rearrange("b s d -> (b s) d").rearrange("(t p) d -> p t d", p=P)
        rows_d = rows.rearrange("(t p) n -> t p n", p=P)
        out_d = out.rearrange("b s d -> (b s) d")
        vec = lambda a: a.rearrange("(o n) -> o n", o=1)

        def swapped(a):
            return a.rearrange("p (c two) -> p c two", two=2)[:, :, ::-1]

        def paired(a):
            return a.rearrange("p (c two) -> p c two", two=2)

        def tile_of(a, t):
            return a[:, bass.ds(t, 1), :].rearrange("p o n -> p (o n)")

        LAST_LAG = 7
        PRO = 8

        def pipeline(eng, step):
            for i in range(PRO):
                step(i, i, 0)
            with eng.Fori(0, (T - PRO) // UNROLL) as u:
                for k in range(UNROLL):
                    step(PRO + k, u * UNROLL + (PRO + k), u * (UNROLL // RING))
            for i in range(T, T + LAST_LAG):
                step(i, i, 0)

        def stage(i, it, lag, u):
            looped = not isinstance(it, int)
            t0 = i - lag
            on_ = looped or 0 <= t0 < T
            rnd = u + t0 // RING if looped else t0 // RING
            return on_, it - lag, t0 % RING, t0 % 2, rnd

        def upto(n, per=1):
            return min(n, T) * per if isinstance(n, int) else n * per

        F_PRO, F_LAST, F_UNROLL = 7, 5, RING

        def ffn_pipeline(eng, step):
            for i in range(F_PRO):
                step(i, i, 0)
            with eng.Fori(0, (NS - F_PRO) // F_UNROLL) as v:
                for k in range(F_UNROLL):
                    step(F_PRO + k, v * F_UNROLL + (F_PRO + k), v * (F_UNROLL // RING))
            for i in range(NS, NS + F_LAST):
                step(i, i, 0)

        def fstage(i, it, lag, u):
            looped = not isinstance(it, int)
            t0 = i - lag
            on_ = looped or 0 <= t0 < NS
            rnd = u + t0 // RING if looped else t0 // RING
            return on_, it - lag, t0 % RING, t0 % 2, rnd

        N_WTS = 16 * 7
        block = stack.enter_context(nc.Block())

        @block.sync
        def _(sp):
            nx = T // X_CH
            sp.dma_start(cf[:, :], const_f).then_inc(s_const, 16)
            sp.dma_start(x_all[:, 0:nx, :], x_d[:, 0:nx, :]).then_inc(s_x[0], 16)
            for n, w in enumerate((Wq, Wk, Wv, Wo)):
                sp.dma_start(w_nat[:, n, :], w).then_inc(s_wts, 16)
            sp.dma_start(mask_i[:, :], mask.rearrange("(t b) o s -> t (b o s)", b=2)).then_inc(s_wts, 16)
            sp.dma_start(ch[:, :], const_h).then_inc(s_const, 16)
            sp.dma_start(bv_bc[:, :], vec(bv).partition_broadcast(P)).then_inc(s_wts, 16)
            sp.dma_start(bo_col[:, :], bo.rearrange("(p o) -> p o", o=1)).then_inc(s_wts, 16)
            sp.wait_ge(s_z0, 3)
            for r in (0, 32):
                sp.dma_start(bias_f[r:r + 1, 0:D], vec(bq)).then_inc(s_qkb, 16)
                sp.dma_start(bias_f[r:r + 1, D:2 * D], vec(bk)).then_inc(s_qkb, 16)
            sp.dma_start(ctx_all[:, 0:nx, :], c_d[:, 0:nx, :]).then_inc(s_c[0], 16)
            for c in range(1, X_CH):
                ts = slice(c * nx, c * nx + nx)
                sp.dma_start(x_all[:, ts, :], x_d[:, ts, :]).then_inc(s_x[c], 16)
                sp.dma_start(ctx_all[:, ts, :], c_d[:, ts, :]).then_inc(s_c[c], 16)
            sp.dma_start(gates[:, 0:1], vec(g_x).partition_broadcast(P)).then_inc(s_late, 16)
            sp.dma_start(gates[:, 1:2], vec(g_f).partition_broadcast(P)).then_inc(s_late, 16)
            sp.dma_start(wr_f[:, :], Wr).then_inc(s_late, 16)
            sp.dma_start(br_bc[:, :], vec(br).partition_broadcast(P)).then_inc(s_late, 16)
            for r in (0, 32):
                sp.dma_start(b1_f[r:r + NE, :], b1).then_inc(s_bld, 16)
                sp.dma_start(b2_f[r:r + NE, :], b2).then_inc(s_bld, 16)
            for s in range(RING):
                sp.sem_inc(row_st[s], 16)

            def step(i, it, u):
                on_, t, s, par, rnd = stage(i, it, 1, u)
                if on_:
                    sp.wait_ge(k_ev, t + 1)
                    alone(sp, sp_passed)
                    wait(sp, st_done, t - RING + 1)
                    alone(sp, sp_passed)
                    for g in range(4):
                        r = slice(STK * g, STK * g + STK)
                        sp.dma_start(kbd[r, s, g // 2, :, g % 2, :],
                                     kT[r, par, :, :].rearrange("p a (b k) -> p (a b) k", b=2)).then_inc(kbd_ld[s], 16)
                if isinstance(it, int) and it < NE:
                    wait(sp, s_w1lo, it - 1)
                    sp.dma_start(w1_f[:, it % 2, :], W1[it]).then_inc(s_w1ld[it % 2], 16)
                    sp.dma_start(w2_f[:, it, :, :], W2[it].rearrange("(c p) d -> p c d", p=P)).then_inc(s_w2ld, 16)
                on_, t, s, par, rnd = stage(i, it, 6, u)
                if on_:
                    sp.wait_ge(zl_done, t + 1)
                    alone(sp, sp_passed)
                    sp.dma_start(rows_d[bass.ds(t, 1), :, :].rearrange("o p n -> (o p) n"), row[:, s, :]
                                 ).then_inc(row_st[s], 16)

            pipeline(sp, step)
            for s in range(RING):
                sp.wait_ge(row_st[s], 16 + 16 * T // RING)

        @block.gpsimd
        def _(pool):
            pool.memset(kbd[:, :, :, :, :, :], 0.0).then_inc(s_init, 1)
            pool.wait_ge(s_const, 32)

            def rstd_of(c):
                ts = slice(c * T // X_CH, (c + 1) * T // X_CH)
                pool.wait_ge(bn_a, (c + 1) * T // X_CH)
                pool.tensor_tensor(rvar[:, ts, :], mv[:, ts, 1:2], eps.rearrange("p (o n) -> p o n", o=1).broadcast_to(
                    [P, T // X_CH, 1]), ALU.add).then_inc(rv1, 1)
                pool.wait_ge(rv1, c + 1)
                pool.tensor_tensor(rstd[:, ts, :], rvar[:, ts, :], power.rearrange("p (o n) -> p o n", o=1).broadcast_to(
                    [P, T // X_CH, 1]), ALU.pow).then_inc(rs1, 1)

            def context_lo(c):
                ts = slice(c * T // X_CH, (c + 1) * T // X_CH)
                pool.wait_ge(s_ch, c + 1)
                pool.tensor_tensor(ctx_l[:, ts, :], ctx_all[:, ts, :], ctx_h[:, ts, :], ALU.subtract).then_inc(s_cl, 1)

            rstd_of(0)
            context_lo(0)

            def step(i, it, u):
                on_, t, s, par, rnd = stage(i, it, 1, u)
                if on_:
                    pool.wait_ge(hi_done, 2 * t + 2)
                    q_f = rot[:, par, 0:D].rearrange("p (h d) -> p h d", d=HD)
                    k_f = rot[:, par, D:2 * D].rearrange("p (h d) -> p h d", d=HD)
                    pool.tensor_tensor(stq[:, s, :, 16:24], q_f, stq[:, s, :, 0:8], ALU.subtract
                                       ).then_inc(lo_done, 1)
                    pool.tensor_tensor(stk[:, par, :, 8:16], k_f, stk[:, par, :, 0:8], ALU.subtract
                                       ).then_inc(lo_done, 1)
                on_, t, s, par, rnd = stage(i, it, 6, u)
                if on_:
                    pool.wait_ge(bn2_a, t + 1)
                    pool.tensor_tensor(rvarb[:, par, :], mvb[:, par, 1:2], eps, ALU.add).then_inc(rv2, 1)
                    pool.wait_ge(rv2, t + 1)
                    pool.tensor_tensor(rstdb[:, par, :], rvarb[:, par, :], power, ALU.pow).then_inc(rs2, 1)
                on_, t, s, par, rnd = stage(i, it, 0, u)
                if on_:
                    wait(pool, q2_done, t - RING + 1)
                    alone(pool, pool_passed)
                    pool.memset(stq[:, s, :, ROW_MAX:ROW_MAX + 1], 0.0).then_inc(mrow, 1)
                    pool.wait_ge(qk_ev, 2 * t + 2)
                    wait(pool, hi_done, 2 * t - 2)
                    wait(pool, lo_done, 2 * t - 2)
                    pool.tensor_tensor(rot[:, par, :], qk[:, par, :], cos_t, ALU.mult).then_inc(rope1, 1)
                    pool.tensor_tensor(paired(rot_s[:, par, :]), swapped(qk[:, par, :]), paired(sin_t),
                                       ALU.mult).then_inc(rope2, 1)
                    pool.wait_ge(rope2, t + 1)
                    pool.tensor_tensor(rot[:, par, :], rot[:, par, :], rot_s[:, par, :], ALU.add).then_inc(rope_done, 1)
                if isinstance(it, int) and it + 1 < X_CH:
                    rstd_of(it + 1)
                    context_lo(it + 1)

            pipeline(pool, step)

            pool.wait_ge(f_zero, 1)
            for s in range(RING):
                pool.wait_ge(row_st[s], 16 + 16 * T // RING)

            def ffn(i, it, u):
                on_, t, s, par, rnd = fstage(i, it, 0, u)
                if on_:
                    pool.wait_ge(f_idx, t + 1)
                    wait(pool, f_x2, t - RING + 1)
                    wait(pool, f_T, t - RING + 1)
                    alone(pool, pool_passed)
                    pool.indirect_dma_start(
                        out=got[:, s, :], out_offset=None, in_=rows,
                        in_offset=bass.IndirectOffsetOnAxis(ap=idx_s[:, s:s + 1], axis=0),
                        bounds_check=B * S - 1, oob_is_err=False).then_inc(f_got[s], 16)
                on_, t, s, par, rnd = fstage(i, it, 5, u)
                if on_:
                    pool.wait_ge(f_fin, t + 1)
                    alone(pool, pool_passed)
                    pool.indirect_dma_start(
                        out=out_d, out_offset=bass.IndirectOffsetOnAxis(ap=idx_o[:, s:s + 1], axis=0),
                        in_=fin[:, s, :], in_offset=None,
                        bounds_check=B * S - 1, oob_is_err=False).then_inc(f_st[s], 16)

            ffn_pipeline(pool, ffn)
            for s in range(RING):
                pool.wait_ge(f_st[s], 16 * len(range(s, NS, RING)))

        @block.scalar
        def _(act):
            for n in range(3):
                act.wait_ge(s_setT, n + 1)
                act.activation(w_h[:, n, :], bank[n][:, 0:D], ACT.Copy, scale=W_SCALE).then_inc(s_wh, 1)
            act.wait_ge(s_setT, 4)
            act.activation(woT[:, :], bank[3][:, 0:D], ACT.Copy).then_inc(s_setE, 1)
            act.wait_ge(s_setT, 5)
            act.activation(mask_f[:, :], bank[5][:, 0:T], ACT.Copy).then_inc(s_setE, 1)
            act.wait_ge(s_mb, 2)

            def context_hi(c):
                ts = slice(c * T // X_CH, (c + 1) * T // X_CH)
                act.wait_ge(s_c[c], 16)
                act.activation(ctx_h[:, ts, :], ctx_all[:, ts, :], ACT.Copy).then_inc(s_ch, 1)

            context_hi(0)

            def step(i, it, u):
                on_, t, s, par, rnd = stage(i, it, 7, u)
                if on_:
                    act.wait_ge(z2T_done, t + 1)
                    act.activation(z2T[:, par, :, :].rearrange("p a n -> p (a n)"), ps_z2, ACT.Copy).then_inc(z2T_ev, 1)
                on_, t, s, par, rnd = stage(i, it, 0, u)
                if on_:
                    act.wait_ge(zcT_done, t + 1)
                    wait(act, proj_done, t - 1)
                    act.activation(zT[:, par, 0, :], ps_z, ACT.Copy).then_inc(zch_ev, 1)
                    act.activation(cT[:, par, :, :].rearrange("p a n -> p (a n)"), ps_c, ACT.Copy).then_inc(c_ev, 1)
                on_, t, s, par, rnd = stage(i, it, 4, u)
                if on_:
                    act.wait_ge(st_done, t + 1)
                    wait(act, pv_done, t - 1)
                    act.activation(pr[:, par, :, :, :].rearrange("p b j q -> p (b j q)"), ps_st[:, :], ACT.Exp,
                                   scale=SCALE).then_inc(p_rdy, 1)
                on_, t, s, par, rnd = stage(i, it, 1, u)
                if on_:
                    act.wait_ge(k_ev, t + 1)
                    wait(act, s_done, t - 1)
                    act.activation(qT[:, par, :, :].rearrange("p a n -> p (a n)"), ps_stk[:, 0:NA * P], ACT.Copy
                                   ).then_inc(q_ev, 1)
                on_, t, s, par, rnd = stage(i, it, 0, u)
                if on_:
                    act.wait_ge(proj_done, t + 1)
                    wait(act, rope2, t - 1)
                    act.activation(qk[:, par, 0:D], ps_proj[:, 0:D], ACT.Copy, scale=1.0 / W_SCALE).then_inc(qk_ev, 1)
                    act.activation(qk[:, par, D:2 * D], ps_proj[:, D:2 * D], ACT.Identity,
                                   scale=mask_s[:, bass.ds(t, 1)]).then_inc(qk_ev, 1)
                    wait(act, pv_done, t - UNROLL + 1)
                    v_ps = ps_proj[:, 2 * D:3 * D].rearrange("p (j hh d) -> p j hh d", hh=2, d=HD)
                    for b in range(2):
                        for hh in range(2):
                            act.activation(vx[64 * hh:64 * hh + 64, i % UNROLL, b, :, 16 * hh:16 * hh + HD],
                                           v_ps[64 * b:64 * b + 64, :, hh, :], ACT.Copy, scale=1.0 / W_SCALE
                                           ).then_inc(v_ev, 1)
                    wait(act, stk_done, t - 1)
                    act.activation(stk[:, par, :, ROW_MASK], cf[:, C_ONE:C_ONE + H], ACT.Identity,
                                   scale=mask_b[:, bass.ds(t, 1)]).then_inc(kb_done, 1)
                if isinstance(it, int) and it < NE:
                    act.wait_ge(s_w1ld[it % 2], 16 * (it // 2 + 1))
                    act.activation(w1_h[:, it, :], w1_f[:, it % 2, :], ACT.Copy, scale=W_SCALE).then_inc(s_w1hi, 1)
                on_, t, s, par, rnd = stage(i, it, 3, u)
                if on_:
                    act.wait_ge(q2_done, t + 1)
                    wait(act, st_done, t - 1)
                    act.activation(q2T[:, par, :, :].rearrange("p a n -> p (a n)"), ps_q2, ACT.Copy).then_inc(q2_ev, 1)
                on_, t, s, par, rnd = stage(i, it, 5, u)
                if on_:
                    act.wait_ge(onT_done, t + 1)
                    wait(act, op_done, t - 1)
                    act.activation(onT[:, par, :], ps_onT, ACT.Copy).then_inc(onT_ev, 1)
                on_, t, s, par, rnd = stage(i, it, 4, u)
                if on_:
                    act.wait_ge(pv_done, t + 1)
                    wait(act, oT_done, t - 1)
                    act.activation(oT[:, par, :, :].rearrange("p a n -> p (a n)"), ps_o, ACT.Copy).then_inc(o_ev, 1)
                if isinstance(it, int) and it + 1 < X_CH:
                    context_hi(it + 1)
                if isinstance(it, int) and it == X_CH:
                    act.wait_ge(s_late, 64)
                    act.activation(tg[:, :], gates[:, :], ACT.Tanh).then_inc(s_tg, 1)

            pipeline(act, step)

            act.wait_ge(r_dif, 1)
            act.activation(lexp[:, :, :], ldif[:, :, :], ACT.Exp).then_inc(r_exp, 1)

            def ffn(i, it, u):
                on_, t, s, par, rnd = fstage(i, it, 2, u)
                if on_:
                    act.wait_ge(f_T, t + 1)
                    wait(act, f_h, t - 1)
                    act.activation(gT[:, par, :, :].rearrange("p a n -> p (a n)"), f_ps_T(par), ACT.Copy).then_inc(f_Tev, 1)
                on_, t, s, par, rnd = fstage(i, it, 3, u)
                if on_:
                    act.wait_ge(f_h, t + 1)
                    wait(act, f_y, t - 1)
                    act.activation(hT[:, par, :, :].rearrange("p c n -> p (c n)"), bank[2 + par], ACT.Gelu,
                                   scale=1.0 / W_SCALE).then_inc(f_gelu, 1)

            ffn_pipeline(act, ffn)

        @block.tensor
        def _(pe):
            pe.wait_ge(s_const, 32)
            pe.wait_ge(s_wts, N_WTS)
            for n in range(4):
                pe.transpose(bank[n][:, 0:D], w_nat[:, n, :], ident).then_inc(s_setT, 1)
            pe.wait_ge(s_mn, 2)
            pe.transpose(bank[5][:, 0:T], mask_n[:, :], cf[0:T, C_ID:C_ID + T]).then_inc(s_setT, 1)
            pe.wait_ge(s_prep, 4)
            pe.matmul(bank[6][:, 0:D], c_bc[:, :], ident, start=True, stop=True).then_inc(s_setT, 1)
            pe.wait_ge(s_wl, 3)
            pe.wait_ge(s_bq, 4)
            pe.wait_ge(s_setE, 2)

            def step(i, it, u):
                on_, t, s, par, rnd = stage(i, it, 7, u)
                if on_:
                    pe.wait_ge(zl_done, t + 1)
                    pe.wait_ge(v_ev, upto(t + 7, 4))
                    wait(pe, z2T_ev, t)
                    for n in range(2):
                        mm = pe.transpose(ps_z2[:, P * n:P * n + P], row_h[:, s, (2 + n) * D:(3 + n) * D], ident_h)
                    mm.then_inc(z2T_done, 1)
                on_, t, s, par, rnd = stage(i, it, 0, u)
                if on_:
                    if isinstance(it, int) and it in (0, PRO - 1):
                        pe.wait_ge(s_cl, 1 if it == 0 else X_CH)
                    pe.wait_ge(z_rdy, t + 1)
                    wait(pe, zcl_ev, t)
                    wait(pe, c_ev, t)
                    wait(pe, q2_ev, t - 3)
                    wait(pe, lg_ev, t - 7)
                    pe.transpose(ps_z, z[:, par, :], ident)
                    pe.transpose(ps_c[:, 0:D], tile_of(ctx_h, t), ident_h)
                    pe.transpose(ps_c[:, D:2 * D], tile_of(ctx_l, t), ident_h).then_inc(zcT_done, 1)
                on_, t, s, par, rnd = stage(i, it, 5, u)
                if on_:
                    pe.wait_ge(o_ev, t + 1)
                    for n in range(2):
                        mm = pe.transpose(ps_oT[:, P * n:P * n + P], oT[:, par, n, :], ident)
                    mm.then_inc(oT_done, 1)
                on_, t, s, par, rnd = stage(i, it, 1, u)
                if on_:
                    wait(pe, q_ev, t)
                    wait(pe, x2_done, t - 4)
                    pe.wait_ge(mrow, t + 1)
                    pe.wait_ge(kb_done, t + 1)
                    pe.wait_ge(hi_done, 2 * t + 2)
                    pe.wait_ge(lo_done, 2 * t + 2)
                    for w in range(2):
                        for a in range(NA):
                            c = (w * NA + a) * P
                            src = stk[:, par, :, :] if w else stq[:, s, :, :]
                            mm = pe.transpose(ps_stk[:, c:c + P],
                                              src[:, 4 * a:4 * a + 4, :].rearrange("p h r -> p (h r)"), ident_h)
                    mm.then_inc(stk_done, 1)
                on_, t, s, par, rnd = stage(i, it, 0, u)
                if on_:
                    pe.wait_ge(zch_ev, t + 1)
                    wait(pe, v_ev, t * 4)
                    wait(pe, z2T_ev, t - 6)
                    pe.wait_ge(c_ev, t + 1)
                    pe.wait_ge(zcl_ev, t + 1)
                    pe.matmul(ps_proj, pick, bias_h[:, 0:3 * D], start=True, stop=False)
                    for n, (half, w) in enumerate(((0, w_h), (1, w_h), (0, w_l))):
                        pe.matmul(ps_proj[:, 0:D], zT[:, par, half, :], w[:, 0, :], start=False, stop=False)
                        mm = pe.matmul(ps_proj[:, D:3 * D], cT[:, par, half, :], w[:, 1:3, :].rearrange("p a n -> p (a n)"),
                                       start=False, stop=(n == 2))
                    mm.then_inc(proj_done, 1)
                on_, t, s, par, rnd = stage(i, it, 2, u)
                if on_:
                    pe.wait_ge(kbd_ld[s], rnd * 64 + 64)
                    pe.wait_ge(q_ev, t + 1)
                    wait(pe, mx_done, t)
                    for j in range(8):
                        for b in range(2):
                            mm = pe.matmul(ps_s[S * b:S * b + S, P * j:P * j + P], qT[:, par, j // 2, S * b:S * b + S],
                                           kbd[:, s, j % 2, 2 * (j // 2) + b, :, :].rearrange("p h k -> p (h k)"),
                                           start=True, stop=True)
                    mm.then_inc(s_done, 1)
                on_, t, s, par, rnd = stage(i, it, 3, u)
                if on_:
                    pe.wait_ge(nm_done, t + 1)
                    pe.wait_ge(zcl_ev, upto(t + 4))
                    pe.wait_ge(c_ev, upto(t + 4))
                    wait(pe, lg_ev, t - 4)
                    for a in range(NA):
                        mm = pe.transpose(ps_q2[:, P * a:P * a + P],
                                          stq[:, s, 4 * a:4 * a + 4, :].rearrange("p h r -> p (h r)"), ident_h)
                    mm.then_inc(q2_done, 1)
                on_, t, s, par, rnd = stage(i, it, 4, u)
                if on_:
                    pe.wait_ge(p_rdy, t + 1)
                    pe.wait_ge(v_ev, t * 4 + 4)
                    wait(pe, on_done, t)
                    for b in range(2):
                        for j in range(8):
                            r = 32 * (j % 4)
                            c = (j // 4) * P + b * S
                            mm = pe.matmul(ps_o[r:r + 32, c:c + S], vx[:, (i - 4) % UNROLL, b, j, :], pr[:, par, b, j, :],
                                           start=True, stop=True)
                    mm.then_inc(pv_done, 1)
                on_, t, s, par, rnd = stage(i, it, 5, u)
                if on_:
                    pe.wait_ge(on_done, t + 1)
                    pe.wait_ge(q_ev, upto(t + 5))
                    wait(pe, x2_done, t)
                    pe.transpose(ps_onT, on[:, par, :], ident).then_inc(onT_done, 1)
                on_, t, s, par, rnd = stage(i, it, 7, u)
                if on_:
                    pe.wait_ge(z2T_ev, t + 1)
                    pe.wait_ge(q2_ev, upto(t + 5))
                    wait(pe, lg_ev, t)
                    if i == 7:
                        pe.wait_ge(s_wrs, 2)
                    pe.matmul(ps_lg, z2T[:, par, 0, :], wr_h[:, 0, :], start=True, stop=False)
                    pe.matmul(ps_lg, z2T[:, par, 1, :], wr_h[:, 0, :], start=False, stop=False)
                    pe.matmul(ps_lg, z2T[:, par, 0, :], wr_h[:, 1, :], start=False, stop=True).then_inc(lg_done, 1)
                on_, t, s, par, rnd = stage(i, it, 3, u)
                if on_:
                    pe.wait_ge(q2_ev, t + 1)
                    wait(pe, p_rdy, t)
                    for b in range(2):
                        for j in range(8):
                            mm = pe.matmul(ps_st[:, 512 * b + S * j:512 * b + S * j + S],
                                           kbd[:, s, j % 2, 2 * (j // 2) + b, :, :].rearrange("p h k -> p (h k)"),
                                           q2T[:, par, j // 2, S * b:S * b + S], start=True, stop=True)
                    mm.then_inc(st_done, 1)
                on_, t, s, par, rnd = stage(i, it, 5, u)
                if on_:
                    pe.wait_ge(onT_ev, t + 1)
                    pe.matmul(ps_op, pick, bias_h[:, 3 * D:4 * D], start=True, stop=False)
                    pe.matmul(ps_op, onT[:, par, :], woT[:, :], start=False, stop=True).then_inc(op_done, 1)

            pipeline(pe, step)

            pe.wait_ge(r_oh, 1)
            ohf = oh[:, :, :].rearrange("p t e -> p (t e)")
            pe.matmul(bank[0][:, 0:T * NE], tri_h, ohf, start=True, stop=True)
            pe.matmul(bank[1][:, 0:T * NE], ones_h, ohf, start=True, stop=True).then_inc(r_pe, 1)
            pe.wait_ge(r_pay, 6)
            for t in range(T):
                mm = pe.matmul(bank[2][:, 0:4 * NS], place[:, t, :], pay[:, t, :, :].rearrange("p c n -> p (c n)"),
                               start=(t == 0), stop=(t == T - 1))
            mm.then_inc(r_pe, 1)

            pe.wait_ge(r_tiles, 1)
            pe.wait_ge(s_w1lo, NE)
            pe.wait_ge(s_w2ld, 16 * NE)
            pe.wait_ge(s_bh, 4)

            experts = {}
            in_range = "the number of an expert is a sum of seven comparisons, so 0 to 7"

            def load_experts(first_tile, n, first):
                regs = nc.values_load_multi_w_load_instructions(
                    te_i[0:1, bass.ds(first_tile, n)], engines=[mybir.EngineType.PE], min_val=0, max_val=NE - 1,
                    skip_runtime_bounds_check_because=in_range)[1]
                experts.clear()
                experts.update({first + m: r for m, r in enumerate(regs)})

            def ffn(i, it, u):
                if not isinstance(it, int) and i == F_PRO:
                    load_experts(it - 4, F_UNROLL + 1, i - 4)
                if isinstance(it, int) and it in (3, NS):
                    load_experts(i - 3 if it == 3 else NS - 4, 4, 0 if it == 3 else NS - 4)
                on_, t, s, par, rnd = fstage(i, it, 2, u)
                if on_:
                    pe.wait_ge(f_got[s], rnd * 16 + 16)
                    wait(pe, f_Tev, t - 1)
                    for n in range(2):
                        mm = pe.transpose(f_ps_T(par)[:, P * n:P * n + P], got_h[:, s, (2 + n) * D:(3 + n) * D], ident_h)
                    mm.then_inc(f_T, 1)
                on_, t, s, par, rnd = fstage(i, it, 3, u)
                if on_:
                    e = experts[i - 3]
                    pe.wait_ge(f_Tev, t + 1)
                    wait(pe, f_gelu, t - 1)
                    for c in range(FC):
                        o = bank[2 + par][:, P * c:P * c + P]
                        w_h = w1_h[:, bass.ds(e, 1), P * c:P * c + P].rearrange("p o n -> p (o n)")
                        w_l = w1_l[:, bass.ds(e, 1), P * c:P * c + P].rearrange("p o n -> p (o n)")
                        one = exp_h[:, bass.ds(e, 1), :].rearrange("p o n -> p (o n)")
                        pe.matmul(o, b1_h[:, P * c:P * c + P], one, start=True, stop=False)
                        pe.matmul(o, w_h, gT[:, par, 0, :], start=False, stop=False)
                        pe.matmul(o, w_h, gT[:, par, 1, :], start=False, stop=False)
                        mm = pe.matmul(o, w_l, gT[:, par, 0, :], start=False, stop=True)
                    mm.then_inc(f_h, 1)
                on_, t, s, par, rnd = fstage(i, it, 4, u)
                if on_:
                    e = experts[i - 4]
                    pe.wait_ge(f_gelu, t + 1)
                    wait(pe, f_fin, t - 1)
                    o = bank[4 + par][:, 0:D]
                    one = exp_h[:, bass.ds(e, 1), :].rearrange("p o n -> p (o n)")
                    pe.matmul(o, one, b2_h[:, :], start=True, stop=False)
                    for c in range(FC):
                        mm = pe.matmul(o, hT[:, par, c, :], w2_f[:, bass.ds(e, 1), c, :].rearrange("p o n -> p (o n)"),
                                       start=False, stop=(c == FC - 1))
                    mm.then_inc(f_y, 1)

            ffn_pipeline(pe, ffn)

        @block.vector
        def _(dve):
            dve.memset(b1_f[:, :], 0.0).then_inc(s_z0, 1)
            dve.memset(b2_f[:, :], 0.0).then_inc(s_z0, 1)
            dve.memset(bias_f[:, :], 0.0).then_inc(s_z0, 1)
            dve.memset(bias_h[:, :], 0.0).then_inc(s_z0, 1)
            dve.memset(stk[:, :, :, :], 0.0).then_inc(s_z0, 1)
            dve.memset(stq[:, :, :, :], 0.0).then_inc(s_z0, 1)
            dve.memset(vx[:, :, :, :, :], 0.0).then_inc(s_z0, 1)
            dve.wait_ge(s_z0, 7)
            dve.memset(stq[:, :, :, ROW_MASK:ROW_MASK + 1], 1.0).then_inc(s_z0, 1)
            dve.memset(stk[:, :, :, ROW_MAX:ROW_MAX + 1], 1.0).then_inc(s_z0, 1)
            for hh in range(2):
                dve.memset(vx[64 * hh:64 * hh + 64, :, :, :, 16 * hh + HD:16 * hh + HD + 1], 1.0).then_inc(s_z0, 1)

            def stats_of(c):
                dve.wait_ge(s_x[c], 16)
                ts = range(c * T // X_CH, (c + 1) * T // X_CH)
                for t in ts:
                    dve.bn_stats(st6[:, t, :], x_all[:, t, :]).then_inc(bn_s, 1)
                for t in ts:
                    dve.wait_ge(bn_s, t + 1)
                    dve.bn_aggr(mv[:, t, :], st6[:, t, :]).then_inc(bn_a, 1)

            stats_of(0)
            dve.wait_ge(s_wts, N_WTS)
            dve.wait_ge(s_const, 32)
            dve.tensor_copy(mask_n[:, :], mask_i[:, :]).then_inc(s_mn, 1)
            dve.wait_ge(s_mn, 1)
            dve.tensor_scalar(mask_n[:, :], mask_n[:, :], 0.0, None, ALU.not_equal).then_inc(s_mn, 1)
            dve.tensor_tensor(c_tmp[:, :], w_nat[:, 3, :], bv_bc[:, :], ALU.mult).then_inc(s_prep, 1)
            dve.wait_ge(s_prep, 1)
            dve.tensor_reduce(c_col[:, 0:1], c_tmp[:, :], AX.X, ALU.add).then_inc(s_prep, 1)
            dve.wait_ge(s_prep, 2)
            dve.tensor_scalar(c_col[:, 1:2], c_col[:, 0:1], bo_col[:, :], None, ALU.add).then_inc(s_prep, 1)
            dve.wait_ge(s_prep, 3)
            dve.tensor_scalar(c_bc[:, :], ones_h, c_col[:, 1:2], None, ALU.mult).then_inc(s_prep, 1)
            for n in range(3):
                dve.wait_ge(s_wh, n + 1)
                dve.scalar_tensor_tensor(out=w_l[:, n, :], in0=bank[n][:, 0:D], scalar=W_SCALE, in1=w_h[:, n, :],
                                         op0=ALU.mult, op1=ALU.subtract).then_inc(s_wl, 1)
            up, low = slice(0, 64), slice(32, 64)
            dve.wait_ge(s_qkb, 64)
            dve.tensor_scalar(bias_h[up, 0:3 * D], bias_f[up, :], W_SCALE, None, ALU.mult).then_inc(s_bq, 1)
            dve.wait_ge(s_setT, 6)
            dve.tensor_copy(bias_h[up, 3 * D:4 * D], bank[6][up, 0:D]).then_inc(s_bq, 1)
            dve.wait_ge(s_bq, 2)
            dve.scalar_tensor_tensor(out=bias_h[low, 0:3 * D], in0=bias_f[low, :], scalar=W_SCALE,
                                     in1=bias_h[low, 0:3 * D], op0=ALU.mult, op1=ALU.subtract).then_inc(s_bq, 1)
            dve.tensor_tensor(bias_h[low, 3 * D:4 * D], bank[6][low, 0:D], bias_h[low, 3 * D:4 * D], ALU.subtract
                              ).then_inc(s_bq, 1)
            dve.wait_ge(s_setE, 2)
            dve.tensor_scalar(mask_b[:, :], mask_f[:, :], 1.0, -MASKED, ALU.subtract, ALU.mult).then_inc(s_mb, 1)
            dve.tensor_scalar(mask_s[:, :], mask_f[:, :], 1.0 / W_SCALE, None, ALU.mult).then_inc(s_mb, 1)
            dve.wait_ge(s_z0, 11)

            def late_weights():
                dve.wait_ge(s_late, 64)
                dve.tensor_copy(wr_h[:, 0, :], wr_f[:, :]).then_inc(s_wrs, 1)
                dve.wait_ge(s_wrs, 1)
                dve.tensor_tensor(wr_h[:, 1, :], wr_f[:, :], wr_h[:, 0, :], ALU.subtract).then_inc(s_wrs, 1)
                dve.wait_ge(s_bld, 64)
                dve.tensor_scalar(b1_h[:, :], b1_f[:, :], W_SCALE, None, ALU.mult).then_inc(s_bh, 1)
                dve.tensor_copy(b2_h[:, :], b2_f[:, :]).then_inc(s_bh, 1)
                dve.wait_ge(s_bh, 2)
                lo = slice(32, 32 + NE)
                dve.scalar_tensor_tensor(out=b1_h[lo, :], in0=b1_f[lo, :], scalar=W_SCALE, in1=b1_h[lo, :],
                                         op0=ALU.mult, op1=ALU.subtract).then_inc(s_bh, 1)
                dve.tensor_tensor(b2_h[lo, :], b2_f[lo, :], b2_h[lo, :], ALU.subtract).then_inc(s_bh, 1)

            def step(i, it, u):
                on_, t, s, par, rnd = stage(i, it, 0, u)
                if on_:
                    if isinstance(it, int) and it in (0, PRO - 1):
                        dve.wait_ge(rs1, 1 if it == 0 else X_CH)
                    wait(dve, zcT_done, t - 1)
                    dve.tensor_scalar(z[:, par, :], tile_of(x_all, t), tile_of(mv[:, :, 0:1], t), tile_of(rstd, t),
                                      ALU.subtract, ALU.mult).then_inc(z_rdy, 1)
                on_, t, s, par, rnd = stage(i, it, 6, u)
                if on_:
                    if i == 6:
                        dve.wait_ge(s_tg, 1)
                    dve.wait_ge(op_done, t + 1)
                    dve.wait_ge(row_st[s], rnd * 16 + 16)
                    dve.scalar_tensor_tensor(out=row[:, s, 0:D], in0=ps_op, scalar=tg[:, 0:1], in1=tile_of(x_all, t),
                                             op0=ALU.mult, op1=ALU.add).then_inc(x2_done, 1)
                    dve.wait_ge(x2_done, t + 1)
                    dve.bn_stats(st6b[:, par, :], row[:, s, 0:D]).then_inc(bn2_s, 1)
                    dve.wait_ge(bn2_s, t + 1)
                    alone(dve, dve_passed)
                    dve.bn_aggr(mvb[:, par, :], st6b[:, par, :]).then_inc(bn2_a, 1)
                on_, t, s, par, rnd = stage(i, it, 0, u)
                if on_:
                    dve.wait_ge(zch_ev, t + 1)
                    dve.wait_ge(c_ev, t + 1)
                    wait(dve, proj_done, t - 1)
                    dve.tensor_tensor(zT[:, par, 1, :], ps_z, zT[:, par, 0, :], ALU.subtract).then_inc(zcl_ev, 1)
                on_, t, s, par, rnd = stage(i, it, 1, u)
                if on_:
                    dve.wait_ge(stk_done, t + 1)
                    if not isinstance(it, int) or i >= 3:
                        dve.wait_ge(kbd_ld[(i - 3) % RING], (u + (i - 3) // RING + 1) * 64)
                    dve.tensor_copy(kT[:, par, :, :].rearrange("p a n -> p (a n)"), ps_stk[:, NA * P:2 * NA * P]
                                    ).then_inc(k_ev, 1)
                on_, t, s, par, rnd = stage(i, it, 5, u)
                if on_:
                    dve.wait_ge(oT_done, t + 1)
                    wait(dve, on_done, t - 1)
                    o_ps = ps_oT.rearrange("p (h c) -> p h c", c=16)
                    dve.reciprocal(rden[:, par, :], o_ps[:, :, HD]).then_inc(rden_done, 1)
                    dve.wait_ge(rden_done, t + 1)
                    wait(dve, onT_done, t - 1)
                    dve.tensor_tensor(on[:, par, :].rearrange("p (h d) -> p h d", d=HD), o_ps[:, :, 0:HD],
                                      rden[:, par, :].rearrange("p (h o) -> p h o", o=1).broadcast_to([P, H, HD]),
                                      ALU.mult).then_inc(on_done, 1)
                on_, t, s, par, rnd = stage(i, it, 6, u)
                if on_:
                    dve.wait_ge(rs2, t + 1)
                    wait(dve, zl_done, t - 1)
                    dve.tensor_scalar(z2[:, par, :], row[:, s, 0:D], mvb[:, par, 0:1], rstdb[:, par, :],
                                      ALU.subtract, ALU.mult).then_inc(z2_done, 1)
                on_, t, s, par, rnd = stage(i, it, 2, u)
                if on_:
                    dve.wait_ge(s_done, t + 1)
                    dve.tensor_reduce(mx[:, par, :], ps_s[:, :].rearrange("p (h k) -> p h k", k=S), AX.X, ALU.max
                                      ).then_inc(mx_done, 1)
                    dve.wait_ge(mx_done, t + 1)
                    dve.tensor_scalar(stq[:, s, :, ROW_MAX], mx[:, par, :], -1.0, None, ALU.mult).then_inc(nm_done, 1)
                on_, t, s, par, rnd = stage(i, it, 6, u)
                if on_:
                    dve.wait_ge(z2_done, t + 1)
                    dve.tensor_copy(row_h[:, s, 2 * D:3 * D], z2[:, par, :]).then_inc(zh_done, 1)
                    dve.wait_ge(zh_done, t + 1)
                    dve.tensor_tensor(row_h[:, s, 3 * D:4 * D], z2[:, par, :], row_h[:, s, 2 * D:3 * D], ALU.subtract
                                      ).then_inc(zl_done, 1)
                if isinstance(it, int) and it < NE:
                    dve.wait_ge(s_w1hi, it + 1)
                    dve.scalar_tensor_tensor(out=w1_l[:, it, :], in0=w1_f[:, it % 2, :], scalar=W_SCALE,
                                             in1=w1_h[:, it, :], op0=ALU.mult, op1=ALU.subtract).then_inc(s_w1lo, 1)
                on_, t, s, par, rnd = stage(i, it, 0, u)
                if on_:
                    dve.wait_ge(rope_done, t + 1)
                    wait(dve, stk_done, t - 1)
                    wait(dve, q2_done, t - RING + 1)
                    q_f = rot[:, par, 0:D].rearrange("p (h o d) -> p h o d", d=HD, o=1)
                    k_f = rot[:, par, D:2 * D].rearrange("p (h o d) -> p h o d", d=HD, o=1)
                    dve.tensor_copy(stq[:, s, :, 0:16].rearrange("p h (c d) -> p h c d", c=2),
                                    q_f.broadcast_to([P, H, 2, HD])).then_inc(hi_done, 1)
                    k_hi = stk[:, par, :, 0:32].rearrange("p h (c d) -> p h c d", c=2)[:, :, :, 0:HD]
                    dve.tensor_copy(k_hi, k_f.broadcast_to([P, H, 2, HD])).then_inc(hi_done, 1)
                on_, t, s, par, rnd = stage(i, it, 7, u)
                if on_:
                    dve.wait_ge(lg_done, t + 1)
                    dve.tensor_tensor(tile_of(logit, t), ps_lg, br_bc[:, :], ALU.add).then_inc(lg_ev, 1)
                if isinstance(it, int) and it + 1 < X_CH:
                    stats_of(it + 1)
                if isinstance(it, int) and it == X_CH:
                    late_weights()

            pipeline(dve, step)

            steps = [0]

            def then(ins):
                steps[0] += 1
                ins.then_inc(r_step, 1)
                dve.wait_ge(r_step, steps[0])

            def bc(a, n):
                return a.rearrange("p (t o) -> p t o", o=1).broadcast_to([P, T, n])

            def over_t(a, n):
                return a.rearrange("p (o n) -> p o n", o=1).broadcast_to([P, T, n])

            dve.wait_ge(lg_ev, T)
            then(dve.memset(cum[:, :, :, :], 0.0))
            then(dve.memset(base[:, :, :], 0.0))
            then(dve.tensor_reduce(lmax[:, :], logit[:, :, :], AX.X, ALU.max))
            dve.tensor_tensor(ldif[:, :, :], logit[:, :, :], bc(lmax[:, :], NE), ALU.subtract).then_inc(r_dif, 1)
            then(dve.tensor_tensor(eq[:, :, :], logit[:, :, :], bc(lmax[:, :], NE), ALU.is_equal))
            then(dve.tensor_tensor(cand[:, :, :], eq[:, :, :], over_t(cf[:, C_REV:C_REV + NE], NE), ALU.mult))
            then(dve.tensor_reduce(cmax[:, :], cand[:, :, :], AX.X, ALU.max))
            dve.tensor_tensor(oh[:, :, :], cand[:, :, :], bc(cmax[:, :], NE), ALU.is_equal).then_inc(r_oh, 1)
            then(dve.tensor_tensor(oh_f[:, :, :], cand[:, :, :], bc(cmax[:, :], NE), ALU.is_equal))
            dve.wait_ge(r_exp, 1)
            then(dve.tensor_reduce(lsum[:, :], lexp[:, :, :], AX.X, ALU.add))
            then(dve.reciprocal(gate[:, :], lsum[:, :]))
            then(dve.tensor_copy(gate_h[:, 0, :], gate[:, :]))
            then(dve.tensor_tensor(gate_h[:, 1, :], gate[:, :], gate_h[:, 0, :], ALU.subtract))
            then(dve.tensor_copy(tile_h[:, :], cf[:, C_TILE:C_TILE + T]))
            dve.wait_ge(r_pe, 1)
            pre = bank[0][:, 0:T * NE].rearrange("p (t e) -> p t e", e=NE)
            tot = bank[1][:, 0:T * NE].rearrange("p (t e) -> p t e", e=NE)
            then(dve.tensor_copy(cum[:, 0, 16:16 + T, :], tot))
            for n in range(5):
                d = 1 << n
                a, b = cum[:, n % 2, :, :], cum[:, 1 - n % 2, :, :]
                then(dve.tensor_tensor(b[:, 16:16 + T, :], a[:, 16:16 + T, :], a[:, 16 - d:16 - d + T, :], ALU.add))
            run = cum[:, 1, 16:16 + T, :]
            then(dve.tensor_scalar(n_f[:, :], run[:, T - 1, :], float(P - 1), None, ALU.add))
            then(dve.tensor_copy(n_i[:, 0, :], n_f[:, :]))
            then(dve.tensor_scalar(n_i[:, 1, :], n_i[:, 0, :], 7, None, ALU.arith_shift_right))
            then(dve.tensor_copy(base[:, 0, 5:4 + NE], n_i[:, 1, 0:NE - 1]))
            for n in range(3):
                d = 1 << n
                a, b = base[:, n % 2, :], base[:, 1 - n % 2, :]
                then(dve.tensor_tensor(b[:, 4:4 + NE], a[:, 4:4 + NE], a[:, 4 - d:4 - d + NE], ALU.add))
            first = base[:, 1, 4:4 + NE]
            then(dve.tensor_tensor(rank[:, 0, :, :], run, tot, ALU.subtract))
            then(dve.tensor_tensor(rank[:, 1, :, :], rank[:, 0, :, :], pre, ALU.add))
            then(dve.scalar_tensor_tensor(out=rank[:, 0, :, :], in0=over_t(first, NE), scalar=float(P),
                                          in1=rank[:, 1, :, :], op0=ALU.mult, op1=ALU.add))
            then(dve.tensor_tensor(rank[:, 2, :, :], rank[:, 0, :, :], oh_f[:, :, :], ALU.mult))
            then(dve.tensor_reduce(dest[:, :], rank[:, 2, :, :], AX.X, ALU.add))
            then(dve.tensor_copy(dest_i[:, 0, :], dest[:, :]))
            then(dve.tensor_scalar(dest_i[:, 1, :], dest_i[:, 0, :], P - 1, None, ALU.bitwise_and))
            then(dve.tensor_scalar(dest_i[:, 2, :], dest_i[:, 0, :], 7, None, ALU.arith_shift_right))
            then(dve.tensor_copy(dest_f[:, 0, :], dest_i[:, 1, :]))
            then(dve.tensor_copy(dest_f[:, 1, :], dest_i[:, 2, :]))
            dve.tensor_tensor(place[:, :, :], over_t(iota, P), bc(dest_f[:, 0, :], P), ALU.is_equal).then_inc(r_pay, 1)
            dve.tensor_tensor(pay[:, :, 0, :], over_t(iota[:, 0:NS], NS), bc(dest_f[:, 1, :], NS), ALU.is_equal
                              ).then_inc(r_pay, 1)
            dve.wait_ge(r_pay, 2)
            for c, v in ((1, tile_h[:, :]), (2, gate_h[:, 0, :]), (3, gate_h[:, 1, :])):
                dve.tensor_tensor(pay[:, :, c, :], pay[:, :, 0, :], bc(v, NS), ALU.mult).then_inc(r_pay, 1)
            dve.wait_ge(r_pay, 5)
            dve.tensor_scalar(pay[:, :, 0, :], pay[:, :, 0, :], cf[:, C_PART:C_PART + 1], None, ALU.mult
                              ).then_inc(r_pay, 1)
            then(dve.tensor_tensor(te_c[:, :, :],
                                   cf[0:1, C_IOTA:C_IOTA + NS].rearrange("p (n o) -> p n o", o=1).broadcast_to([1, NS, NE - 1]),
                                   base[0:1, 1, 5:4 + NE].rearrange("p (o n) -> p o n", o=1).broadcast_to([1, NS, NE - 1]),
                                   ALU.is_ge))
            then(dve.tensor_reduce(te_f[:, :], te_c[:, :, :], AX.X, ALU.add))
            then(dve.tensor_copy(te_i[:, :], te_f[:, :]))
            dve.wait_ge(r_pe, 2)
            got_ps = bank[2][:, 0:4 * NS].rearrange("p (c n) -> p c n", c=4)
            then(dve.tensor_copy(idx[:, 0, :], got_ps[:, 0, :]))
            then(dve.tensor_scalar(idx[:, 1, :], idx[:, 0, :], 0.0, OUT_OF_RANGE, ALU.is_equal, ALU.mult))
            then(dve.scalar_tensor_tensor(out=idx[:, 2, :], in0=got_ps[:, 1, :], scalar=float(P), in1=idx[:, 1, :],
                                          op0=ALU.mult, op1=ALU.add))
            then(dve.scalar_tensor_tensor(out=idx[:, 3, :], in0=idx[:, 0, :], scalar=-1.0, in1=idx[:, 2, :],
                                          op0=ALU.add, op1=ALU.add))
            then(dve.tensor_copy(slot_gate[:, 0, :], got_ps[:, 2, :]))
            then(dve.tensor_tensor(slot_gate[:, 1, :], got_ps[:, 3, :], slot_gate[:, 0, :], ALU.add))
            then(dve.tensor_scalar(slot_gate[:, 0, :], slot_gate[:, 1, :], tg[:, 1:2], None, ALU.mult))
            dve.memset(got[:, :, :], 0.0).then_inc(f_zero, 1)
            dve.engine_nop().then_inc(r_tiles, 1)

            def ffn(i, it, u):
                on_, t, s, par, rnd = fstage(i, it, 0, u)
                if on_:
                    if s != s or not isinstance(it, int) or it >= RING:
                        dve.wait_ge(f_got[s], rnd * 16)
                    alone(dve, dve_passed)
                    dve.tensor_copy(idx_s[:, s:s + 1], idx[:, 3, bass.ds(t, 1)]).then_inc(f_idx, 1)
                on_, t, s, par, rnd = fstage(i, it, 3, u)
                if on_:
                    dve.wait_ge(f_got[s], rnd * 16 + 16)
                    wait(dve, f_st[s], rnd * 16)
                    alone(dve, dve_passed)
                    dve.tensor_copy(idx_o[:, s:s + 1], idx[:, 3, bass.ds(t, 1)]).then_inc(f_io, 1)
                    dve.tensor_copy(fin[:, s, :], got[:, s, 0:D]).then_inc(f_x2, 1)
                on_, t, s, par, rnd = fstage(i, it, 4, u)
                if on_:
                    dve.wait_ge(f_y, t + 1)
                    dve.wait_ge(f_x2, t + 1)
                    dve.scalar_tensor_tensor(out=fin[:, s, :], in0=bank[4 + par][:, 0:D],
                                             scalar=slot_gate[:, 0, bass.ds(t, 1)], in1=fin[:, s, :],
                                             op0=ALU.mult, op1=ALU.add).then_inc(f_fin, 1)

            ffn_pipeline(dve, ffn)


_INS = ['x', 'ctx_1024', 'mask_Bx1xS2_if1', 'g_xattn', 'g_ffn', 'L0_xattn_Wq', 'L0_xattn_bq', 'L0_xattn_Wk',
        'L0_xattn_bk', 'L0_xattn_Wv', 'L0_xattn_bv', 'L0_xattn_Wo', 'L0_xattn_bo', 'L0_ffn_W1', 'L0_ffn_b1',
        'L0_ffn_W2', 'L0_ffn_b2', 'L0_ffn_Wr', 'L0_ffn_br']


def kernel(**inputs):
    from concourse import bacc
    from concourse.bass_utils import run_bass_kernel_spmd

    nc = bacc.Bacc("TRN2", target_bir_lowering=False, num_devices=1)
    arrays, args = {}, []
    tables = dict(zip(("const_f", "const_h"), constants()))
    for name in _INS + list(tables):
        a = np.ascontiguousarray(tables[name] if name in tables else inputs[name])
        arrays[f"in_{name}"] = a
        args.append(nc.dram_tensor(f"in_{name}", a.shape, mybir.dt.from_np(a.dtype), kind="ExternalInput").ap())
    rows = nc.dram_tensor("rows", (B * S, ROW), F32, kind="Internal").ap()
    out = nc.dram_tensor("out_0", (B, S, D), F32, kind="ExternalOutput").ap()
    build(nc, *args, rows, out)
    r = run_bass_kernel_spmd(nc, [arrays], core_ids=[0])
    return r.results[0]["out_0"]
```

```python
import math
from contextlib import ExitStack

import numpy as np

import concourse.bass as bass
from concourse import mybir

F32 = mybir.dt.float32
F16 = mybir.dt.float16
I32 = mybir.dt.int32
ALU = mybir.AluOpType
ACT = mybir.ActivationFunctionType
AX = mybir.AxisListType

P = 128
B, S, D = 64, 64, 128
H, HD = 16, 8
T = B * S // P
NE, FF = 8, 512
FC = FF // P
NS = T + NE - 1
NA = 4
STK = 32
ROW_MAX, ROW_MASK = 24, 25
MASKED = -60000.0
SCALE = 1.0 / math.sqrt(HD)
EPS = 1e-5
OUT_OF_RANGE = 8192.0
ROW = 2 * D
RING = 4
PAY = 8
UNROLL = 8
X_CH = 4
GRP = 4
W_SCALE = 64.0

C_ID, C_COS, C_SIN = 0, 128, 384
C_IOTA, C_REV, C_PART, C_ONE, C_POW, C_EPS, NCF = 640, 768, 776, 777, 793, 794, 795
K_ID, K_TRI, K_ONE, K_EXP, K_PRE = 0, 128, 256, 384, 384 + NE * P
TPC = P // NE
NCH = K_PRE + T // TPC * (T + 1) * NE


def constants():
    f = np.zeros((P, NCF), np.float32)
    h = np.zeros((P, NCH), np.float16)
    r = np.arange(P)
    f[:, C_ID:C_ID + P] = np.eye(P)
    half = HD // 2
    div = np.exp(np.arange(half, dtype=np.float32) * np.float32(-(math.log(10000.0) / half)))
    ang = (np.arange(S, dtype=np.float32)[:, None] * div[None, :]).astype(np.float32)
    cos, sin = np.cos(ang.astype(np.float64)), np.sin(ang.astype(np.float64))
    c = np.repeat(cos, 2, axis=1)
    s = np.stack([-sin, sin], axis=-1).reshape(S, HD)
    f[:, C_COS:C_COS + 2 * D] = np.tile(c, (P // S, 2 * H))
    f[:, C_SIN:C_SIN + 2 * D] = np.tile(s, (P // S, 2 * H))
    f[:, C_IOTA:C_IOTA + P] = r[None, :]
    f[:, C_REV:C_REV + NE] = NE - np.arange(NE)[None, :]
    f[:, C_PART] = r + 1
    f[:, C_ONE:C_ONE + H] = 1
    f[:, C_POW] = -0.5
    f[:, C_EPS] = EPS
    h[:, K_ID:K_ID + P] = np.eye(P)
    h[:, K_TRI:K_TRI + P] = r[:, None] < r[None, :]
    h[:, K_ONE:K_ONE + P] = 1
    pre = h[:, K_PRE:].reshape(P, T // TPC, T + 1, NE)
    for c in range(T // TPC):
        for r_ in range(P):
            pre[r_, c, c * TPC + r_ // NE + 1:, r_ % NE] = 1
    e = h[:, K_EXP:K_EXP + NE * P].reshape(P, NE, P)
    for i in range(NE):
        e[i, i, :] = 1
        e[32 + i, i, :] = 1
    return f, h


def wait(eng, sem, n):
    if isinstance(n, int) and n <= 0:
        return
    eng.wait_ge(sem, n)


def alone(eng, passed):
    eng.sem_inc(passed, 1)


def build(nc, x, ctx_in, mask, g_x, g_f, Wq, bq, Wk, bk, Wv, bv, Wo, bo, W1, b1, W2, b2, Wr, br,
          const_f, const_h, rows, out):
    stack = ExitStack()
    with stack:
        def sb(name, shape, dt=F32):
            return stack.enter_context(nc.sbuf_tensor(name, shape, dt))

        def sem(name):
            return stack.enter_context(nc.semaphore(name))

        cf = sb("cf", [P, NCF])
        ch = sb("ch", [P, NCH], F16)
        ident = cf[:, C_ID:C_ID + P]
        cos_t = cf[:, C_COS:C_COS + 2 * D]
        sin_t = cf[:, C_SIN:C_SIN + 2 * D]
        iota = cf[:, C_IOTA:C_IOTA + P]
        power = cf[:, C_POW:C_POW + 1]
        eps = cf[:, C_EPS:C_EPS + 1]
        ident_h = ch[:, K_ID:K_ID + P]
        tri_h = ch[:, K_TRI:K_TRI + P]
        ones_h = ch[:, K_ONE:K_ONE + P]
        exp_h = ch[:, K_EXP:K_EXP + NE * P].rearrange("p (e n) -> p e n", e=NE)
        pre_h = ch[:, K_PRE:].rearrange("p (c n) -> p c n", c=T // TPC)
        w_nat = sb("w_nat", [P, 4, D])
        w_h = sb("w_h", [P, 3, D], F16)
        w_l = sb("w_l", [P, 3, D], F16)
        woT = sb("woT", [P, D])
        bias_f = sb("bias_f", [P, 3 * D])
        bias_h = sb("bias_h", [P, 4 * D], F16)
        bv_bc = sb("bv_bc", [P, D])
        bo_col = sb("bo_col", [P, 1])
        c_tmp = sb("c_tmp", [P, D])
        c_col = sb("c_col", [P, 2])
        c_bc = sb("c_bc", [P, D])
        gates = sb("gates", [P, 2])
        warm = sb("warm", [P, 2])
        tg = sb("tg", [P, 2])
        mask_i = sb("mask_i", [T, P], I32)
        mask_n = sb("mask_n", [T, P])
        mask_f = sb("mask_f", [P, T])
        mask_s = sb("mask_s", [P, T])
        mask_b = sb("mask_b", [P, T])
        wr_f = sb("wr_f", [P, NE])
        wr_h = sb("wr_h", [P, 2, NE], F16)
        br_bc = sb("br_bc", [P, NE])
        w1_f = sb("w1_f", [P, 2, FF])
        w1_h = sb("w1_h", [P, NE, FF], F16)
        w1_l = sb("w1_l", [P, NE, FF], F16)
        w2_f = sb("w2_f", [P, NE, FC, D])
        b1_f = sb("b1_f", [P, FF])
        b1_h = sb("b1_h", [P, FF], F16)
        b2_f = sb("b2_f", [P, D])
        b2_h = sb("b2_h", [P, D], F16)

        x_all = sb("x_all", [P, T, D])
        ctx_all = sb("ctx_all", [P, T, D])
        ctx_h = sb("ctx_h", [P, T, D], F16)
        ctx_l = sb("ctx_l", [P, T, D], F16)
        st6 = sb("st6", [P, T, 6])
        mv = sb("mv", [P, T, 2])
        rstd = sb("rstd", [P, T, 1])
        rvar = sb("rvar", [P, T, 1])
        z = sb("z", [P, 2, D])
        zT = sb("zT", [P, 2, 2, D], F16)
        cT = sb("cT", [P, 2, 2, D], F16)
        qk = sb("qk", [P, 2, 2 * D])
        rot = sb("rot", [P, 2, 2 * D])
        rot_s = sb("rot_s", [P, 2, 2 * D])
        stq = sb("stq", [P, RING, H, STK], F16)
        stk = sb("stk", [P, 2, H, STK], F16)
        kT = sb("kT", [P, 2, NA, P], F16)
        qT = sb("qT", [P, 2, NA, P], F16)
        q2T = sb("q2T", [P, 2, NA, P], F16)
        kbd = sb("kbd", [P, RING, 2, 2 * NA, 2, S], F16)
        vx = sb("vx", [P, RING, 2, 8, 32])
        mx = sb("mx", [P, 2, H])
        pr = sb("pr", [P, 2, 2, 8, S])
        oT = sb("oT", [P, 2, 2, P])
        rden = sb("rden", [P, 2, H])
        on = sb("on", [P, 2, D])
        onT = sb("onT", [P, 2, P])
        row = sb("row", [P, RING, ROW])
        row_h = row[:, :, :].bitcast(F16)
        st6b = sb("st6b", [P, 2, 6])
        mvb = sb("mvb", [P, 2, 2])
        rstdb = sb("rstdb", [P, 2, 1])
        rvarb = sb("rvarb", [P, 2, 1])
        z2 = sb("z2", [P, 2, D])
        z2T = sb("z2T", [P, 2, 2, P], F16)
        logit = sb("logit", [P, T, NE])

        lmax = sb("lmax", [P, T])
        ldif = sb("ldif", [P, T, NE])
        lexp = sb("lexp", [P, T, NE])
        lsum = sb("lsum", [P, T])
        gate = sb("gate", [P, T])
        gate_h = sb("gate_h", [P, 2, T], F16)
        eq = sb("eq", [P, T, NE])
        cand = sb("cand", [P, T, NE])
        cmax = sb("cmax", [P, T])
        oh = sb("oh", [P, T, NE], F16)
        cnt = sb("cnt", [P, 2, P], F16)
        n_f = sb("n_f", [P, NE])
        n_i = sb("n_i", [P, 2, NE], I32)
        base = sb("base", [P, 2, 4 + NE])
        rank = sb("rank", [P, 3, T, NE])
        dest = sb("dest", [P, T])
        dest_i = sb("dest_i", [P, 3, T], I32)
        dest_f = sb("dest_f", [P, 2, T])
        place = ctx_h
        slot_oh = ctx_l[:, :, :].rearrange("p t d -> p (t d)")[:, 0:T * NS].rearrange("p (t n) -> p t n", t=T)
        pay = ctx_all[:, :, :].rearrange("p t d -> p (t d)")[:, 0:T * 2 * NS].bitcast(F16).rearrange(
            "p (t c n) -> p t c n", t=T, c=4)
        idx = sb("idx", [P, 4, NS])
        slot_gate = sb("slot_gate", [P, 2, NS])
        te_c = sb("te_c", [1, NS, NE - 1])
        te_f = sb("te_f", [1, NS])
        te_i = sb("te_i", [1, NS], I32)

        idx_s = sb("idx_s", [P, RING], I32)
        idx_o = sb("idx_o", [P, RING], I32)
        got = sb("got", [P, RING, ROW])
        got_h = got[:, :, :].bitcast(F16)
        gT = sb("gT", [P, 2, 2, P], F16)
        hT = sb("hT", [P, 2, FC, P])
        fin = sb("fin", [P, RING, D])

        ps = [stack.enter_context(nc.psum_tensor(f"ps{i}", [P, 1024], F32)) for i in range(4)]
        bank = [ps[i // 2][:, 512 * (i % 2):512 * (i % 2) + 512] for i in range(8)]

        pick = exp_h[:, 0, :]

        def f_ps_T(par):
            return bank[par][:, 0:P].bitcast(F16)

        ps_st = ps[0]
        ps_s = ps[1]
        ps_z = bank[4][:, 0:D]
        ps_c = bank[4][:, D:2 * D].bitcast(F16)
        ps_stk = bank[5].bitcast(F16)
        ps_onT = bank[5][:, 0:P]
        ps_op = bank[5][:, 256:256 + D]
        ps_proj = bank[6][:, 0:3 * D]
        ps_lg = bank[6][:, 384:384 + NE]
        ps_z2 = bank[6][:, 256:256 + P].bitcast(F16)
        ps_q2 = bank[7][:, 0:2 * P].bitcast(F16)
        ps_o = bank[7][:, 0:2 * P]
        ps_oT = bank[7][:, 256:256 + 2 * P]

        s_const, s_wts, s_w1hi, s_w1lo, s_w2ld, s_bld, s_qkb = (sem(n) for n in (
            "const16_loaded", "weights_loaded", "w1_hi_made", "w1_lo_made", "w2_loaded", "expert_biases_loaded",
            "biases_loaded"))
        s_x = [sem(f"x_loaded{c}") for c in range(X_CH)]
        s_c = [sem(f"context_loaded{c}") for c in range(X_CH)]
        s_ch, s_cl = sem("context_hi_made"), sem("context_lo_made")
        s_vo = sem("value_and_output_biases_loaded")
        s_cf = sem("const32_loaded")
        s_late, s_bc = sem("late_weights_loaded"), sem("output_bias_split")
        s_wh, s_wl, s_bq = sem("weights_hi_made"), sem("weights_lo_made"), sem("biases_split")
        s_w1ld = [sem(f"w1_loaded{i}") for i in range(2)]
        s_z0, s_wrs, s_bh, s_mb = sem("zeroed"), sem("router_split"), sem("expert_biases_split"), sem("mask_bias_made")
        s_init, s_mn, s_prep, s_setT, s_setE, s_tg = (sem(n) for n in (
            "buffers_zeroed", "mask_ready", "setup_steps", "setup_transposed", "setup_copied", "gates_ready"))
        kbd_ld = [sem(f"kbd_loaded{i}") for i in range(RING)]
        row_st = [sem(f"row_stored{i}") for i in range(RING)]
        (bn_s, bn_a, rs1, z_rdy, zcT_done, zch_ev, c_ev, zcl_ev, proj_done, qk_ev, v_ev, rope1, rope2, rope_done,
         hi_done, lo_done, stk_done, k_ev, q_ev, s_done, mx_done, nm_done, q2_done, q2_ev, st_done, p_rdy,
         pv_done, o_ev, oT_done, rden_done, on_done, onT_done, onT_ev, op_done, x2_done, bn2_s, bn2_a, rs2, z2_done,
         zh_done, zl_done, z2T_done, z2T_ev, lg_done, lg_ev) = (sem(n) for n in (
             "stats", "mean_var", "rstd_made", "z_made", "zc_transposed", "z_hi_made", "context_copied", "z_lo_made", "projected",
             "qk_copied", "v_copied", "rope_cos", "rope_sin", "rope_made", "hi_made", "lo_made",
             "stacks_transposed", "k_copied", "q_copied", "scores_made", "max_made", "negmax_made",
             "q2_transposed", "q2_copied", "scoresT_made", "probs_made", "pv_made", "o_copied",
             "o_transposed", "rden_made", "o_normalised", "on_transposed", "on_copied", "attn_projected", "x2_made",
             "stats2", "mean_var2", "rstd2_made", "z2_made", "z2_hi_made", "z2_lo_made", "z2_transposed", "z2_copied",
             "logits_made", "logits_copied"))
        sp_passed, pool_passed, dve_passed = sem("sp_passed"), sem("pool_passed"), sem("dve_passed")
        rv1, rv2, mrow = sem("var_eps"), sem("var_eps2"), sem("max_row_cleared")
        kb_done, f_io = sem("mask_rows_made"), sem("ffn_index_out")
        r_dif, r_oh, r_cnt, r_gate, r_slot, r_place, r_pay, r_paid = (sem(n) for n in (
            "route_differences", "route_onehot", "route_counts", "route_gate_split", "route_slot_onehot",
            "route_place_onehot", "route_token_payload", "route_gate_payload"))
        f_got0 = sem("gather_buffers_zeroed")
        r_warm = sem("gelu_table_loaded")
        r_step, r_exp, r_pe, r_tiles = (sem(n) for n in ("route_step", "route_exp", "route_products", "route_tiles"))
        (f_idx, f_T, f_Tev, f_h, f_gelu, f_y, f_x2, f_fin, f_zero) = (sem(n) for n in (
            "ffn_index", "ffn_transposed", "ffn_copied", "ffn_hidden", "ffn_gelu", "ffn_y", "ffn_x2", "ffn_final",
            "ffn_zeroed"))
        f_got = [sem(f"ffn_gathered{i}") for i in range(RING)]
        f_st = [sem(f"ffn_scattered{i}") for i in range(RING)]

        c_d = ctx_in.rearrange("b s d -> (b s) d").rearrange("(t p) d -> p t d", p=P)
        x_d = x.rearrange("b s d -> (b s) d").rearrange("(t p) d -> p t d", p=P)
        rows_d = rows.rearrange("(t p) n -> t p n", p=P)
        out_d = out.rearrange("b s d -> (b s) d")
        vec = lambda a: a.rearrange("(o n) -> o n", o=1)

        def swapped(a):
            return a.rearrange("p (c two) -> p c two", two=2)[:, :, ::-1]

        def paired(a):
            return a.rearrange("p (c two) -> p c two", two=2)

        def tile_of(a, t):
            return a[:, bass.ds(t, 1), :].rearrange("p o n -> p (o n)")

        LAST_LAG = 7
        PRO = 8

        def pipeline(eng, step):
            for i in range(PRO):
                step(i, i, 0)
            with eng.Fori(0, (T - PRO) // UNROLL) as u:
                for k in range(UNROLL):
                    step(PRO + k, u * UNROLL + (PRO + k), u * (UNROLL // RING))
            for i in range(T, T + LAST_LAG):
                step(i, i, 0)

        def stage(i, it, lag, u):
            looped = not isinstance(it, int)
            t0 = i - lag
            on_ = looped or 0 <= t0 < T
            rnd = u + t0 // RING if looped else t0 // RING
            return on_, it - lag, t0 % RING, t0 % 2, rnd

        def expert_at(i, u, it, early, k0):
            if isinstance(it, int):
                return (early.index(i), early.index(i)) if i in early else (None, 0)
            k = i - PRO
            if k % 4 != k0:
                return None, 0
            return u + 2 + k // 4, k // 4

        def upto(n, per=1):
            return min(n, T) * per if isinstance(n, int) else n * per

        F_PRO, F_LAST, F_UNROLL = 7, 5, 2 * RING

        def ffn_pipeline(eng, step):
            for i in range(F_PRO):
                step(i, i, 0)
            with eng.Fori(0, (NS - F_PRO) // F_UNROLL) as v:
                for k in range(F_UNROLL):
                    step(F_PRO + k, v * F_UNROLL + (F_PRO + k), v * (F_UNROLL // RING))
            for i in range(NS, NS + F_LAST):
                step(i, i, 0)

        def fstage(i, it, lag, u):
            looped = not isinstance(it, int)
            t0 = i - lag
            on_ = looped or 0 <= t0 < NS
            rnd = u + t0 // RING if looped else t0 // RING
            return on_, it - lag, t0 % RING, t0 % 2, rnd

        N_WTS = 16 * 5
        block = stack.enter_context(nc.Block())

        @block.sync
        def _(sp):
            nx = T // X_CH
            sp.dma_start(cf[:, :], const_f).then_inc(s_cf, 16)
            sp.dma_start(x_all[:, 0:nx, :], x_d[:, 0:nx, :]).then_inc(s_x[0], 16)
            for n, w in enumerate((Wq, Wk, Wv, Wo)):
                sp.dma_start(w_nat[:, n, :], w).then_inc(s_wts, 16)
            sp.dma_start(mask_i[:, :], mask.rearrange("(t b) o s -> t (b o s)", b=2)).then_inc(s_wts, 16)
            early = K_EXP + P
            sp.dma_start(ch[:, 0:early], const_h[:, 0:early]).then_inc(s_const, 16)
            sp.dma_start(ctx_all[:, 0:nx, :], c_d[:, 0:nx, :]).then_inc(s_c[0], 16)
            sp.dma_start(bv_bc[:, :], vec(bv).partition_broadcast(P)).then_inc(s_vo, 16)
            sp.dma_start(bo_col[:, :], bo.rearrange("(p o) -> p o", o=1)).then_inc(s_vo, 16)
            sp.wait_ge(s_z0, 3)
            for r in (0, 32):
                sp.dma_start(bias_f[r:r + 1, 0:D], vec(bq)).then_inc(s_qkb, 16)
                sp.dma_start(bias_f[r:r + 1, D:2 * D], vec(bk)).then_inc(s_qkb, 16)
            for c in range(1, X_CH):
                ts = slice(c * nx, c * nx + nx)
                sp.dma_start(x_all[:, ts, :], x_d[:, ts, :]).then_inc(s_x[c], 16)
                sp.dma_start(ctx_all[:, ts, :], c_d[:, ts, :]).then_inc(s_c[c], 16)
            sp.dma_start(gates[:, 0:1], vec(g_x).partition_broadcast(P)).then_inc(s_late, 16)
            sp.dma_start(gates[:, 1:2], vec(g_f).partition_broadcast(P)).then_inc(s_late, 16)
            sp.dma_start(wr_f[:, :], Wr).then_inc(s_late, 16)
            sp.dma_start(br_bc[:, :], vec(br).partition_broadcast(P)).then_inc(s_late, 16)
            sp.dma_start(ch[:, early:], const_h[:, early:]).then_inc(s_late, 16)
            for r in (0, 32):
                sp.dma_start(b1_f[r:r + NE, :], b1).then_inc(s_bld, 16)
                sp.dma_start(b2_f[r:r + NE, :], b2).then_inc(s_bld, 16)
            for s in range(RING):
                sp.sem_inc(row_st[s], 16)

            def step(i, it, u):
                on_, t, s, par, rnd = stage(i, it, 1, u)
                if on_:
                    sp.wait_ge(k_ev, t + 1)
                    alone(sp, sp_passed)
                    wait(sp, st_done, t - RING + 1)
                    alone(sp, sp_passed)
                    for g in range(4):
                        r = slice(STK * g, STK * g + STK)
                        sp.dma_start(kbd[r, s, g // 2, :, g % 2, :],
                                     kT[r, par, :, :].rearrange("p a (b k) -> p (a b) k", b=2)).then_inc(kbd_ld[s], 16)
                e, slot = expert_at(i, u, it, (1, 2), 0)
                if e is not None:
                    wait(sp, s_w1lo, e - 1)
                    alone(sp, sp_passed)
                    sp.dma_start(w1_f[:, slot, :], W1[bass.ds(e, 1), :, :].rearrange("o p n -> (o p) n")
                                 ).then_inc(s_w1ld[slot], 16)
                    sp.dma_start(w2_f[:, bass.ds(e, 1), :, :].rearrange("p o c d -> p (o c) d"),
                                 W2[bass.ds(e, 1), :, :].rearrange("o (c p) d -> p (o c) d", p=P)).then_inc(s_w2ld, 16)
                on_, t, s, par, rnd = stage(i, it, 6, u)
                if on_:
                    sp.wait_ge(zl_done, t + 1)
                    alone(sp, sp_passed)
                    sp.dma_start(rows_d[bass.ds(t, 1), :, :].rearrange("o p n -> (o p) n"), row[:, s, :]
                                 ).then_inc(row_st[s], 16)

            pipeline(sp, step)
            for s in range(RING):
                sp.wait_ge(row_st[s], 16 + 16 * T // RING)

        @block.gpsimd
        def _(pool):
            pool.memset(kbd[:, 0:2, :, :, :, :], 0.0).then_inc(s_init, 1)
            pool.wait_ge(s_cf, 16)


            def rstd_of(c):
                ts = slice(c * GRP, (c + 1) * GRP)
                pool.wait_ge(bn_a, (c + 1) * GRP)
                pool.tensor_tensor(rvar[:, ts, :], mv[:, ts, 1:2], eps.rearrange("p (o n) -> p o n", o=1).broadcast_to(
                    [P, GRP, 1]), ALU.add).then_inc(rv1, 1)
                pool.wait_ge(rv1, c + 1)
                pool.tensor_tensor(rstd[:, ts, :], rvar[:, ts, :], power.rearrange("p (o n) -> p o n", o=1).broadcast_to(
                    [P, GRP, 1]), ALU.pow).then_inc(rs1, 1)

            def context_lo(c):
                ts = slice(c * GRP, (c + 1) * GRP)
                pool.wait_ge(s_ch, c + 1)
                pool.tensor_tensor(ctx_l[:, ts, :], ctx_all[:, ts, :], ctx_h[:, ts, :], ALU.subtract).then_inc(s_cl, 1)

            rstd_of(0)
            context_lo(0)
            pool.memset(kbd[:, 2:RING, :, :, :, :], 0.0).then_inc(s_init, 1)

            def step(i, it, u):
                on_, t, s, par, rnd = stage(i, it, 6, u)
                if on_:
                    pool.wait_ge(bn2_a, t + 1)
                    pool.tensor_tensor(rvarb[:, par, :], mvb[:, par, 1:2], eps, ALU.add).then_inc(rv2, 1)
                    pool.wait_ge(rv2, t + 1)
                    pool.tensor_tensor(rstdb[:, par, :], rvarb[:, par, :], power, ALU.pow).then_inc(rs2, 1)
                on_, t, s, par, rnd = stage(i, it, 1, u)
                if on_:
                    pool.wait_ge(hi_done, 2 * t + 2)
                    q_f = rot[:, par, 0:D].rearrange("p (h d) -> p h d", d=HD)
                    k_f = rot[:, par, D:2 * D].rearrange("p (h d) -> p h d", d=HD)
                    pool.tensor_tensor(stq[:, s, :, 16:24], q_f, stq[:, s, :, 0:8], ALU.subtract
                                       ).then_inc(lo_done, 1)
                    pool.tensor_tensor(stk[:, par, :, 8:16], k_f, stk[:, par, :, 0:8], ALU.subtract
                                       ).then_inc(lo_done, 1)
                if isinstance(it, int) and 1 <= it < T // GRP:
                    rstd_of(it)
                    context_lo(it)
                on_, t, s, par, rnd = stage(i, it, 0, u)
                if on_:
                    wait(pool, q2_done, t - RING + 1)
                    alone(pool, pool_passed)
                    pool.memset(stq[:, s, :, ROW_MAX:ROW_MAX + 1], 0.0).then_inc(mrow, 1)
                    pool.wait_ge(qk_ev, 2 * t + 2)
                    wait(pool, hi_done, 2 * t - 2)
                    wait(pool, lo_done, 2 * t - 2)
                    pool.tensor_tensor(rot[:, par, :], qk[:, par, :], cos_t, ALU.mult).then_inc(rope1, 1)
                    pool.tensor_tensor(paired(rot_s[:, par, :]), swapped(qk[:, par, :]), paired(sin_t),
                                       ALU.mult).then_inc(rope2, 1)
                    pool.wait_ge(rope2, t + 1)
                    pool.tensor_tensor(rot[:, par, :], rot[:, par, :], rot_s[:, par, :], ALU.add).then_inc(rope_done, 1)

            pipeline(pool, step)

            pool.memset(got[:, :, :], 0.0).then_inc(f_got0, 1)
            pool.wait_ge(r_gate, 2)
            for n in range(T // PAY):
                ts = slice(n * PAY, (n + 1) * PAY)
                pool.wait_ge(r_slot, n + 1)
                for c in range(2):
                    pool.tensor_tensor(pay[:, ts, 2 + c, :], slot_oh[:, ts, :], gate_h[:, c, ts].rearrange(
                        "p (t o) -> p t o", o=1).broadcast_to([P, PAY, NS]), ALU.mult).then_inc(r_paid, 1)

            pool.wait_ge(f_got0, 1)
            for s in range(RING):
                pool.wait_ge(row_st[s], 16 + 16 * T // RING)

            def ffn(i, it, u):
                on_, t, s, par, rnd = fstage(i, it, 0, u)
                if on_:
                    pool.wait_ge(f_idx, t + 1)
                    wait(pool, f_x2, t - RING + 1)
                    wait(pool, f_T, t - RING + 1)
                    alone(pool, pool_passed)
                    pool.indirect_dma_start(
                        out=got[:, s, :], out_offset=None, in_=rows,
                        in_offset=bass.IndirectOffsetOnAxis(ap=idx_s[:, s:s + 1], axis=0),
                        bounds_check=B * S - 1, oob_is_err=False).then_inc(f_got[s], 16)
                on_, t, s, par, rnd = fstage(i, it, 5, u)
                if on_:
                    pool.wait_ge(f_fin, t + 1)
                    alone(pool, pool_passed)
                    pool.indirect_dma_start(
                        out=out_d, out_offset=bass.IndirectOffsetOnAxis(ap=idx_o[:, s:s + 1], axis=0),
                        in_=fin[:, s, :], in_offset=None,
                        bounds_check=B * S - 1, oob_is_err=False).then_inc(f_st[s], 16)

            ffn_pipeline(pool, ffn)
            for s in range(RING):
                pool.wait_ge(f_st[s], 16 * len(range(s, NS, RING)))

        @block.scalar
        def _(act):
            for n in range(3):
                act.wait_ge(s_setT, n + 1)
                act.activation(w_h[:, n, :], bank[n][:, 0:D], ACT.Copy, scale=W_SCALE).then_inc(s_wh, 1)
            act.wait_ge(s_setT, 4)
            act.activation(woT[:, :], bank[3][:, 0:D], ACT.Copy).then_inc(s_setE, 1)
            act.wait_ge(s_setT, 5)
            act.activation(mask_f[:, :], bank[5][:, 0:T], ACT.Copy).then_inc(s_setE, 1)
            def context_hi(c):
                ts = slice(c * GRP, (c + 1) * GRP)
                act.wait_ge(s_c[c // 2], 16)
                act.activation(ctx_h[:, ts, :], ctx_all[:, ts, :], ACT.Copy).then_inc(s_ch, 1)

            context_hi(0)
            act.wait_ge(s_mb, 2)

            def step(i, it, u):
                on_, t, s, par, rnd = stage(i, it, 0, u)
                if on_:
                    act.wait_ge(zcT_done, t + 1)
                    wait(act, proj_done, t - 1)
                    act.activation(zT[:, par, 0, :], ps_z, ACT.Copy).then_inc(zch_ev, 1)
                    act.activation(cT[:, par, :, :].rearrange("p a n -> p (a n)"), ps_c, ACT.Copy).then_inc(c_ev, 1)
                on_, t, s, par, rnd = stage(i, it, 3, u)
                if on_:
                    act.wait_ge(q2_done, t + 1)
                    wait(act, st_done, t - 1)
                    act.activation(q2T[:, par, :, :].rearrange("p a n -> p (a n)"), ps_q2, ACT.Copy).then_inc(q2_ev, 1)
                on_, t, s, par, rnd = stage(i, it, 3, u)
                if on_:
                    act.wait_ge(st_done, t + 1)
                    wait(act, pv_done, t - 1)
                    act.activation(pr[:, par, :, :, :].rearrange("p b j q -> p (b j q)"), ps_st[:, :], ACT.Exp,
                                   scale=SCALE).then_inc(p_rdy, 1)
                on_, t, s, par, rnd = stage(i, it, 0, u)
                if on_:
                    act.wait_ge(proj_done, t + 1)
                    wait(act, rope2, t - 1)
                    act.activation(qk[:, par, 0:D], ps_proj[:, 0:D], ACT.Copy, scale=1.0 / W_SCALE).then_inc(qk_ev, 1)
                    act.activation(qk[:, par, D:2 * D], ps_proj[:, D:2 * D], ACT.Identity,
                                   scale=mask_s[:, bass.ds(t, 1)]).then_inc(qk_ev, 1)
                    wait(act, pv_done, t - RING + 1)
                    v_ps = ps_proj[:, 2 * D:3 * D].rearrange("p (j hh d) -> p j hh d", hh=2, d=HD)
                    for b in range(2):
                        for hh in range(2):
                            act.activation(vx[64 * hh:64 * hh + 64, s, b, :, 16 * hh:16 * hh + HD],
                                           v_ps[64 * b:64 * b + 64, :, hh, :], ACT.Copy, scale=1.0 / W_SCALE
                                           ).then_inc(v_ev, 1)
                    wait(act, stk_done, t - 1)
                    act.activation(stk[:, par, :, ROW_MASK], cf[:, C_ONE:C_ONE + H], ACT.Identity,
                                   scale=mask_b[:, bass.ds(t, 1)]).then_inc(kb_done, 1)
                on_, t, s, par, rnd = stage(i, it, 1, u)
                if on_:
                    act.wait_ge(k_ev, t + 1)
                    wait(act, s_done, t - 1)
                    act.activation(qT[:, par, :, :].rearrange("p a n -> p (a n)"), ps_stk[:, 0:NA * P], ACT.Copy
                                   ).then_inc(q_ev, 1)
                on_, t, s, par, rnd = stage(i, it, 3, u)
                if on_:
                    act.wait_ge(pv_done, t + 1)
                    wait(act, oT_done, t - 1)
                    act.activation(oT[:, par, :, :].rearrange("p a n -> p (a n)"), ps_o, ACT.Copy).then_inc(o_ev, 1)
                on_, t, s, par, rnd = stage(i, it, 6, u)
                if on_:
                    act.wait_ge(z2T_done, t + 1)
                    wait(act, lg_done, t - 1)
                    act.activation(z2T[:, par, :, :].rearrange("p a n -> p (a n)"), ps_z2, ACT.Copy).then_inc(z2T_ev, 1)
                on_, t, s, par, rnd = stage(i, it, 4, u)
                if on_:
                    act.wait_ge(onT_done, t + 1)
                    wait(act, op_done, t - 1)
                    act.activation(onT[:, par, :], ps_onT, ACT.Copy).then_inc(onT_ev, 1)
                if isinstance(it, int) and it + 1 < T // GRP:
                    context_hi(it + 1)
                e, slot = expert_at(i, u, it, (4, 6), 1)
                if e is not None:
                    act.wait_ge(s_w1ld[slot], 16 if isinstance(it, int) else u * 8 + 32)
                    act.activation(tile_of(w1_h, e), w1_f[:, slot, :], ACT.Copy, scale=W_SCALE).then_inc(s_w1hi, 1)
                if isinstance(it, int) and it == X_CH:
                    act.wait_ge(s_late, 80)
                    act.activation(tg[:, :], gates[:, :], ACT.Tanh).then_inc(s_tg, 1)

            pipeline(act, step)

            act.wait_ge(r_dif, 1)
            act.activation(lexp[:, :, :], ldif[:, :, :], ACT.Exp).then_inc(r_exp, 1)
            act.wait_ge(r_pe, 1)
            act.activation(cnt[:, :, :].rearrange("p c n -> p (c n)"), bank[1][:, 0:2 * P], ACT.Copy).then_inc(r_cnt, 1)
            act.activation(warm[:, :], gates[:, :], ACT.Gelu).then_inc(r_warm, 1)
            for n in range(T // PAY):
                ts = slice(n * PAY, (n + 1) * PAY)
                act.wait_ge(r_slot, n + 1)
                act.activation(pay[:, ts, 0, :], slot_oh[:, ts, :], ACT.Identity, scale=cf[:, C_PART:C_PART + 1]
                               ).then_inc(r_pay, 1)
                for t in range(n * PAY, (n + 1) * PAY):
                    act.activation(pay[:, t, 1, :], slot_oh[:, t, :], ACT.Copy, scale=float(t)).then_inc(r_pay, 1)

            def ffn(i, it, u):
                on_, t, s, par, rnd = fstage(i, it, 2, u)
                if on_:
                    act.wait_ge(f_T, t + 1)
                    wait(act, f_h, t - 1)
                    act.activation(gT[:, par, :, :].rearrange("p a n -> p (a n)"), f_ps_T(par), ACT.Copy).then_inc(f_Tev, 1)
                on_, t, s, par, rnd = fstage(i, it, 3, u)
                if on_:
                    act.wait_ge(f_h, t + 1)
                    wait(act, f_y, t - 1)
                    act.activation(hT[:, par, :, :].rearrange("p c n -> p (c n)"), bank[2 + par], ACT.Gelu,
                                   scale=1.0 / W_SCALE).then_inc(f_gelu, 1)

            ffn_pipeline(act, ffn)

        @block.tensor
        def _(pe):
            pe.wait_ge(s_cf, 16)
            pe.wait_ge(s_wts, N_WTS)
            for n in range(4):
                pe.transpose(bank[n][:, 0:D], w_nat[:, n, :], ident).then_inc(s_setT, 1)
            pe.wait_ge(s_mn, 2)
            pe.transpose(bank[5][:, 0:T], mask_n[:, :], cf[0:T, C_ID:C_ID + T]).then_inc(s_setT, 1)
            pe.wait_ge(s_const, 16)
            pe.wait_ge(s_setE, 2)

            def step(i, it, u):
                on_, t, s, par, rnd = stage(i, it, 0, u)
                if on_:
                    if i % GRP == 0:
                        pe.wait_ge(s_cl, i // GRP + 1 if i < PRO else T // GRP)
                    pe.wait_ge(z_rdy, t + 1)
                    wait(pe, zcl_ev, t)
                    wait(pe, c_ev, t)
                    pe.transpose(ps_z, z[:, par, :], ident)
                    pe.transpose(ps_c[:, 0:D], tile_of(ctx_h, t), ident_h)
                    pe.transpose(ps_c[:, D:2 * D], tile_of(ctx_l, t), ident_h).then_inc(zcT_done, 1)
                on_, t, s, par, rnd = stage(i, it, 3, u)
                if on_:
                    pe.wait_ge(nm_done, t + 1)
                    wait(pe, o_ev, t)
                    for a in range(NA):
                        mm = pe.transpose(ps_q2[:, P * a:P * a + P],
                                          stq[:, s, 4 * a:4 * a + 4, :].rearrange("p h r -> p (h r)"), ident_h)
                    mm.then_inc(q2_done, 1)
                on_, t, s, par, rnd = stage(i, it, 7, u)
                if on_:
                    pe.wait_ge(z2T_ev, t + 1)
                    pe.wait_ge(v_ev, upto(t + 7, 4))
                    wait(pe, lg_ev, t)
                    if i == 7:
                        pe.wait_ge(s_wrs, 2)
                    pe.matmul(ps_lg, z2T[:, par, 0, :], wr_h[:, 0, :], start=True, stop=False)
                    pe.matmul(ps_lg, z2T[:, par, 1, :], wr_h[:, 0, :], start=False, stop=False)
                    pe.matmul(ps_lg, z2T[:, par, 0, :], wr_h[:, 1, :], start=False, stop=True).then_inc(lg_done, 1)
                on_, t, s, par, rnd = stage(i, it, 5, u)
                if on_:
                    pe.wait_ge(onT_ev, t + 1)
                    pe.matmul(ps_op, pick, bias_h[:, 3 * D:4 * D], start=True, stop=False)
                    pe.matmul(ps_op, onT[:, par, :], woT[:, :], start=False, stop=True).then_inc(op_done, 1)
                on_, t, s, par, rnd = stage(i, it, 3, u)
                if on_:
                    if i == 3:
                        pe.wait_ge(s_bc, 2)
                    pe.wait_ge(q2_ev, t + 1)
                    wait(pe, p_rdy, t)
                    for b in range(2):
                        for j in range(8):
                            mm = pe.matmul(ps_st[:, 512 * b + S * j:512 * b + S * j + S],
                                           kbd[:, s, j % 2, 2 * (j // 2) + b, :, :].rearrange("p h k -> p (h k)"),
                                           q2T[:, par, j // 2, S * b:S * b + S], start=True, stop=True)
                    mm.then_inc(st_done, 1)
                on_, t, s, par, rnd = stage(i, it, 4, u)
                if on_:
                    pe.wait_ge(o_ev, t + 1)
                    pe.wait_ge(q2_ev, upto(t + 2))
                    for n in range(2):
                        mm = pe.transpose(ps_oT[:, P * n:P * n + P], oT[:, par, n, :], ident)
                    mm.then_inc(oT_done, 1)
                on_, t, s, par, rnd = stage(i, it, 0, u)
                if on_:
                    if i == 0:
                        pe.wait_ge(s_wl, 3)
                        pe.wait_ge(s_bq, 2)
                    pe.wait_ge(zch_ev, t + 1)
                    wait(pe, v_ev, t * 4)
                    wait(pe, lg_ev, t - 6)
                    pe.wait_ge(c_ev, t + 1)
                    pe.wait_ge(zcl_ev, t + 1)
                    pe.matmul(ps_proj, pick, bias_h[:, 0:3 * D], start=True, stop=False)
                    for n, (half, w) in enumerate(((0, w_h), (1, w_h), (0, w_l))):
                        pe.matmul(ps_proj[:, 0:D], zT[:, par, half, :], w[:, 0, :], start=False, stop=False)
                        mm = pe.matmul(ps_proj[:, D:3 * D], cT[:, par, half, :], w[:, 1:3, :].rearrange("p a n -> p (a n)"),
                                       start=False, stop=(n == 2))
                    mm.then_inc(proj_done, 1)
                on_, t, s, par, rnd = stage(i, it, 1, u)
                if on_:
                    wait(pe, q_ev, t)
                    wait(pe, x2_done, t - 3)
                    pe.wait_ge(mrow, t + 1)
                    pe.wait_ge(kb_done, t + 1)
                    pe.wait_ge(hi_done, 2 * t + 2)
                    pe.wait_ge(lo_done, 2 * t + 2)
                    for w in range(2):
                        for a in range(NA):
                            c = (w * NA + a) * P
                            src = stk[:, par, :, :] if w else stq[:, s, :, :]
                            mm = pe.transpose(ps_stk[:, c:c + P],
                                              src[:, 4 * a:4 * a + 4, :].rearrange("p h r -> p (h r)"), ident_h)
                    mm.then_inc(stk_done, 1)
                if isinstance(it, int) and it == 1:
                    pe.wait_ge(s_prep, 4)
                    pe.matmul(bank[0][:, 0:D], c_bc[:, :], ident, start=True, stop=True).then_inc(s_setT, 1)
                on_, t, s, par, rnd = stage(i, it, 2, u)
                if on_:
                    pe.wait_ge(kbd_ld[s], rnd * 64 + 64)
                    pe.wait_ge(q_ev, t + 1)
                    wait(pe, mx_done, t)
                    for j in range(8):
                        for b in range(2):
                            mm = pe.matmul(ps_s[S * b:S * b + S, P * j:P * j + P], qT[:, par, j // 2, S * b:S * b + S],
                                           kbd[:, s, j % 2, 2 * (j // 2) + b, :, :].rearrange("p h k -> p (h k)"),
                                           start=True, stop=True)
                    mm.then_inc(s_done, 1)
                on_, t, s, par, rnd = stage(i, it, 3, u)
                if on_:
                    pe.wait_ge(p_rdy, t + 1)
                    pe.wait_ge(v_ev, t * 4 + 4)
                    wait(pe, on_done, t)
                    for b in range(2):
                        for j in range(8):
                            r = 32 * (j % 4)
                            c = (j // 4) * P + b * S
                            mm = pe.matmul(ps_o[r:r + 32, c:c + S], vx[:, s, b, j, :], pr[:, par, b, j, :],
                                           start=True, stop=True)
                    mm.then_inc(pv_done, 1)
                on_, t, s, par, rnd = stage(i, it, 6, u)
                if on_:
                    pe.wait_ge(zl_done, t + 1)
                    pe.wait_ge(v_ev, upto(t + 7, 4))
                    wait(pe, lg_ev, t)
                    wait(pe, z2T_ev, t)
                    for n in range(2):
                        mm = pe.transpose(ps_z2[:, P * n:P * n + P], row_h[:, s, (2 + n) * D:(3 + n) * D], ident_h)
                    mm.then_inc(z2T_done, 1)
                on_, t, s, par, rnd = stage(i, it, 4, u)
                if on_:
                    pe.wait_ge(on_done, t + 1)
                    pe.wait_ge(q_ev, upto(t + 4))
                    wait(pe, x2_done, t)
                    pe.transpose(ps_onT, on[:, par, :], ident).then_inc(onT_done, 1)

            pipeline(pe, step)

            pe.wait_ge(r_oh, 1)
            pe.wait_ge(f_zero, 1)
            ohf = oh[:, :, :].rearrange("p t e -> p (t e)")
            for c in range(T // TPC):
                mm = pe.matmul(bank[1][:, c * P:c * P + P], ohf[:, c * P:c * P + P], ones_h, start=True, stop=True)
            mm.then_inc(r_pe, 1)
            pe.wait_ge(r_cnt, 1)
            for c in range(T // TPC):
                pe.matmul(bank[0][:, 0:(T + 1) * NE], cnt[:, c, :], pre_h[:, c, :], start=(c == 0), stop=False)
            pe.matmul(bank[0][:, 0:T * NE], tri_h, ohf, start=False, stop=True).then_inc(r_pe, 1)
            for t in range(T):
                if t % PAY == 0:
                    n = t // PAY + 1
                    pe.wait_ge(r_place, n)
                    pe.wait_ge(r_pay, n * (PAY + 1))
                    pe.wait_ge(r_paid, 2 * n)
                mm = pe.matmul(bank[6][:, 0:4 * NS], place[:, t, :], pay[:, t, :, :].rearrange("p c n -> p (c n)"),
                               start=(t == 0), stop=(t == T - 1))
            mm.then_inc(r_pe, 1)

            pe.wait_ge(r_tiles, 1)
            pe.wait_ge(s_w1lo, NE)
            pe.wait_ge(s_w2ld, 16 * NE)
            pe.wait_ge(s_bh, 4)

            experts = {}
            in_range = "the number of an expert is a sum of seven comparisons, so 0 to 7"

            def load_experts(first_tile, n, first):
                regs = nc.values_load_multi_w_load_instructions(
                    te_i[0:1, bass.ds(first_tile, n)], engines=[mybir.EngineType.PE], min_val=0, max_val=NE - 1,
                    skip_runtime_bounds_check_because=in_range)[1]
                experts.clear()
                experts.update({first + m: r for m, r in enumerate(regs)})

            def ffn(i, it, u):
                if not isinstance(it, int) and i == F_PRO:
                    load_experts(it - 4, F_UNROLL + 1, i - 4)
                if isinstance(it, int) and it in (3, NS):
                    load_experts(i - 3 if it == 3 else NS - 4, 4, 0 if it == 3 else NS - 4)
                on_, t, s, par, rnd = fstage(i, it, 2, u)
                if on_:
                    pe.wait_ge(f_got[s], rnd * 16 + 16)
                    wait(pe, f_Tev, t - 1)
                    for n in range(2):
                        mm = pe.transpose(f_ps_T(par)[:, P * n:P * n + P], got_h[:, s, (2 + n) * D:(3 + n) * D], ident_h)
                    mm.then_inc(f_T, 1)
                on_, t, s, par, rnd = fstage(i, it, 3, u)
                if on_:
                    e = experts[i - 3]
                    pe.wait_ge(f_Tev, t + 1)
                    wait(pe, f_gelu, t - 1)
                    for c in range(FC):
                        o = bank[2 + par][:, P * c:P * c + P]
                        w_h = w1_h[:, bass.ds(e, 1), P * c:P * c + P].rearrange("p o n -> p (o n)")
                        w_l = w1_l[:, bass.ds(e, 1), P * c:P * c + P].rearrange("p o n -> p (o n)")
                        one = exp_h[:, bass.ds(e, 1), :].rearrange("p o n -> p (o n)")
                        pe.matmul(o, b1_h[:, P * c:P * c + P], one, start=True, stop=False)
                        pe.matmul(o, w_h, gT[:, par, 0, :], start=False, stop=False)
                        pe.matmul(o, w_h, gT[:, par, 1, :], start=False, stop=False)
                        mm = pe.matmul(o, w_l, gT[:, par, 0, :], start=False, stop=True)
                    mm.then_inc(f_h, 1)
                on_, t, s, par, rnd = fstage(i, it, 4, u)
                if on_:
                    e = experts[i - 4]
                    pe.wait_ge(f_gelu, t + 1)
                    wait(pe, f_fin, t - 1)
                    o = bank[4 + par][:, 0:D]
                    one = exp_h[:, bass.ds(e, 1), :].rearrange("p o n -> p (o n)")
                    pe.matmul(o, one, b2_h[:, :], start=True, stop=False)
                    for c in range(FC):
                        mm = pe.matmul(o, hT[:, par, c, :], w2_f[:, bass.ds(e, 1), c, :].rearrange("p o n -> p (o n)"),
                                       start=False, stop=(c == FC - 1))
                    mm.then_inc(f_y, 1)

            ffn_pipeline(pe, ffn)

        @block.vector
        def _(dve):
            dve.memset(b1_f[:, :], 0.0).then_inc(s_z0, 1)
            dve.memset(b2_f[:, :], 0.0).then_inc(s_z0, 1)
            dve.memset(bias_f[:, :], 0.0).then_inc(s_z0, 1)
            dve.memset(bias_h[:, :], 0.0).then_inc(s_z0, 1)
            dve.memset(stk[:, :, :, :], 0.0).then_inc(s_z0, 1)
            dve.memset(stq[:, :, :, :], 0.0).then_inc(s_z0, 1)
            dve.memset(vx[:, :, :, :, :], 0.0).then_inc(s_z0, 1)
            dve.wait_ge(s_z0, 7)
            dve.memset(stq[:, :, :, ROW_MASK:ROW_MASK + 1], 1.0).then_inc(s_z0, 1)
            dve.memset(stk[:, :, :, ROW_MAX:ROW_MAX + 1], 1.0).then_inc(s_z0, 1)
            for hh in range(2):
                dve.memset(vx[64 * hh:64 * hh + 64, :, :, :, 16 * hh + HD:16 * hh + HD + 1], 1.0).then_inc(s_z0, 1)

            def stats_of(n):
                dve.wait_ge(s_x[n // 2], 16)
                ts = range(n * GRP, (n + 1) * GRP)
                for t in ts:
                    dve.bn_stats(st6[:, t, :], x_all[:, t, :]).then_inc(bn_s, 1)
                for t in ts:
                    dve.wait_ge(bn_s, t + 1)
                    dve.bn_aggr(mv[:, t, :], st6[:, t, :]).then_inc(bn_a, 1)

            dve.memset(base[:, :, :], 0.0).then_inc(f_zero, 1)
            stats_of(0)
            dve.wait_ge(s_wts, N_WTS)
            dve.wait_ge(s_cf, 16)
            dve.tensor_copy(mask_n[:, :], mask_i[:, :]).then_inc(s_mn, 1)
            dve.wait_ge(s_mn, 1)
            dve.tensor_scalar(mask_n[:, :], mask_n[:, :], 0.0, None, ALU.not_equal).then_inc(s_mn, 1)
            for n in range(3):
                dve.wait_ge(s_wh, n + 1)
                dve.scalar_tensor_tensor(out=w_l[:, n, :], in0=bank[n][:, 0:D], scalar=W_SCALE, in1=w_h[:, n, :],
                                         op0=ALU.mult, op1=ALU.subtract).then_inc(s_wl, 1)
            dve.wait_ge(s_setE, 2)
            dve.tensor_scalar(mask_b[:, :], mask_f[:, :], 1.0, -MASKED, ALU.subtract, ALU.mult).then_inc(s_mb, 1)
            dve.tensor_scalar(mask_s[:, :], mask_f[:, :], 1.0 / W_SCALE, None, ALU.mult).then_inc(s_mb, 1)
            dve.wait_ge(s_z0, 11)

            up, low = slice(0, 64), slice(32, 64)

            def bias_halves():
                dve.wait_ge(s_qkb, 64)
                dve.tensor_scalar(bias_h[up, 0:3 * D], bias_f[up, :], W_SCALE, None, ALU.mult).then_inc(s_bq, 1)
                dve.wait_ge(s_bq, 1)
                dve.scalar_tensor_tensor(out=bias_h[low, 0:3 * D], in0=bias_f[low, :], scalar=W_SCALE,
                                         in1=bias_h[low, 0:3 * D], op0=ALU.mult, op1=ALU.subtract).then_inc(s_bq, 1)

            def output_bias():
                dve.wait_ge(s_const, 16)
                dve.wait_ge(s_vo, 32)
                dve.tensor_tensor(c_tmp[:, :], w_nat[:, 3, :], bv_bc[:, :], ALU.mult).then_inc(s_prep, 1)
                dve.wait_ge(s_prep, 1)
                dve.tensor_reduce(c_col[:, 0:1], c_tmp[:, :], AX.X, ALU.add).then_inc(s_prep, 1)
                dve.wait_ge(s_prep, 2)
                dve.tensor_scalar(c_col[:, 1:2], c_col[:, 0:1], bo_col[:, :], None, ALU.add).then_inc(s_prep, 1)
                dve.wait_ge(s_prep, 3)
                dve.tensor_scalar(c_bc[:, :], ones_h, c_col[:, 1:2], None, ALU.mult).then_inc(s_prep, 1)

            def output_bias_halves():
                dve.wait_ge(s_setT, 6)
                dve.tensor_copy(bias_h[up, 3 * D:4 * D], bank[0][up, 0:D]).then_inc(s_bc, 1)
                dve.wait_ge(s_bc, 1)
                dve.tensor_tensor(bias_h[low, 3 * D:4 * D], bank[0][low, 0:D], bias_h[low, 3 * D:4 * D], ALU.subtract
                                  ).then_inc(s_bc, 1)

            def router_halves():
                dve.wait_ge(s_late, 80)
                dve.tensor_copy(wr_h[:, 0, :], wr_f[:, :]).then_inc(s_wrs, 1)
                dve.wait_ge(s_wrs, 1)
                dve.tensor_tensor(wr_h[:, 1, :], wr_f[:, :], wr_h[:, 0, :], ALU.subtract).then_inc(s_wrs, 1)

            def expert_biases():
                dve.wait_ge(s_bld, 64)
                dve.tensor_scalar(b1_h[:, :], b1_f[:, :], W_SCALE, None, ALU.mult).then_inc(s_bh, 1)
                dve.tensor_copy(b2_h[:, :], b2_f[:, :]).then_inc(s_bh, 1)
                dve.wait_ge(s_bh, 2)
                lo = slice(32, 32 + NE)
                dve.scalar_tensor_tensor(out=b1_h[lo, :], in0=b1_f[lo, :], scalar=W_SCALE, in1=b1_h[lo, :],
                                         op0=ALU.mult, op1=ALU.subtract).then_inc(s_bh, 1)
                dve.tensor_tensor(b2_h[lo, :], b2_f[lo, :], b2_h[lo, :], ALU.subtract).then_inc(s_bh, 1)

            def step(i, it, u):
                on_, t, s, par, rnd = stage(i, it, 0, u)
                if on_:
                    if i % GRP == 0:
                        dve.wait_ge(rs1, i // GRP + 1 if i < PRO else T // GRP)
                    wait(dve, zcT_done, t - 1)
                    dve.tensor_scalar(z[:, par, :], tile_of(x_all, t), tile_of(mv[:, :, 0:1], t), tile_of(rstd, t),
                                      ALU.subtract, ALU.mult).then_inc(z_rdy, 1)
                on_, t, s, par, rnd = stage(i, it, 3, u)
                if on_:
                    dve.wait_ge(s_done, t + 1)
                    dve.tensor_reduce(mx[:, par, :], ps_s[:, :].rearrange("p (h k) -> p h k", k=S), AX.X, ALU.max
                                      ).then_inc(mx_done, 1)
                    dve.wait_ge(mx_done, t + 1)
                    dve.tensor_scalar(stq[:, s, :, ROW_MAX], mx[:, par, :], -1.0, None, ALU.mult).then_inc(nm_done, 1)
                on_, t, s, par, rnd = stage(i, it, 1, u)
                if on_:
                    dve.wait_ge(rope_done, t + 1)
                    wait(dve, stk_done, t - 1)
                    wait(dve, q2_done, t - RING + 1)
                    q_f = rot[:, par, 0:D].rearrange("p (h o d) -> p h o d", d=HD, o=1)
                    k_f = rot[:, par, D:2 * D].rearrange("p (h o d) -> p h o d", d=HD, o=1)
                    dve.tensor_copy(stq[:, s, :, 0:16].rearrange("p h (c d) -> p h c d", c=2),
                                    q_f.broadcast_to([P, H, 2, HD])).then_inc(hi_done, 1)
                    k_hi = stk[:, par, :, 0:32].rearrange("p h (c d) -> p h c d", c=2)[:, :, :, 0:HD]
                    dve.tensor_copy(k_hi, k_f.broadcast_to([P, H, 2, HD])).then_inc(hi_done, 1)
                on_, t, s, par, rnd = stage(i, it, 6, u)
                if on_:
                    dve.wait_ge(rs2, t + 1)
                    wait(dve, zl_done, t - 1)
                    dve.tensor_scalar(z2[:, par, :], row[:, s, 0:D], mvb[:, par, 0:1], rstdb[:, par, :],
                                      ALU.subtract, ALU.mult).then_inc(z2_done, 1)
                e, slot = expert_at(i, u, it, (5, 7), 2)
                if e is not None:
                    dve.wait_ge(s_w1hi, e + 1)
                    dve.scalar_tensor_tensor(out=tile_of(w1_l, e), in0=w1_f[:, slot, :], scalar=W_SCALE,
                                             in1=tile_of(w1_h, e), op0=ALU.mult, op1=ALU.subtract).then_inc(s_w1lo, 1)
                on_, t, s, par, rnd = stage(i, it, 7, u)
                if on_:
                    dve.wait_ge(lg_done, t + 1)
                    dve.tensor_tensor(tile_of(logit, t), ps_lg, br_bc[:, :], ALU.add).then_inc(lg_ev, 1)
                on_, t, s, par, rnd = stage(i, it, 0, u)
                if on_:
                    dve.wait_ge(zch_ev, t + 1)
                    dve.wait_ge(c_ev, t + 1)
                    wait(dve, proj_done, t - 1)
                    dve.tensor_tensor(zT[:, par, 1, :], ps_z, zT[:, par, 0, :], ALU.subtract).then_inc(zcl_ev, 1)
                on_, t, s, par, rnd = stage(i, it, 5, u)
                if on_:
                    if i == 5:
                        dve.wait_ge(s_tg, 1)
                    dve.wait_ge(op_done, t + 1)
                    dve.wait_ge(row_st[s], rnd * 16 + 16)
                    dve.scalar_tensor_tensor(out=row[:, s, 0:D], in0=ps_op, scalar=tg[:, 0:1], in1=tile_of(x_all, t),
                                             op0=ALU.mult, op1=ALU.add).then_inc(x2_done, 1)
                on_, t, s, par, rnd = stage(i, it, 4, u)
                if on_:
                    dve.wait_ge(oT_done, t + 1)
                    wait(dve, on_done, t - 1)
                    o_ps = ps_oT.rearrange("p (h c) -> p h c", c=16)
                    dve.reciprocal(rden[:, par, :], o_ps[:, :, HD]).then_inc(rden_done, 1)
                on_, t, s, par, rnd = stage(i, it, 6, u)
                if on_:
                    dve.wait_ge(z2_done, t + 1)
                    dve.tensor_copy(row_h[:, s, 2 * D:3 * D], z2[:, par, :]).then_inc(zh_done, 1)
                on_, t, s, par, rnd = stage(i, it, 4, u)
                if on_:
                    dve.wait_ge(rden_done, t + 1)
                    o_ps = ps_oT.rearrange("p (h c) -> p h c", c=16)
                    wait(dve, onT_done, t - 1)
                    dve.tensor_tensor(on[:, par, :].rearrange("p (h d) -> p h d", d=HD), o_ps[:, :, 0:HD],
                                      rden[:, par, :].rearrange("p (h o) -> p h o", o=1).broadcast_to([P, H, HD]),
                                      ALU.mult).then_inc(on_done, 1)
                on_, t, s, par, rnd = stage(i, it, 5, u)
                if on_:
                    dve.wait_ge(x2_done, t + 1)
                    dve.bn_stats(st6b[:, par, :], row[:, s, 0:D]).then_inc(bn2_s, 1)
                on_, t, s, par, rnd = stage(i, it, 6, u)
                if on_:
                    dve.wait_ge(zh_done, t + 1)
                    dve.tensor_tensor(row_h[:, s, 3 * D:4 * D], z2[:, par, :], row_h[:, s, 2 * D:3 * D], ALU.subtract
                                      ).then_inc(zl_done, 1)
                if isinstance(it, int) and it == 0:
                    bias_halves()
                if isinstance(it, int) and it + 1 < T // GRP:
                    stats_of(it + 1)
                on_, t, s, par, rnd = stage(i, it, 5, u)
                if on_:
                    dve.wait_ge(bn2_s, t + 1)
                    alone(dve, dve_passed)
                    dve.bn_aggr(mvb[:, par, :], st6b[:, par, :]).then_inc(bn2_a, 1)
                on_, t, s, par, rnd = stage(i, it, 1, u)
                if on_:
                    dve.wait_ge(stk_done, t + 1)
                    if not isinstance(it, int) or i >= 3:
                        dve.wait_ge(kbd_ld[(i - 3) % RING], (u + (i - 3) // RING + 1) * 64)
                    dve.tensor_copy(kT[:, par, :, :].rearrange("p a n -> p (a n)"), ps_stk[:, NA * P:2 * NA * P]
                                    ).then_inc(k_ev, 1)
                if isinstance(it, int) and it == 0:
                    output_bias()
                if isinstance(it, int) and it == 1:
                    output_bias_halves()
                if isinstance(it, int) and it == PRO - 2:
                    router_halves()
                if isinstance(it, int) and it == T + 1:
                    expert_biases()

            pipeline(dve, step)

            steps = [0]

            def then(ins):
                steps[0] += 1
                ins.then_inc(r_step, 1)
                dve.wait_ge(r_step, steps[0])

            def bc(a, n):
                return a.rearrange("p (t o) -> p t o", o=1).broadcast_to([P, T, n])

            def over_t(a, n):
                return a.rearrange("p (o n) -> p o n", o=1).broadcast_to([P, T, n])

            dve.wait_ge(lg_ev, T)
            then(dve.tensor_reduce(lmax[:, :], logit[:, :, :], AX.X, ALU.max))
            dve.tensor_tensor(ldif[:, :, :], logit[:, :, :], bc(lmax[:, :], NE), ALU.subtract).then_inc(r_dif, 1)
            then(dve.tensor_tensor(eq[:, :, :], logit[:, :, :], bc(lmax[:, :], NE), ALU.is_equal))
            then(dve.tensor_tensor(cand[:, :, :], eq[:, :, :], over_t(cf[:, C_REV:C_REV + NE], NE), ALU.mult))
            then(dve.tensor_reduce(cmax[:, :], cand[:, :, :], AX.X, ALU.max))
            dve.tensor_tensor(oh[:, :, :], cand[:, :, :], bc(cmax[:, :], NE), ALU.is_equal).then_inc(r_oh, 1)
            dve.wait_ge(r_exp, 1)
            then(dve.tensor_reduce(lsum[:, :], lexp[:, :, :], AX.X, ALU.add))
            then(dve.reciprocal(gate[:, :], lsum[:, :]))
            dve.tensor_copy(gate_h[:, 0, :], gate[:, :]).then_inc(r_gate, 1)
            dve.wait_ge(r_gate, 1)
            dve.tensor_tensor(gate_h[:, 1, :], gate[:, :], gate_h[:, 0, :], ALU.subtract).then_inc(r_gate, 1)
            dve.wait_ge(r_pe, 2)
            pre = bank[0][:, 0:T * NE].rearrange("p (t e) -> p t e", e=NE)
            total = bank[0][:, T * NE:(T + 1) * NE]
            then(dve.tensor_scalar(n_f[:, :], total, float(P - 1), None, ALU.add))
            then(dve.tensor_copy(n_i[:, 0, :], n_f[:, :]))
            then(dve.tensor_scalar(n_i[:, 1, :], n_i[:, 0, :], 7, None, ALU.arith_shift_right))
            then(dve.tensor_copy(base[:, 0, 5:4 + NE], n_i[:, 1, 0:NE - 1]))
            for n in range(3):
                d = 1 << n
                a, b = base[:, n % 2, :], base[:, 1 - n % 2, :]
                then(dve.tensor_tensor(b[:, 4:4 + NE], a[:, 4:4 + NE], a[:, 4 - d:4 - d + NE], ALU.add))
            first = base[:, 1, 4:4 + NE]
            then(dve.scalar_tensor_tensor(out=rank[:, 0, :, :], in0=over_t(first, NE), scalar=float(P),
                                          in1=pre, op0=ALU.mult, op1=ALU.add))
            then(dve.tensor_tensor(rank[:, 2, :, :], rank[:, 0, :, :], oh[:, :, :], ALU.mult))
            then(dve.tensor_reduce(dest[:, :], rank[:, 2, :, :], AX.X, ALU.add))
            then(dve.tensor_copy(dest_i[:, 0, :], dest[:, :]))
            then(dve.tensor_scalar(dest_i[:, 1, :], dest_i[:, 0, :], P - 1, None, ALU.bitwise_and))
            then(dve.tensor_scalar(dest_i[:, 2, :], dest_i[:, 0, :], 7, None, ALU.arith_shift_right))
            then(dve.tensor_copy(dest_f[:, 0, :], dest_i[:, 1, :]))
            then(dve.tensor_copy(dest_f[:, 1, :], dest_i[:, 2, :]))
            for n, ts in enumerate(slice(a, a + PAY) for a in range(0, T, PAY)):
                def bg(a, w):
                    return a.rearrange("p (t o) -> p t o", o=1).broadcast_to([P, PAY, w])

                def og(a, w):
                    return a.rearrange("p (o n) -> p o n", o=1).broadcast_to([P, PAY, w])

                dve.tensor_tensor(slot_oh[:, ts, :], og(iota[:, 0:NS], NS), bg(dest_f[:, 1, ts], NS), ALU.is_equal
                                  ).then_inc(r_slot, 1)
                dve.tensor_tensor(place[:, ts, :], og(iota, P), bg(dest_f[:, 0, ts], P), ALU.is_equal).then_inc(r_place, 1)
            then(dve.tensor_tensor(te_c[:, :, :],
                                   cf[0:1, C_IOTA:C_IOTA + NS].rearrange("p (n o) -> p n o", o=1).broadcast_to([1, NS, NE - 1]),
                                   base[0:1, 1, 5:4 + NE].rearrange("p (o n) -> p o n", o=1).broadcast_to([1, NS, NE - 1]),
                                   ALU.is_ge))
            then(dve.tensor_reduce(te_f[:, :], te_c[:, :, :], AX.X, ALU.add))
            then(dve.tensor_copy(te_i[:, :], te_f[:, :]))
            dve.wait_ge(r_pe, 3)
            got_ps = bank[6][:, 0:4 * NS].rearrange("p (c n) -> p c n", c=4)
            then(dve.tensor_copy(idx[:, 0, :], got_ps[:, 0, :]))
            then(dve.tensor_scalar(idx[:, 1, :], idx[:, 0, :], 0.0, OUT_OF_RANGE, ALU.is_equal, ALU.mult))
            then(dve.scalar_tensor_tensor(out=idx[:, 2, :], in0=got_ps[:, 1, :], scalar=float(P), in1=idx[:, 1, :],
                                          op0=ALU.mult, op1=ALU.add))
            then(dve.scalar_tensor_tensor(out=idx[:, 3, :], in0=idx[:, 0, :], scalar=-1.0, in1=idx[:, 2, :],
                                          op0=ALU.add, op1=ALU.add))
            dve.engine_nop().then_inc(r_tiles, 1)

            def ffn(i, it, u):
                on_, t, s, par, rnd = fstage(i, it, 0, u)
                if on_:
                    if s != s or not isinstance(it, int) or it >= RING:
                        dve.wait_ge(f_got[s], rnd * 16)
                    alone(dve, dve_passed)
                    dve.tensor_copy(idx_s[:, s:s + 1], idx[:, 3, bass.ds(t, 1)]).then_inc(f_idx, 1)
                if isinstance(it, int) and it == 2:
                    then(dve.tensor_copy(slot_gate[:, 0, :], got_ps[:, 2, :]))
                    then(dve.tensor_tensor(slot_gate[:, 1, :], got_ps[:, 3, :], slot_gate[:, 0, :], ALU.add))
                    then(dve.tensor_scalar(slot_gate[:, 0, :], slot_gate[:, 1, :], tg[:, 1:2], None, ALU.mult))
                on_, t, s, par, rnd = fstage(i, it, 3, u)
                if on_:
                    dve.wait_ge(f_got[s], rnd * 16 + 16)
                    wait(dve, f_st[s], rnd * 16)
                    alone(dve, dve_passed)
                    dve.tensor_copy(idx_o[:, s:s + 1], idx[:, 3, bass.ds(t, 1)]).then_inc(f_io, 1)
                    dve.tensor_copy(fin[:, s, :], got[:, s, 0:D]).then_inc(f_x2, 1)
                on_, t, s, par, rnd = fstage(i, it, 4, u)
                if on_:
                    dve.wait_ge(f_y, t + 1)
                    dve.wait_ge(f_x2, t + 1)
                    dve.scalar_tensor_tensor(out=fin[:, s, :], in0=bank[4 + par][:, 0:D],
                                             scalar=slot_gate[:, 0, bass.ds(t, 1)], in1=fin[:, s, :],
                                             op0=ALU.mult, op1=ALU.add).then_inc(f_fin, 1)

            ffn_pipeline(dve, ffn)


_INS = ['x', 'ctx_1024', 'mask_Bx1xS2_if1', 'g_xattn', 'g_ffn', 'L0_xattn_Wq', 'L0_xattn_bq', 'L0_xattn_Wk',
        'L0_xattn_bk', 'L0_xattn_Wv', 'L0_xattn_bv', 'L0_xattn_Wo', 'L0_xattn_bo', 'L0_ffn_W1', 'L0_ffn_b1',
        'L0_ffn_W2', 'L0_ffn_b2', 'L0_ffn_Wr', 'L0_ffn_br']


def kernel(**inputs):
    from concourse import bacc
    from concourse.bass_utils import run_bass_kernel_spmd

    nc = bacc.Bacc("TRN2", target_bir_lowering=False, num_devices=1)
    arrays, args = {}, []
    tables = dict(zip(("const_f", "const_h"), constants()))
    for name in _INS + list(tables):
        a = np.ascontiguousarray(tables[name] if name in tables else inputs[name])
        arrays[f"in_{name}"] = a
        args.append(nc.dram_tensor(f"in_{name}", a.shape, mybir.dt.from_np(a.dtype), kind="ExternalInput").ap())
    rows = nc.dram_tensor("rows", (B * S, ROW), F32, kind="Internal").ap()
    out = nc.dram_tensor("out_0", (B, S, D), F32, kind="ExternalOutput").ap()
    build(nc, *args, rows, out)
    r = run_bass_kernel_spmd(nc, [arrays], core_ids=[0])
    return r.results[0]["out_0"]
```
